# Optimizing a Trainium2 kernel written in Bass

```python
import numpy as np
import jax
import jax.numpy as jnp

def _softmax(x, axis=-1):
    return jax.nn.softmax(x, axis=axis)

def _gelu(x):
    return jax.nn.gelu(x, approximate=True)

def _silu(x):
    return jax.nn.silu(x)

def _sigmoid(x):
    return jax.nn.sigmoid(x)

def _layernorm(x, axis=-1, eps=1e-05):
    m = jnp.mean(x, axis=axis, keepdims=True)
    v = jnp.var(x, axis=axis, keepdims=True)
    return (x - m) / jnp.sqrt(v + eps)

def _scatter_add(tgt, idx, src, axis=0):
    return tgt.at[idx].add(src)

def _segment_sum(src, seg, n):
    return jax.ops.segment_sum(src, seg, n)
kernel_name = 'mk_adj_ffn_d2_adj_r2_7ddf5a'

def setup_inputs(seed: int=0):
    np.random.seed(seed)
    _w = jnp.asarray

    def _rec_inputs():
        import jax
        import jax.numpy as jnp
        _gk = jax.random.key(seed)
        x = -0.0002928 + 1 * jax.random.normal(jax.random.fold_in(_gk, 1), (3327, 256), jnp.float32)
        _a = jax.random.bernoulli(jax.random.fold_in(_gk, 2), 0.00480914, (3327, 3327))
        _a = jnp.logical_or(_a, jnp.swapaxes(_a, -1, -2))
        _a = jnp.logical_or(_a, jnp.eye(3327, dtype=bool))
        _af = _a.astype(jnp.float32)
        adj = _af
        return (x, adj)
    x, adj = _rec_inputs()

    def _L0_gnn_setup():
        import jax, jax.numpy as jnp
        import numpy as np
        N = 4096
        D_IN = 256
        D_OUT = 256
        NEG_BIG = -9000000000000000.0
        key = jax.random.key(seed)
        kx, ka, kw, kb, kn, ke = jax.random.split(key, 6)
        x = jax.random.normal(kx, (N, D_IN), dtype=jnp.float32)
        adj = (jax.random.uniform(ka, (N, N)) > 0.9).astype(jnp.float32)
        stdv = 1.0 / np.sqrt(D_OUT)
        weight = jax.random.uniform(kw, (D_IN, D_OUT), minval=-stdv, maxval=stdv, dtype=jnp.float32)
        bias = jax.random.uniform(kb, (D_OUT,), minval=-stdv, maxval=stdv, dtype=jnp.float32)
        node_w = jax.random.uniform(kn, (D_IN, 1), minval=-1.0, maxval=1.0, dtype=jnp.float32)
        stdv_e = 1.0 / np.sqrt(D_IN)
        edge_w = jax.random.uniform(ke, (D_IN, D_IN), minval=-stdv_e, maxval=stdv_e, dtype=jnp.float32)
        return {'x': x, 'adj': adj, 'weight': weight, 'bias': bias, 'node_w': node_w, 'edge_w': edge_w}
    _L0_gnn_all = _L0_gnn_setup()
    _L0_gnn_in = {k: v for k, v in _L0_gnn_all.items() if k in ('weight', 'bias', 'node_w', 'edge_w')}
    del _L0_gnn_all

    def _L0_ffn_setup():
        import jax, jax.numpy as jnp
        import numpy as np
        D_MODEL = 256
        NUM_EXPERTS = 8
        TOP_K = 2
        FFN_MULT = 2
        HIDDEN = FFN_MULT * D_MODEL
        BATCH, SEQ = (4, 1024)
        key = jax.random.key(seed)
        k_x, k_g, k_bg, k_w1, k_w3, k_w2 = jax.random.split(key, 6)
        sd = 1.0 / np.sqrt(D_MODEL).astype(np.float32)
        sh = 1.0 / np.sqrt(HIDDEN).astype(np.float32)
        return {'x': jax.random.normal(k_x, (BATCH, SEQ, D_MODEL), dtype=jnp.float32), 'Wg': jax.random.normal(k_g, (D_MODEL, NUM_EXPERTS), dtype=jnp.float32) * sd, 'bg': jax.random.normal(k_bg, (NUM_EXPERTS,), dtype=jnp.float32) * 0.01, 'W1': jax.random.normal(k_w1, (NUM_EXPERTS, D_MODEL, HIDDEN), dtype=jnp.float32) * sd, 'W3': jax.random.normal(k_w3, (NUM_EXPERTS, D_MODEL, HIDDEN), dtype=jnp.float32) * sd, 'W2': jax.random.normal(k_w2, (NUM_EXPERTS, HIDDEN, D_MODEL), dtype=jnp.float32) * sh}
    _L0_ffn_all = _L0_ffn_setup()
    _L0_ffn_in = {k: v for k, v in _L0_ffn_all.items() if k in ('Wg', 'bg', 'W1', 'W3', 'W2')}
    del _L0_ffn_all

    def _L1_gnn_setup():
        import jax, jax.numpy as jnp
        import numpy as np
        N_NODES = 4096
        DIM = 256
        key = jax.random.key(seed)
        k1, k2, k3, k4 = jax.random.split(key, 4)
        x = jax.random.normal(k1, (N_NODES, DIM), dtype=jnp.float32)
        adj = jax.random.uniform(k2, (N_NODES, N_NODES), dtype=jnp.float32)
        bound = 1.0 / np.sqrt(DIM)
        W = jax.random.uniform(k3, (DIM, DIM), minval=-bound, maxval=bound, dtype=jnp.float32)
        b = jax.random.uniform(k4, (DIM,), minval=-bound, maxval=bound, dtype=jnp.float32)
        return {'x': x, 'adj': adj, 'W': W, 'b': b}
    _L1_gnn_all = _L1_gnn_setup()
    _L1_gnn_in = {k: v for k, v in _L1_gnn_all.items() if k in ('W', 'b')}
    del _L1_gnn_all

    def _L1_ffn_setup():
        import jax, jax.numpy as jnp
        import numpy as np
        B, S, D = (8, 1024, 256)
        E, K, H = (8, 2, 1024)
        key = jax.random.key(seed)
        ks = jax.random.split(key, 6)
        scale = 0.02
        return {'x': jax.random.normal(ks[0], (B, S, D), dtype=jnp.float32), 'gate_w': jax.random.normal(ks[1], (E, D), dtype=jnp.float32) * scale, 'w1': jax.random.normal(ks[2], (E, H, D), dtype=jnp.float32) * scale, 'b1': jax.random.normal(ks[3], (E, H), dtype=jnp.float32) * scale, 'w2': jax.random.normal(ks[4], (E, D, H), dtype=jnp.float32) * scale, 'b2': jax.random.normal(ks[5], (E, D), dtype=jnp.float32) * scale}
    _L1_ffn_all = _L1_ffn_setup()
    _L1_ffn_in = {k: v for k, v in _L1_ffn_all.items() if k in ('gate_w', 'w1', 'b1', 'w2', 'b2')}
    del _L1_ffn_all
    return {'x': x, 'adj': adj, 'L0_gnn_weight': _L0_gnn_in['weight'], 'L0_gnn_bias': _L0_gnn_in['bias'], 'L0_gnn_node_w': _L0_gnn_in['node_w'], 'L0_gnn_edge_w': _L0_gnn_in['edge_w'], 'L0_ffn_Wg': _L0_ffn_in['Wg'], 'L0_ffn_bg': _L0_ffn_in['bg'], 'L0_ffn_W1': _L0_ffn_in['W1'], 'L0_ffn_W3': _L0_ffn_in['W3'], 'L0_ffn_W2': _L0_ffn_in['W2'], 'L1_gnn_W': _L1_gnn_in['W'], 'L1_gnn_b': _L1_gnn_in['b'], 'L1_ffn_gate_w': _L1_ffn_in['gate_w'], 'L1_ffn_w1': _L1_ffn_in['w1'], 'L1_ffn_b1': _L1_ffn_in['b1'], 'L1_ffn_w2': _L1_ffn_in['w2'], 'L1_ffn_b2': _L1_ffn_in['b2']}

def reference(x, adj, L0_gnn_weight, L0_gnn_bias, L0_gnn_node_w, L0_gnn_edge_w, L0_ffn_Wg, L0_ffn_bg, L0_ffn_W1, L0_ffn_W3, L0_ffn_W2, L1_gnn_W, L1_gnn_b, L1_ffn_gate_w, L1_ffn_w1, L1_ffn_b1, L1_ffn_w2, L1_ffn_b2):
    import jax
    import jax.numpy as jnp

    def _L0_gnn_ref(x, adj, weight, bias, node_w, edge_w):
        import jax, jax.numpy as jnp
        import numpy as np
        N = 4096
        D_IN = 256
        D_OUT = 256
        NEG_BIG = -9000000000000000.0
        node_att = jax.nn.softmax(x @ node_w, axis=0)
        h = x @ edge_w
        e = h @ h.T
        e = jnp.where(adj > 0, e, NEG_BIG)
        edge_att = jax.nn.softmax(e, axis=1)
        combined_att = node_att * edge_att
        support = x @ weight
        output = adj * combined_att @ support
        return output + bias

    def _L0_ffn_ref(x, Wg, bg, W1, W3, W2):
        import jax, jax.numpy as jnp
        import numpy as np
        D_MODEL = 256
        NUM_EXPERTS = 8
        TOP_K = 2
        FFN_MULT = 2
        HIDDEN = FFN_MULT * D_MODEL
        BATCH, SEQ = (4, 1024)
        B, S, D = x.shape
        E = Wg.shape[1]
        xt = x.reshape(-1, D)
        T = xt.shape[0]
        logits = xt @ Wg + bg
        top_vals, top_idx = jax.lax.top_k(logits, TOP_K)
        top_probs = jax.nn.softmax(top_vals, axis=-1)
        gate_w = jnp.zeros((T, E), dtype=xt.dtype).at[jnp.arange(T)[:, None], top_idx].add(top_probs)

        def body(y, expert):
            w1, w3, w2, g = expert
            h = jax.nn.silu(xt @ w1) * (xt @ w3)
            return (y + g[:, None] * (h @ w2), None)
        y0 = jnp.zeros_like(xt)
        y, _ = jax.lax.scan(body, y0, (W1, W3, W2, gate_w.T))
        return y.reshape(B, S, D)

    def _L1_gnn_ref(x, adj, W, b):
        import jax, jax.numpy as jnp
        import numpy as np
        N_NODES = 4096
        DIM = 256
        agg = jnp.matmul(adj, x)
        out = jnp.matmul(agg, W.T) + b
        return jax.nn.relu(out)

    def _L1_ffn_ref(x, gate_w, w1, b1, w2, b2):
        import jax, jax.numpy as jnp
        import numpy as np
        B, S, D = (8, 1024, 256)
        E, K, H = (8, 2, 1024)
        batch, seq, dim = x.shape
        x_flat = x.reshape(-1, dim)
        T = x_flat.shape[0]
        gate_logits = x_flat @ gate_w.T
        topk_vals, topk_idx = jax.lax.top_k(gate_logits, K)
        topk_w = jax.nn.softmax(topk_vals, axis=-1)
        comb = jnp.zeros((T, E), dtype=x_flat.dtype)
        comb = comb.at[jnp.arange(T)[:, None], topk_idx].add(topk_w)
        out = jnp.zeros_like(x_flat)
        for e in range(E):
            h = jax.nn.gelu(x_flat @ w1[e].T + b1[e], approximate=False)
            y = h @ w2[e].T + b2[e]
            out = out + comb[:, e:e + 1] * y
        return out.reshape(batch, seq, dim)
    x = x + _L0_gnn_ref(_layernorm(x, axis=-1), adj, L0_gnn_weight, L0_gnn_bias, L0_gnn_node_w, L0_gnn_edge_w)
    x = x + _L0_ffn_ref(_layernorm(x, axis=-1)[None], L0_ffn_Wg, L0_ffn_bg, L0_ffn_W1, L0_ffn_W3, L0_ffn_W2)[0]
    x = x + _L1_gnn_ref(_layernorm(x, axis=-1), adj, L1_gnn_W, L1_gnn_b)
    x = x + _L1_ffn_ref(_layernorm(x, axis=-1)[None], L1_ffn_gate_w, L1_ffn_w1, L1_ffn_b1, L1_ffn_w2, L1_ffn_b2)[0]
    return x

_drawn_inputs = setup_inputs


def setup_inputs(seed=0):
    import zlib

    import numpy as np

    out = dict(_drawn_inputs(seed))
    spreads = {}
    factors = {'L0_gnn_weight': 8.0,
     'L0_gnn_node_w': 6.124,
     'L1_gnn_b': 5.936,
     'L1_ffn_b1': 28.549,
     'L1_ffn_b2': 8.0}
    for name, (base, spread) in spreads.items():
        noise = np.random.default_rng([zlib.crc32(name.encode()), seed]).standard_normal(out[name].shape)
        drawn = base * np.exp(spread * noise) if base else spread * noise
        out[name] = jnp.asarray(drawn.astype(out[name].dtype))
    for name, factor in factors.items():
        out[name] = (out[name] * factor).astype(out[name].dtype)
    return out
```

```python
import concourse.bass as bass
from concourse import mybir
from contextlib import ExitStack

F32 = mybir.dt.float32
F32R = mybir.dt.float32r
F16 = mybir.dt.float16
BF16 = mybir.dt.bfloat16
I32 = mybir.dt.int32
ALU = mybir.AluOpType
ACT = mybir.ActivationFunctionType
AX = mybir.AxisListType.X
RMAX = bass.bass_isa.ReduceOp.max
RADD = bass.bass_isa.ReduceOp.add

P = 128
N = 3327
T = (N + P - 1) // P
NP = T * P
TAIL = N - (T - 1) * P
TAIL_A = TAIL // 16 * 16
D = 256
KD = D // P
EPS = 1e-5
BIG = 2.0 ** 100
CH = 512
CHUNKS = [(c, min(CH, NP - c)) for c in range(0, NP, CH)]
NC = len(CHUNKS)
GROUPS = [(g, min(4, T - g)) for g in range(0, T, 4)]
NG = len(GROUPS)
E = 8
H0 = 512
H1 = 1024
PAIRS = 2 * N
S = (PAIRS - E) // P + E
PAIR_ROWS = 2 * NP


def tiles(eng, count, step):
    turns = (count - 1) // 2
    step(0, 0, 0, True, False)
    step(1, 0, 1, True, False)
    with eng.Fori(1, turns) as i:
        step(i * 2, i, 0, False, False)
        step(i * 2 + 1, i, 1, False, False)
    for t in range(2 * turns, count):
        step(t, t // 2, t % 2, False, t == count - 1)


class Chain:

    def __init__(self, eng, sem):
        self.eng, self.sem, self.n = eng, sem, 0

    def __call__(self, ins):
        ins.then_inc(self.sem, 1)
        self.n += 1
        self.eng.wait_ge(self.sem, self.n)


class Stage:

    def __init__(self, nc, ctx, name):
        self.nc, self.ctx, self.name, self.sems = nc, ctx, name, []
        ctx.callback(self.end)

    def sb(self, name, shape, dt=F32):
        return self.ctx.enter_context(self.nc.sbuf_tensor(f"{self.name}_{name}", shape, dt))

    def sem(self, name):
        self.sems.append(self.nc.alloc_semaphore(f"{self.name}_{name}"))
        return self.sems[-1]

    def end(self):
        self.nc.clear_and_free_semaphores(self.sems)
        self.nc.all_engine_barrier()


def load_nodes(sp, X, src, halves, tail):
    full = src[0:(T - 1) * P, :].rearrange("(t p) d -> p t d", p=P)
    mid = T // 2
    sp.dma_start(X[:, 0:mid, :], full[:, 0:mid, :]).then_inc(halves[0], 16)
    sp.dma_start(X[:, mid:T - 1, :], full[:, mid:T - 1, :]).then_inc(halves[1], 16)
    base = (T - 1) * P
    sp.dma_start(X[0:TAIL_A, T - 1, :], src[base:base + TAIL_A, :]).then_inc(tail, 16)
    sp.dma_start(X[TAIL_A:TAIL, T - 1, :], src[base + TAIL_A:N, :]).then_inc(tail, 16)


def row_statistics(dve, link, X, ST, MV, arrived, var_ready, std_ready):
    mid = T // 2
    start = link.n
    for lo, hi, (sem, n) in ((0, mid, arrived[0]), (mid, T - 1, arrived[1]), (T - 1, T, arrived[2])):
        dve.wait_ge(sem, n)
        if hi - lo > 1:
            with dve.Fori(lo, hi) as t:
                dve.bn_stats(ST[:, t, :], X[:, t, :]).then_inc(link.sem, 1)
        else:
            dve.bn_stats(ST[:, lo, :], X[:, lo, :]).then_inc(link.sem, 1)
    link.n = start + T
    dve.wait_ge(link.sem, link.n)
    me, qe, mo, qo = (ST[:, :, k] for k in (1, 2, 4, 5))
    mean, rstd, var, tmp = (MV[:, k, :] for k in range(4))
    link(dve.tensor_tensor(tmp, me, mo, ALU.subtract))
    link(dve.tensor_tensor(mean, me, mo, ALU.add))
    link(dve.tensor_tensor(tmp, tmp, tmp, ALU.mult))
    link(dve.tensor_scalar(mean, mean, 0.5, None, ALU.mult))
    link(dve.tensor_tensor(var, qe, qo, ALU.add))
    link(dve.scalar_tensor_tensor(tmp, tmp, D / 4.0, var, ALU.mult, ALU.add))
    dve.tensor_scalar(var, tmp, 1.0 / D, EPS, ALU.mult, ALU.add).then_inc(var_ready, 1)
    dve.wait_ge(std_ready, 1)
    link(dve.reciprocal(rstd, tmp))
    link(dve.tensor_tensor(tmp, rstd, rstd, ALU.mult))
    link(dve.tensor_tensor(tmp, tmp, var, ALU.mult))
    link(dve.tensor_scalar(tmp, tmp, -0.5, 1.5, ALU.mult, ALU.add))
    link(dve.tensor_tensor(rstd, rstd, tmp, ALU.mult))


def square_root(act, MV, var_ready, std_ready):
    act.wait_ge(var_ready, 1)
    act.activation(MV[:, 3, :], MV[:, 2, :], ACT.Sqrt).then_inc(std_ready, 1)


def project(nc, a, bank):
    with ExitStack() as ctx:
        s = Stage(nc, ctx, "proj")
        X = s.sb("x", [P, T, D])
        ST = s.sb("stats", [P, T, 6])
        MV = s.sb("mean_var", [P, 4, T])
        XS = s.sb("normed", [P, 2, D])
        XT = s.sb("normed_t", [P, 2, KD, P])
        EW = s.sb("edge_w", [P, KD, D])
        WN = s.sb("weight_node", [P, KD, D + 1])
        ID = s.sb("identity", [P, P])
        ONES = s.sb("ones", [P, P])
        NL = s.sb("node_logits", [P, T])
        VAL = s.sb("valid", [P, T])
        SM = s.sb("small", [P, 4])
        HT, SUP, NATT = a["HT"], a["SUP"], a["NATT"]
        halves = [s.sem("x_first_half"), s.sem("x_second_half")]
        tail = s.sem("x_last_tile")
        edge_in, node_in = s.sem("edge_w_loaded"), s.sem("weight_loaded")
        chain = s.sem("dve_chain")
        padded = s.sem("pad_zeroed")
        consts = s.sem("constants_ready")
        var_ready, std_ready = s.sem("variance_ready"), s.sem("std_ready")
        normed, transposed, xt_ready = s.sem("normed"), s.sem("transposed"), s.sem("xt_ready")
        projected, hi_ready, lo_ready = s.sem("projected"), s.sem("hi_ready"), s.sem("lo_ready")
        mx_ready, mx_all = s.sem("logit_max_ready"), s.sem("logit_max_all")
        nmx_ready, e_ready, sum_all = s.sem("neg_max_ready"), s.sem("exp_ready"), s.sem("sum_all")
        with nc.Block() as block:
            @block.sync
            def _(sp):
                sp.wait_ge(padded, 1)
                load_nodes(sp, X, a["x"], halves, tail)
                sp.dma_start(EW[:], a["edge_w"].rearrange("(k p) f -> p k f", p=P)).then_inc(edge_in, 16)
                sp.dma_start(WN[:, :, 0:D], a["weight"].rearrange("(k p) f -> p k f", p=P)).then_inc(node_in, 16)
                sp.dma_start(WN[:, :, D:D + 1], a["node_w"].rearrange("(k p) f -> p k f", p=P), allow_slow_non_contiguous=True).then_inc(node_in, 16)

            @block.gpsimd
            def _(pool):
                pool.memset(ID[:], 0.0).then_inc(consts, 1)
                pool.wait_ge(consts, 1)
                pool.affine_select(out=ID[:], in_=ID[:], compare_op=ALU.not_equal, fill=1.0, base=0,
                                   pattern=[[-1, P]], channel_multiplier=1).then_inc(consts, 1)
                pool.memset(VAL[:], 1.0).then_inc(consts, 1)
                pool.wait_ge(consts, 3)
                pool.affine_select(out=VAL[:], in_=VAL[:], compare_op=ALU.is_gt, fill=0.0, base=N,
                                   pattern=[[-P, T]], channel_multiplier=-1).then_inc(consts, 1)
                pool.wait_ge(mx_ready, 1)
                pool.partition_all_reduce(SM[:, 1:2], SM[:, 0:1], P, RMAX).then_inc(mx_all, 1)
                pool.wait_ge(e_ready, 1)
                pool.partition_all_reduce(SM[:, 3:4], SM[:, 2:3], P, RADD).then_inc(sum_all, 1)

            @block.vector
            def _(dve):
                link = Chain(dve, chain)
                dve.memset(X[:, T - 1, :], 0.0).then_inc(padded, 1)
                row_statistics(dve, link, X, ST, MV, [(halves[0], 16), (halves[1], 16), (tail, 32)],
                               var_ready, std_ready)

                def norm(t, slot, first):
                    if not first:
                        dve.wait_ge(transposed, t - 1)
                    dve.tensor_scalar(XS[:, slot, :], X[:, t, :], MV[:, 0, bass.ds(t, 1)], MV[:, 1, bass.ds(t, 1)],
                                      ALU.subtract, ALU.mult).then_inc(normed, 1)

                def step(t, uses, slot, first, last):
                    if not last:
                        norm(t + 1, 1 - slot, first and slot == 0)
                    dve.wait_ge(hi_ready, t + 1)
                    dve.tensor_tensor(SUP[:, t, 1, :], bank[2 + slot][:, 0:D], SUP[:, t, 0, :].bitcast(F32), ALU.subtract)
                    dve.tensor_tensor(HT[:, 1, :, bass.ds(t * P, P)],
                                      bank[4 + slot][:, 0:D].rearrange("p (k n) -> p k n", k=KD),
                                      HT[:, 0, :, bass.ds(t * P, P)].bitcast(F32), ALU.subtract).then_inc(lo_ready, 1)

                norm(0, 0, True)
                tiles(dve, T, step)
                dve.wait_ge(lo_ready, T)
                dve.wait_ge(consts, 4)
                link(dve.tensor_tensor(NL[:], NL[:], VAL[:], ALU.mult))
                link(dve.tensor_scalar(VAL[:], VAL[:], BIG, -BIG, ALU.mult, ALU.add))
                link(dve.tensor_tensor(NL[:], NL[:], VAL[:], ALU.add))
                dve.reduce_max(SM[:, 0:1], NL[:], AX).then_inc(mx_ready, 1)
                dve.wait_ge(mx_all, 1)
                dve.tensor_scalar(SM[:, 1:2], SM[:, 1:2], -1.0, None, ALU.mult).then_inc(nmx_ready, 1)
                dve.wait_ge(sum_all, 1)
                link(dve.reciprocal(SM[:, 3:4], SM[:, 3:4]))
                link(dve.tensor_scalar(NATT[:], NATT[:], SM[:, 3:4], None, ALU.mult))

            @block.scalar
            def _(act):
                square_root(act, MV, var_ready, std_ready)

                def copy_t(t, slot, first):
                    act.wait_ge(transposed, t + 1)
                    if not first:
                        act.wait_ge(projected, t - 1)
                    act.copy(XT[:, slot, :, :], bank[slot][:, 0:D].rearrange("p (k n) -> p k n", k=KD)).then_inc(xt_ready, 1)

                def step(t, uses, slot, first, last):
                    if not last:
                        copy_t(t + 1, 1 - slot, first and slot == 0)
                    act.wait_ge(projected, t + 1)
                    act.copy(SUP[:, t, 0, :], bank[2 + slot][:, 0:D])
                    act.copy(NL[:, bass.ds(t, 1)], bank[2 + slot][:, D:D + 1])
                    act.copy(HT[:, 0, :, bass.ds(t * P, P)],
                             bank[4 + slot][:, 0:D].rearrange("p (k n) -> p k n", k=KD)).then_inc(hi_ready, 1)

                copy_t(0, 0, True)
                tiles(act, T, step)
                act.wait_ge(nmx_ready, 1)
                act.activation(NATT[:], NL[:], ACT.Exp, bias=SM[:, 1:2], accum_out=SM[:, 2:3]).then_inc(e_ready, 1)

            @block.tensor
            def _(pe):
                def flip(t, slot, first):
                    pe.wait_ge(normed, t + 1)
                    if not first:
                        pe.wait_ge(xt_ready, t - 1)
                    for k in range(KD):
                        last = pe.transpose(bank[slot][:, k * P:(k + 1) * P], XS[:, slot, k * P:(k + 1) * P], ID[:])
                    last.then_inc(transposed, 1)

                def step(t, uses, slot, first, last):
                    if not last:
                        flip(t + 1, 1 - slot, first and slot == 0)
                    pe.wait_ge(xt_ready, t + 1)
                    if not first:
                        pe.wait_ge(lo_ready, t - 1)
                    for k in range(KD):
                        pe.matmul(bank[2 + slot][:, 0:D + 1], XT[:, slot, k, :], WN[:, k, :], start=k == 0, stop=k == KD - 1)
                    for f in range(KD):
                        for k in range(KD):
                            ins = pe.matmul(bank[4 + slot][:, f * P:(f + 1) * P], EW[:, k, f * P:(f + 1) * P],
                                            XT[:, slot, k, :], start=k == 0, stop=k == KD - 1)
                    ins.then_inc(projected, 1)

                pe.wait_ge(consts, 2)
                flip(0, 0, True)
                pe.wait_ge(edge_in, 16)
                pe.wait_ge(node_in, 32)
                tiles(pe, T, step)


def attend(nc, a, bank):
    HT, SUP, NATT = a["HT"], a["SUP"], a["NATT"]
    with ExitStack() as ctx:
        s = Stage(nc, ctx, "attn")
        ADJ = s.sb("adj", [P, 2, NP])
        NEG = s.sb("mask", [P, 2, NP], BF16)
        SC = s.sb("scores", [P, 2, NP])
        HS = s.sb("h_tile", [P, 2, 2, KD, P], F32R)
        PT = s.sb("probs_t", [P, 2, 2, CH], F32R)
        ID = s.sb("identity", [P, P])
        XB = s.sb("x", [P, 2, D])
        XO = s.sb("x_out", [P, 2, D])
        BB = s.sb("bias", [P, D])
        MX = s.sb("max", [P, 2, NC])
        TAKER = s.sb("wait_taker", [P, 2, NC])
        SM = s.sb("small", [P, 2, 6])
        consts = s.sem("constants_ready")
        bias_in = s.sem("bias_loaded")
        edge = s.sem("pad_column_zeroed")
        adj_in = [s.sem(f"adj_loaded{i}") for i in range(2)]
        x_in = [s.sem(f"x_loaded{i}") for i in range(2)]
        mask_ready = s.sem("mask_ready")
        mask_out = [s.sem(f"mask_stored{i}") for i in range(2)]
        h_ready, qk_done, masked = s.sem("h_ready"), s.sem("scores_ready"), s.sem("scores_masked")
        neg_max, exp_done = s.sem("neg_max_ready"), s.sem("probs_ready")
        max_ready, out_part, out_ready = s.sem("max_ready"), s.sem("out_part"), s.sem("out_ready")
        flipped, hi_ready, lo_ready = s.sem("probs_transposed"), s.sem("probs_hi"), s.sem("probs_lo")
        pv_group = s.sem("group_multiplied")
        factor, x_ready = s.sem("factor_ready"), s.sem("x_out_ready")
        x_out = [s.sem(f"x_stored{i}") for i in range(2)]

        def rows(dram, t):
            return dram[bass.ds(t * P, P), :]

        def half(slot, g):
            return (slot + g) % 2

        with nc.Block() as block:
            @block.sync
            def _(sp):
                sp.wait_ge(edge, 1)
                sp.dma_start(BB[:], a["bias"].partition_broadcast(P)).then_inc(bias_in, 16)

                def store(t, slot):
                    sp.wait_ge(out_ready, t + 1)
                    sp.dma_start(rows(a["x1"], t), XO[:, slot, :]).then_inc(x_out[slot], 16)

                def step(t, uses, slot, first, last):
                    if not first:
                        sp.wait_ge(mask_ready, t - 1)
                        sp.wait_ge(x_ready, t - 1)
                    if last:
                        base = (T - 1) * P
                        for lo, hi in ((0, TAIL_A), (TAIL_A, TAIL)):
                            sp.dma_start(ADJ[lo:hi, slot, 0:N], a["adj"][base + lo:base + hi, :]).then_inc(adj_in[slot], 16)
                            sp.dma_start(XB[lo:hi, slot, :], a["x"][base + lo:base + hi, :]).then_inc(x_in[slot], 16)
                    else:
                        sp.dma_start(ADJ[:, slot, 0:N], rows(a["adj"], t)).then_inc(adj_in[slot], 16)
                        sp.dma_start(XB[:, slot, :], rows(a["x"], t)).then_inc(x_in[slot], 16)
                    if not first:
                        store(t - 2, slot)
                tiles(sp, T, step)
                store(T - 2, T % 2)
                store(T - 1, (T - 1) % 2)
                for slot in range(2):
                    sp.wait_ge(x_out[slot], T // 2 * 16)

            @block.gpsimd
            def _(pool):
                pool.memset(ID[:], 0.0).then_inc(consts, 1)
                pool.wait_ge(consts, 1)
                pool.affine_select(out=ID[:], in_=ID[:], compare_op=ALU.not_equal, fill=1.0, base=0,
                                   pattern=[[-1, P]], channel_multiplier=1).then_inc(consts, 1)
                pool.memset(ADJ[:, :, N:NP], 0.0).then_inc(edge, 1)

                def step(t, uses, slot, first, last):
                    pool.wait_ge(adj_in[slot], (uses + 1) * 16 + (16 if last else 0))
                    if not first:
                        pool.wait_ge(masked, (t - 1) * NC)
                        pool.wait_ge(mask_out[slot], uses * 16)
                    pool.tensor_copy(HS[:, slot, :, :, :].rearrange("p a k n -> p (a k) n"),
                                     HT[:, :, :, bass.ds(t * P, P)].rearrange("p a k n -> p (a k) n").bitcast(F32)).then_inc(h_ready, 1)
                    pool.tensor_scalar(NEG[:, slot, :], ADJ[:, slot, :], BIG, -BIG, ALU.mult, ALU.add).then_inc(mask_ready, 1)
                pool.wait_ge(edge, 1)
                tiles(pool, T, step)

            @block.scalar
            def _(act):
                def step(t, uses, slot, first, last):
                    act.wait_ge(mask_ready, t + 1)
                    act.dma_start(a["mask"][t, :, :], NEG[:, slot, :]).then_inc(mask_out[slot], 16)
                    act.wait_ge(neg_max, t + 1)
                    act.activation(SC[:, slot, :], SC[:, slot, :], ACT.Exp, bias=SM[:, slot, 0:1],
                                   accum_out=SM[:, slot, 1:2]).then_inc(exp_done, 1)
                    for g, (g0, gn) in enumerate(GROUPS):
                        act.wait_ge(flipped, t * NG + g + 1)
                        if not (first and slot == 0 and g < 2):
                            act.wait_ge(pv_group, t * NG + (g - 1))
                        act.copy(PT[:, half(slot, g), 0, 0:gn * P], bank[4 + half(slot, g)][:, 0:gn * P]).then_inc(hi_ready, 1)
                tiles(act, T, step)
                for slot in range(2):
                    act.wait_ge(mask_out[slot], T // 2 * 16)

            @block.vector
            def _(dve):
                def score(t, slot, first):
                    dve.wait_ge(mask_ready, t + 1)
                    if not first:
                        dve.wait_ge(flipped, (t - 1) * NG)
                    for c, (c0, cn) in enumerate(CHUNKS):
                        dve.wait_ge(qk_done, t * NC + c + 1)
                        dve.memset(TAKER[:, slot, c:c + 1], 0.0)
                        dve.tensor_tensor_reduce(out=SC[:, slot, c0:c0 + cn], in0=bank[c % 4][:, 0:cn],
                                                 in1=NEG[:, slot, c0:c0 + cn], scale=1.0, scalar=-3.0e38,
                                                 op0=ALU.add, op1=ALU.max,
                                                 accum_out=MX[:, slot, c:c + 1]).then_inc(masked, 1)
                    dve.wait_ge(masked, t * NC + NC)
                    dve.reduce_max(SM[:, slot, 2:3], MX[:, slot, :], AX).then_inc(max_ready, 1)
                    dve.wait_ge(max_ready, t + 1)
                    dve.tensor_scalar(SM[:, slot, 3:4], SM[:, slot, 2:3], -BIG / 2, None, ALU.is_gt)
                    dve.tensor_scalar(SM[:, slot, 0:1], SM[:, slot, 2:3], -1.0, None, ALU.mult).then_inc(neg_max, 1)

                def step(t, uses, slot, first, last):
                    if not last:
                        score(t + 1, 1 - slot, first and slot == 0)
                    for g, (g0, gn) in enumerate(GROUPS):
                        dve.wait_ge(hi_ready, t * NG + g + 1)
                        dve.tensor_tensor(PT[:, half(slot, g), 1, 0:gn * P], bank[4 + half(slot, g)][:, 0:gn * P],
                                          PT[:, half(slot, g), 0, 0:gn * P].bitcast(F32), ALU.subtract).then_inc(lo_ready, 1)
                    dve.wait_ge(exp_done, t + 1)
                    dve.reciprocal(SM[:, slot, 4:5], SM[:, slot, 1:2]).then_inc(factor, 1)
                    dve.wait_ge(factor, t * 2 + 1)
                    dve.scalar_tensor_tensor(SM[:, slot, 5:6], SM[:, slot, 4:5], SM[:, slot, 3:4],
                                             NATT[:, bass.ds(t, 1)], ALU.mult, ALU.mult).then_inc(factor, 1)
                    dve.wait_ge(x_in[slot], (uses + 1) * 16 + (16 if last else 0))
                    if not first:
                        dve.wait_ge(x_out[slot], uses * 16)
                    dve.tensor_tensor(XO[:, slot, :], XB[:, slot, :], BB[:], ALU.add).then_inc(x_ready, 1)
                    dve.wait_ge(factor, t * 2 + 2)
                    dve.wait_ge(pv_group, (t + 1) * NG)
                    dve.wait_ge(x_ready, t + 1)
                    dve.scalar_tensor_tensor(XO[:, slot, :], bank[6 + slot][:, D:2 * D], SM[:, slot, 5:6],
                                             XO[:, slot, :], ALU.mult, ALU.add).then_inc(out_part, 1)
                    dve.wait_ge(out_part, t + 1)
                    dve.scalar_tensor_tensor(XO[:, slot, :], bank[6 + slot][:, 0:D], SM[:, slot, 5:6],
                                             XO[:, slot, :], ALU.mult, ALU.add).then_inc(out_ready, 1)

                dve.wait_ge(bias_in, 16)
                score(0, 0, True)
                tiles(dve, T, step)

            @block.tensor
            def _(pe):
                def scores(t, slot, first):
                    pe.wait_ge(h_ready, t + 1)
                    for c, (c0, cn) in enumerate(CHUNKS):
                        if c >= 4:
                            pe.wait_ge(masked, t * NC + c - 3)
                        elif not first or slot:
                            pe.wait_ge(masked, t * NC - NC + 1 + max(x for x in range(NC) if x % 4 == c))
                        parts = [(0, 0), (0, 1), (1, 0)]
                        for n, (hs, hm) in enumerate(parts):
                            for k in range(KD):
                                ins = pe.matmul(bank[c % 4][:, 0:cn], HS[:, slot, hs, k, :], HT[:, hm, k, c0:c0 + cn],
                                                start=n == 0 and k == 0, stop=n == 2 and k == KD - 1)
                        ins.then_inc(qk_done, 1)

                def flip(t, slot, g, first):
                    g0, gn = GROUPS[g]
                    if not (first and slot == 0 and g < 2):
                        pe.wait_ge(lo_ready, t * NG + g - 1)
                    for j in range(gn):
                        ins = pe.transpose(bank[4 + half(slot, g)][:, j * P:(j + 1) * P],
                                           SC[:, slot, (g0 + j) * P:(g0 + j + 1) * P], ID[:])
                    ins.then_inc(flipped, 1)

                def step(t, uses, slot, first, last):
                    if not last:
                        scores(t + 1, 1 - slot, first and slot == 0)
                    pe.wait_ge(exp_done, t + 1)
                    flip(t, slot, 0, first)
                    if not first:
                        pe.wait_ge(out_ready, t - 1)
                    for g, (g0, gn) in enumerate(GROUPS):
                        if g + 1 < NG:
                            flip(t, slot, g + 1, first)
                        pe.wait_ge(lo_ready, t * NG + g + 1)
                        for j in range(gn):
                            jt = g0 + j
                            part = PT[:, half(slot, g), :, j * P:(j + 1) * P]
                            if jt < T - 1:
                                pe.matmul(bank[6 + slot][:, :], part[:, 0, :], SUP[:, jt, :, :].rearrange("p a d -> p (a d)"),
                                          start=jt == 0, stop=False)
                            ins = pe.matmul(bank[6 + slot][:, 0:D], part[:, 1, :], SUP[:, jt, 0, :],
                                            start=False, stop=False)
                            if jt == T - 1:
                                ins = pe.matmul(bank[6 + slot][:, :], part[:, 0, :], SUP[:, jt, :, :].rearrange("p a d -> p (a d)"),
                                                start=False, stop=True)
                        ins.then_inc(pv_group, 1)
                pe.wait_ge(consts, 2)
                scores(0, 0, True)
                tiles(pe, T, step)


def combine(nc, a, bank, x_in, gates, x_out, parts):
    with ExitStack() as ctx:
        s = Stage(nc, ctx, "comb1" if parts is not None else "comb2")
        X = s.sb("x", [P, T, D])
        Y = s.sb("y", [P, 2, T, D])
        mid = T // 2
        spans = [(0, mid), (mid, T)]
        x_loaded = [s.sem(f"x_loaded{i}") for i in range(2)]
        y_loaded = [s.sem(f"y_loaded{i}") for i in range(2)]
        first_added, added = s.sem("first_added"), s.sem("added")
        x_stored = s.sem("x_stored")
        chain = s.sem("dve_chain")
        var_ready, std_ready = s.sem("variance_ready"), s.sem("std_ready")
        normed, hi_ready = s.sem("normed"), s.sem("hi_ready")
        if parts is not None:
            ST = s.sb("stats", [P, T, 6])
            MV = s.sb("mean_var", [P, 4, T])

        def by_tile(dram):
            return dram.rearrange("(t p) d -> p t d", p=P)

        with nc.Block() as block:
            @block.sync
            def _(sp):
                for n, (lo, hi) in enumerate(spans):
                    sp.dma_start(X[:, lo:hi, :], by_tile(x_in)[:, lo:hi, :]).then_inc(x_loaded[n], 16)
                    for k in range(2):
                        sp.dma_start(Y[:, k, lo:hi, :], by_tile(a["y"][k * NP:(k + 1) * NP, :])[:, lo:hi, :]).then_inc(y_loaded[n], 16)
                if parts is not None:
                    for n, (lo, hi) in enumerate(spans):
                        sp.wait_ge(added, hi)
                        sp.dma_start(by_tile(x_out)[:, lo:hi, :], X[:, lo:hi, :]).then_inc(x_stored, 16)
                    sp.wait_ge(x_stored, 32)
                else:
                    base = (T - 1) * P
                    for lo, hi in ((0, mid), (mid, T - 1)):
                        sp.wait_ge(added, hi)
                        sp.dma_start(x_out[lo * P:hi * P, :].rearrange("(t p) d -> p t d", p=P), X[:, lo:hi, :]).then_inc(x_stored, 16)
                    sp.wait_ge(added, T)
                    sp.dma_start(x_out[base:base + TAIL_A, :], X[0:TAIL_A, T - 1, :]).then_inc(x_stored, 16)
                    sp.dma_start(x_out[base + TAIL_A:N, :], X[TAIL_A:TAIL, T - 1, :]).then_inc(x_stored, 16)
                    sp.wait_ge(x_stored, 64)

            @block.vector
            def _(dve):
                for n, (lo, hi) in enumerate(spans):
                    dve.wait_ge(x_loaded[n], 16)
                    dve.wait_ge(y_loaded[n], 32)
                    with dve.Fori(lo, hi) as t:
                        dve.scalar_tensor_tensor(X[:, t, :], Y[:, 0, t, :], gates[:, 0, bass.ds(t, 1)], X[:, t, :],
                                                 ALU.mult, ALU.add).then_inc(first_added, 1)
                        dve.wait_ge(first_added, t + 1)
                        dve.scalar_tensor_tensor(X[:, t, :], Y[:, 1, t, :], gates[:, 1, bass.ds(t, 1)], X[:, t, :],
                                                 ALU.mult, ALU.add).then_inc(added, 1)
                if parts is None:
                    return
                link = Chain(dve, chain)
                row_statistics(dve, link, X, ST, MV, [(added, mid), (added, T), (added, T)], var_ready, std_ready)
                with dve.Fori(0, T) as t:
                    dve.tensor_scalar(Y[:, 0, t, :], X[:, t, :], MV[:, 0, bass.ds(t, 1)], MV[:, 1, bass.ds(t, 1)],
                                      ALU.subtract, ALU.mult).then_inc(normed, 1)
                with dve.Fori(0, T) as t:
                    dve.wait_ge(hi_ready, t + 1)
                    dve.tensor_tensor(parts[:, t, 1, :], Y[:, 0, t, :], parts[:, t, 0, :], ALU.subtract)

            @block.scalar
            def _(act):
                if parts is None:
                    return
                square_root(act, MV, var_ready, std_ready)
                with act.Fori(0, T) as t:
                    act.wait_ge(normed, t + 1)
                    act.copy(parts[:, t, 0, :], Y[:, 0, t, :]).then_inc(hi_ready, 1)


def route(nc, a, bank, name, x_in, gate_w, gate_b, r):
    with ExitStack() as ctx:
        s = Stage(nc, ctx, name)
        X = s.sb("x", [P, T, D])
        ST = s.sb("stats", [P, T, 6])
        MV = s.sb("mean_var", [P, 4, T])
        XS = s.sb("normed", [P, 2, D])
        XT = s.sb("normed_t", [P, 2, KD, P])
        GW = s.sb("gate_w", [P, KD, E])
        GB = s.sb("gate_b", [P, E])
        ID = s.sb("identity", [P, P])
        ONES = s.sb("ones", [P, P])
        BEFORE = s.sb("before", [P, P])
        VAL = s.sb("valid", [P, T])
        IE, IK, IQ = s.sb("iota_expert", [P, E]), s.sb("iota_tile", [P, T]), s.sb("iota_place", [P, P])
        IS, ROW = s.sb("iota_slot_tile", [P, S]), s.sb("empty_row", [P, S])
        PAIR = s.sb("pair", [P, 2, T])
        LG = s.sb("logits", [P, T, E])
        W3D = [s.sb(f"work{i}", [P, T, E]) for i in range(3)]
        OH = [s.sb(f"one_hot{i}", [P, T, E]) for i in range(2)]
        TOP = s.sb("top", [P, 4, T])
        SCAN = [s.sb(f"scan{i}", [P, E, T]) for i in range(3)]
        EX = [s.sb(f"per_expert{i}", [P, E]) for i in range(4)]
        SL, SI, QI = s.sb("slot", [P, 2, T]), s.sb("slot_int", [P, 2, T], I32), s.sb("place_int", [P, 2, T], I32)
        SF, QF = s.sb("slot_tile", [P, 2, T]), s.sb("slot_place", [P, 2, T])
        OQ, OS = s.sb("hot_place", [P, 2, 2, P]), s.sb("hot_tile", [P, 2, 2, S])
        EC = s.sb("expert_cmp", [P, S, E])
        V = [s.sb(f"value{i}", [P, S]) for i in range(3)]
        halves = [s.sem("x_first_half"), s.sem("x_second_half")]
        gate_in = s.sem("gate_loaded")
        consts, c0 = s.sem("constants_ready"), s.sem("constants_begun")
        chain = s.sem("dve_chain")
        var_ready, std_ready = s.sem("variance_ready"), s.sem("std_ready")
        normed, transposed, xt_ready = s.sem("normed"), s.sem("transposed"), s.sem("xt_ready")
        gated, logit_ready = s.sem("gated"), s.sem("logit_ready")
        kept, xn_stored = s.sem("normed_kept"), s.sem("normed_stored")
        diff_ready, exp_ready = s.sem("difference_ready"), s.sem("gate_exp_ready")
        used_ready, counted = s.sem("pairs_ready"), s.sem("pairs_counted")
        hot_ready, hot_used = s.sem("one_hots_ready"), s.sem("one_hots_used")
        mid = T // 2
        NCONST = 10
        with nc.Block() as block:
            @block.sync
            def _(sp):
                view = x_in.rearrange("(t p) d -> p t d", p=P)
                sp.dma_start(X[:, 0:mid, :], view[:, 0:mid, :]).then_inc(halves[0], 16)
                sp.dma_start(X[:, mid:T, :], view[:, mid:T, :]).then_inc(halves[1], 16)
                sp.dma_start(GW[:], gate_w).then_inc(gate_in, 16)
                if gate_b is not None:
                    sp.dma_start(GB[:], gate_b.partition_broadcast(P)).then_inc(gate_in, 16)
                out = a["xn"].rearrange("(t p) d -> p t d", p=P)
                for lo, hi in ((0, mid), (mid, T)):
                    sp.wait_ge(kept, hi)
                    sp.dma_start(out[:, lo:hi, :], X[:, lo:hi, :]).then_inc(xn_stored, 16)
                sp.wait_ge(xn_stored, 32)

            @block.gpsimd
            def _(pool):
                pool.memset(ID[:], 0.0).then_inc(c0, 1)
                pool.memset(BEFORE[:], 1.0).then_inc(c0, 1)
                pool.memset(VAL[:], 1.0).then_inc(c0, 1)
                if gate_b is None:
                    pool.memset(GB[:], 0.0).then_inc(consts, 1)
                else:
                    pool.memset(ST[:, 0, :], 0.0).then_inc(consts, 1)
                pool.wait_ge(c0, 3)
                pool.affine_select(out=ID[:], in_=ID[:], compare_op=ALU.not_equal, fill=1.0, base=0,
                                   pattern=[[-1, P]], channel_multiplier=1).then_inc(consts, 1)
                pool.affine_select(out=BEFORE[:], in_=BEFORE[:], compare_op=ALU.is_gt, fill=0.0, base=0,
                                   pattern=[[1, P]], channel_multiplier=-1).then_inc(consts, 1)
                pool.affine_select(out=VAL[:], in_=VAL[:], compare_op=ALU.is_gt, fill=0.0, base=N,
                                   pattern=[[-P, T]], channel_multiplier=-1).then_inc(consts, 1)
                small = dict(allow_small_or_imprecise_dtypes=True)
                pool.iota(IE[:], [[1, E]], base=0, channel_multiplier=0, **small).then_inc(consts, 1)
                pool.iota(IK[:], [[P, T]], base=0, channel_multiplier=0, **small).then_inc(consts, 1)
                pool.iota(IQ[:], [[1, P]], base=0, channel_multiplier=0, **small).then_inc(consts, 1)
                pool.iota(IS[:], [[1, S]], base=0, channel_multiplier=0, **small).then_inc(consts, 1)
                pool.iota(ROW[:], [[P, S]], base=PAIR_ROWS + 1, channel_multiplier=1, **small).then_inc(consts, 1)
                pool.iota(PAIR[:], [[NP, 2], [P, T]], base=1, channel_multiplier=1, **small).then_inc(consts, 1)

                def keep(t, uses, slot, first, last):
                    pool.wait_ge(normed, t + 1)
                    pool.tensor_copy(X[:, t, :], XS[:, slot, :]).then_inc(kept, 1)
                tiles(pool, T, keep)

            @block.tensor
            def _(pe):
                def flip(t, slot, first):
                    pe.wait_ge(normed, t + 1)
                    if not first:
                        pe.wait_ge(xt_ready, t - 1)
                    for k in range(KD):
                        last = pe.transpose(bank[slot][:, k * P:(k + 1) * P], XS[:, slot, k * P:(k + 1) * P], ID[:])
                    last.then_inc(transposed, 1)

                def step(t, uses, slot, first, last):
                    if not last:
                        flip(t + 1, 1 - slot, first and slot == 0)
                    pe.wait_ge(xt_ready, t + 1)
                    if not first:
                        pe.wait_ge(logit_ready, t - 1)
                    for k in range(KD):
                        ins = pe.matmul(bank[2 + slot][:, 0:E], XT[:, slot, k, :], GW[:, k, :], start=k == 0, stop=k == KD - 1)
                    ins.then_inc(gated, 1)

                pe.wait_ge(consts, NCONST)
                flip(0, 0, True)
                pe.wait_ge(gate_in, 16 if gate_b is None else 32)
                tiles(pe, T, step)
                pe.wait_ge(used_ready, 1)
                used = W3D[0][:].rearrange("p t e -> p (t e)")
                pe.matmul(bank[6][:, 0:T * E], BEFORE[:], used, start=True, stop=True)
                pe.matmul(bank[7][:, 0:T * E], ONES[:], used, start=True, stop=True).then_inc(counted, 1)

                def invert(t, uses, slot, first, last):
                    pe.wait_ge(hot_ready, t + 1)
                    for k in range(2):
                        ins = pe.matmul(bank[0][:, 0:S], OQ[:, slot, k, :], OS[:, slot, k, :],
                                        start=first and slot == 0 and k == 0, stop=last and k == 1)
                    ins.then_inc(hot_used, 1)
                tiles(pe, T, invert)

            @block.scalar
            def _(act):
                square_root(act, MV, var_ready, std_ready)

                def copy_t(t, uses, slot, first, last):
                    act.wait_ge(transposed, t + 1)
                    if not first:
                        act.wait_ge(gated, t - 1)
                    act.copy(XT[:, slot, :, :], bank[slot][:, 0:D].rearrange("p (k n) -> p k n", k=KD)).then_inc(xt_ready, 1)
                tiles(act, T, copy_t)
                act.wait_ge(diff_ready, 1)
                act.activation(TOP[:, 3, :], TOP[:, 2, :], ACT.Exp).then_inc(exp_ready, 1)

            @block.vector
            def _(dve):
                link = Chain(dve, chain)
                link(dve.memset(ONES[:], 1.0))
                dve.wait_ge(consts, NCONST)
                row_statistics(dve, link, X, ST, MV, [(halves[0], 16), (halves[1], 16), (halves[1], 16)],
                               var_ready, std_ready)
                dve.wait_ge(gate_in, 16 if gate_b is None else 32)

                def norm(t, slot, first):
                    if not first:
                        dve.wait_ge(transposed, t - 1)
                        dve.wait_ge(kept, t - 1)
                    dve.tensor_scalar(XS[:, slot, :], X[:, t, :], MV[:, 0, bass.ds(t, 1)], MV[:, 1, bass.ds(t, 1)],
                                      ALU.subtract, ALU.mult).then_inc(normed, 1)

                def step(t, uses, slot, first, last):
                    if not last:
                        norm(t + 1, 1 - slot, first and slot == 0)
                    dve.wait_ge(gated, t + 1)
                    dve.tensor_tensor(LG[:, t, :], bank[2 + slot][:, 0:E], GB[:], ALU.add).then_inc(logit_ready, 1)
                norm(0, 0, True)
                tiles(dve, T, step)
                dve.wait_ge(logit_ready, T)

                def per_tile(v):
                    return v.unsqueeze(2).to_broadcast([P, T, E])

                def per_expert(v):
                    return v.unsqueeze(1).to_broadcast([P, T, E])

                A, B, C = (w[:] for w in W3D)
                m = [TOP[:, 0, :], TOP[:, 1, :]]
                rest = LG[:]
                for k in range(2):
                    link(dve.reduce_max(m[k], rest, AX))
                    link(dve.tensor_tensor(A, rest, per_tile(m[k]), ALU.is_equal))
                    link(dve.scalar_tensor_tensor(B, A, -float(E), per_expert(IE[:]), ALU.mult, ALU.add))
                    link(dve.tensor_reduce(out=TOP[:, 2, :], in_=B, axis=AX, op=ALU.min))
                    link(dve.tensor_tensor(OH[k][:], B, per_tile(TOP[:, 2, :]), ALU.is_equal))
                    if k == 0:
                        link(dve.scalar_tensor_tensor(C, OH[0][:], -3.0e38, rest, ALU.mult, ALU.add))
                        rest = C
                dve.tensor_tensor(TOP[:, 2, :], m[1], m[0], ALU.subtract).then_inc(diff_ready, 1)
                link(dve.tensor_tensor(B, OH[0][:], OH[1][:], ALU.add))
                dve.tensor_tensor(A, B, per_tile(VAL[:]), ALU.mult).then_inc(used_ready, 1)
                dve.wait_ge(exp_ready, 1)
                link(dve.tensor_scalar(TOP[:, 2, :], TOP[:, 3, :], 1.0, None, ALU.add))
                link(dve.reciprocal(r["gates"][:, 0, :], TOP[:, 2, :]))
                link(dve.tensor_tensor(r["gates"][:, 1, :], r["gates"][:, 0, :], TOP[:, 3, :], ALU.mult))
                dve.wait_ge(counted, 1)
                tot, ping, pong = (v[:] for v in SCAN)
                link(dve.tensor_copy(tot, bank[7][:, 0:T * E].rearrange("p (t e) -> p e t", e=E)))
                src, dst, other = tot, ping, pong
                shift = 1
                while shift < T:
                    dve.tensor_copy(dst[:, :, 0:shift], src[:, :, 0:shift]).then_inc(chain, 1)
                    link.n += 1
                    link(dve.tensor_tensor(dst[:, :, shift:T], src[:, :, shift:T], src[:, :, 0:T - shift], ALU.add))
                    src, dst, other = dst, other, dst
                    shift *= 2
                count, held, ends, more = (v[:] for v in EX)
                link(dve.tensor_copy(count.unsqueeze(2), src[:, :, T - 1:T]))
                link(dve.tensor_tensor(dst, count.unsqueeze(2).to_broadcast([P, E, T]),
                                       IK[:].unsqueeze(1).to_broadcast([P, E, T]), ALU.is_gt))
                link(dve.reduce_sum(held, dst, AX))
                e_src, e_dst, e_other = held, ends, more
                shift = 1
                while shift < E:
                    dve.tensor_copy(e_dst[:, 0:shift], e_src[:, 0:shift]).then_inc(chain, 1)
                    link.n += 1
                    link(dve.tensor_tensor(e_dst[:, shift:E], e_src[:, shift:E], e_src[:, 0:E - shift], ALU.add))
                    e_src, e_dst, e_other = e_dst, e_other, e_dst
                    shift *= 2
                ends = e_src
                link(dve.tensor_tensor(EC[:], ends.unsqueeze(1).to_broadcast([P, S, E]),
                                       IS[:].unsqueeze(2).to_broadcast([P, S, E]), ALU.is_le))
                link(dve.reduce_sum(V[0][:], EC[:], AX))
                link(dve.tensor_scalar(V[1][:], V[0][:], E - 1.0, None, ALU.min))
                link(dve.tensor_copy(r["expert"][:], V[1][:]))
                link(dve.tensor_tensor(count, ends, held, ALU.subtract))
                link(dve.tensor_scalar(count, count, float(P), None, ALU.mult))
                link(dve.tensor_tensor(A, src.rearrange("p e t -> p t e"), tot.rearrange("p e t -> p t e"), ALU.subtract))
                link(dve.tensor_tensor(B, A, bank[6][:, 0:T * E].rearrange("p (t e) -> p t e", e=E), ALU.add))
                link(dve.tensor_tensor(A, B, per_expert(count), ALU.add))
                link(dve.tensor_scalar(TOP[:, 0, :], VAL[:], -float(S * P), float(S * P), ALU.mult, ALU.add))
                for k in range(2):
                    link(dve.tensor_tensor(B, A, OH[k][:], ALU.mult))
                    link(dve.reduce_sum(TOP[:, 1, :], B, AX))
                    link(dve.tensor_tensor(TOP[:, 2, :], TOP[:, 1, :], VAL[:], ALU.mult))
                    link(dve.tensor_tensor(SL[:, k, :], TOP[:, 2, :], TOP[:, 0, :], ALU.add))
                link(dve.tensor_copy(SI[:], SL[:]))
                link(dve.tensor_scalar(QI[:], SI[:], P - 1, None, ALU.bitwise_and))
                link(dve.tensor_copy(QF[:], QI[:]))
                link(dve.tensor_scalar(QI[:], SI[:], P.bit_length() - 1, None, ALU.arith_shift_right))
                link(dve.tensor_copy(SF[:], QI[:]))

                def hot(t, uses, slot, first, last):
                    if not first:
                        dve.wait_ge(hot_used, t - 1)
                    for k in range(2):
                        dve.tensor_scalar(OQ[:, slot, k, :], IQ[:], QF[:, k, bass.ds(t, 1)], None, ALU.is_equal)
                        ins = dve.tensor_scalar(OS[:, slot, k, :], IS[:], SF[:, k, bass.ds(t, 1)], PAIR[:, k, bass.ds(t, 1)],
                                                ALU.is_equal, ALU.mult)
                    ins.then_inc(hot_ready, 1)
                tiles(dve, T, hot)
                dve.wait_ge(hot_used, T)
                v0, v1, v2 = (v[:] for v in V)
                link(dve.tensor_copy(v0, bank[0][:, 0:S]))
                link(dve.tensor_scalar(v1, v0, 0.0, None, ALU.is_equal))
                link(dve.tensor_tensor(v2, v1, ROW[:], ALU.mult))
                link(dve.scalar_tensor_tensor(v1, v0, -1.0, v2, ALU.add, ALU.add))
                link(dve.tensor_copy(r["dst"][:], v1))
                link(dve.tensor_scalar(v1, v0, NP + 0.5, -float(NP), ALU.is_gt, ALU.mult))
                link(dve.scalar_tensor_tensor(v2, v0, -1.0, v1, ALU.add, ALU.add))
                link(dve.tensor_scalar(v1, v2, 0.0, None, ALU.max))
                link(dve.tensor_copy(r["tok"][:], v1))


def experts(nc, a, bank, name, w_in, b_in, w_out, b_out, H, r):
    gated = b_in is None
    KH = H // P
    HB = H // CH
    WIN = 2 * H if gated else H
    assert WIN == 2 * CH
    with ExitStack() as ctx:
        s = Stage(nc, ctx, name)
        WI = s.sb("w_in", [P, KD, E * WIN])
        WO = s.sb("w_out", [P, KH, E * D])
        ID = s.sb("identity", [P, P])
        XG = s.sb("x_gathered", [P, 2, D])
        TAKER = s.sb("wait_taker", [P, 2, 2])
        ZERO = s.sb("zero", [NP - N, D])
        zeroed, pad_stored = s.sem("zeroed"), s.sem("pad_stored")
        XT = s.sb("x_t", [P, 2, KD, P])
        PRE = s.sb("before_act", [P, 1 if gated else 2, WIN if not gated else H])
        HH = s.sb("hidden", [P, 2, H])
        HTT = s.sb("hidden_t", [P, 2, KH, P])
        YS = s.sb("y", [P, 2, D])
        TOKS, DSTS = s.sb("tok", [P, 2], I32), s.sb("dst", [P, 2], I32)
        if not gated:
            BI, BO = s.sb("b_in", [P, E * H]), s.sb("b_out", [P, E * D])
        consts = s.sem("identity_ready")
        w_in_loaded, w_out_loaded, b_loaded = s.sem("w_in_loaded"), s.sem("w_out_loaded"), s.sem("b_loaded")
        tok_ready, dst_ready = s.sem("tok_ready"), s.sem("dst_ready")
        gathered = [s.sem(f"gathered{i}") for i in range(2)]
        scattered = [s.sem(f"scattered{i}") for i in range(2)]
        x_flipped, xt_ready = s.sem("x_transposed"), s.sem("xt_ready")
        first_done, pre_ready, act_ready, h_ready = s.sem("first_product"), s.sem("pre_ready"), s.sem("act_ready"), s.sem("hidden_ready")
        h_flipped, ht_ready = s.sem("hidden_transposed"), s.sem("hidden_t_ready")
        second_done, y_ready = s.sem("second_product"), s.sem("y_ready")
        h_done = act_ready if not gated else h_ready
        with nc.Block() as block:
            @block.sync
            def _(sp):
                sp.wait_ge(zeroed, 1)
                for k in range(2):
                    sp.dma_start(a["y"][k * NP + N:k * NP + NP, :], ZERO[:]).then_inc(pad_stored, 16)
                sp.dma_start(WI[:, 0, :], w_in[:, 0, :]).then_inc(w_in_loaded, 16)
                sp.dma_start(WI[:, 1, :], w_in[:, 1, :]).then_inc(w_in_loaded, 16)
                if not gated:
                    sp.dma_start(BI[:], b_in.partition_broadcast(P)).then_inc(b_loaded, 16)
                    sp.dma_start(BO[:], b_out.partition_broadcast(P)).then_inc(b_loaded, 16)
                sp.dma_start(WO[:], w_out).then_inc(w_out_loaded, 16)
                sp.wait_ge(pad_stored, 32)

            @block.gpsimd
            def _(pool):
                pool.memset(ZERO[:], 0.0).then_inc(zeroed, 1)
                pool.memset(ID[:], 0.0).then_inc(consts, 1)
                pool.wait_ge(consts, 1)
                pool.affine_select(out=ID[:], in_=ID[:], compare_op=ALU.not_equal, fill=1.0, base=0,
                                   pattern=[[-1, P]], channel_multiplier=1).then_inc(consts, 1)

                def gather(t, uses, slot, first):
                    if not first:
                        pool.wait_ge(x_flipped, t - 1)
                    pool.tensor_copy(TOKS[:, slot:slot + 1], r["tok"][:, bass.ds(t, 1)]).then_inc(tok_ready, 1)
                    pool.wait_ge(tok_ready, t + 1)
                    pool.tensor_tensor(TAKER[:, 0, slot:slot + 1], ID[:, 0:1], ID[:, 0:1], ALU.add)
                    pool.indirect_dma_start(out=XG[:, slot, :], out_offset=None, in_=a["xn"],
                                            in_offset=bass.IndirectOffsetOnAxis(ap=TOKS[:, slot:slot + 1], axis=0)
                                            ).then_inc(gathered[slot], 16)

                def step(t, uses, slot, first, last):
                    if not last:
                        gather(t + 1, uses + slot, 1 - slot, first and slot == 0)
                    if not (first and slot == 0):
                        scatter(t - 1, uses - (1 - slot), 1 - slot, first)
                    if last:
                        scatter(t, uses, slot, False)

                def scatter(t, uses, slot, first):
                    if not first:
                        pool.wait_ge(scattered[slot], uses * 16)
                    pool.tensor_copy(DSTS[:, slot:slot + 1], r["dst"][:, bass.ds(t, 1)]).then_inc(dst_ready, 1)
                    pool.wait_ge(dst_ready, t + 1)
                    pool.wait_ge(y_ready, t + 1)
                    pool.tensor_tensor(TAKER[:, 1, slot:slot + 1], ID[:, 0:1], ID[:, 0:1], ALU.add)
                    pool.indirect_dma_start(out=a["y"], out_offset=bass.IndirectOffsetOnAxis(ap=DSTS[:, slot:slot + 1], axis=0),
                                            in_=YS[:, slot, :], in_offset=None).then_inc(scattered[slot], 16)
                pool.wait_ge(consts, 2)
                gather(0, 0, 0, True)
                tiles(pool, S, step)
                pool.wait_ge(scattered[0], (S + 1) // 2 * 16)
                pool.wait_ge(scattered[1], S // 2 * 16)

            @block.tensor
            def _(pe):
                def expert_of(t):
                    return pe.value_load(r["expert"][0:1, bass.ds(t, 1)], min_val=0, max_val=E - 1)

                def first_layer(t, uses, slot, first):
                    pe.wait_ge(gathered[slot], (uses + 1) * 16)
                    if not (first and slot == 0):
                        pe.wait_ge(xt_ready, t)
                    for k in range(KD):
                        ins = pe.transpose(bank[0][:, k * P:(k + 1) * P], XG[:, slot, k * P:(k + 1) * P], ID[:])
                    ins.then_inc(x_flipped, 1)
                    e = expert_of(t)
                    pe.wait_ge(xt_ready, t + 1)
                    if not first:
                        pe.wait_ge(h_ready if gated else pre_ready, t - 1)
                    for b in range(2):
                        for k in range(KD):
                            ins = pe.matmul(bank[2 + 2 * slot + b][:, :], XT[:, slot, k, :],
                                            WI[:, k, bass.ds(e * WIN + b * CH, CH)], start=k == 0, stop=k == KD - 1)
                    ins.then_inc(first_done, 1)

                def second_layer(t, uses, slot, first):
                    pe.wait_ge(h_done, t + 1)
                    for j in range(HB):
                        which = slot if HB == 1 else j
                        if not (first and (HB > 1) <= (slot == 0)):
                            pe.wait_ge(ht_ready, t * HB + j - 1)
                        for k in range(4):
                            ins = pe.transpose(bank[1 if which == 0 else 6][:, k * P:(k + 1) * P],
                                               HH[:, slot, (4 * j + k) * P:(4 * j + k + 1) * P], ID[:])
                        ins.then_inc(h_flipped, 1)
                    e = expert_of(t)
                    pe.wait_ge(ht_ready, (t + 1) * HB)
                    if not (first and slot == 0):
                        pe.wait_ge(y_ready, t)
                    for k in range(KH):
                        ins = pe.matmul(bank[7][:, 0:D], HTT[:, slot, k, :], WO[:, k, bass.ds(e * D, D)],
                                        start=k == 0, stop=k == KH - 1)
                    ins.then_inc(second_done, 1)

                def step(t, uses, slot, first, last):
                    if not last:
                        first_layer(t + 1, uses + slot, 1 - slot, first and slot == 0)
                    second_layer(t, uses, slot, first)

                pe.wait_ge(consts, 2)
                pe.wait_ge(w_in_loaded, 32)
                first_layer(0, 0, 0, True)
                pe.wait_ge(w_out_loaded, 16)
                tiles(pe, S, step)

            @block.scalar
            def _(act):
                def copy_x(t, slot, first):
                    act.wait_ge(x_flipped, t + 1)
                    if not first:
                        act.wait_ge(first_done, t - 1)
                    act.copy(XT[:, slot, :, :], bank[0][:, 0:D].rearrange("p (k n) -> p k n", k=KD)).then_inc(xt_ready, 1)

                def step(t, uses, slot, first, last):
                    if not last:
                        copy_x(t + 1, 1 - slot, first and slot == 0)
                    if gated:
                        act.wait_ge(first_done, t + 1)
                        if not (first and slot == 0):
                            act.wait_ge(h_ready, t)
                        act.activation(PRE[:, 0, :], bank[2 + 2 * slot][:, :], ACT.Silu).then_inc(act_ready, 1)
                    else:
                        act.wait_ge(pre_ready, t + 1)
                        if not first:
                            act.wait_ge(h_flipped, (t - 1) * HB)
                        act.activation(HH[:, slot, :], PRE[:, slot, :], ACT.Gelu).then_inc(act_ready, 1)
                    for j in range(HB):
                        which = slot if HB == 1 else j
                        act.wait_ge(h_flipped, t * HB + j + 1)
                        if not first:
                            act.wait_ge(second_done, t - 1)
                        act.copy(HTT[:, slot, 4 * j:4 * j + 4, :],
                                 bank[1 if which == 0 else 6][:, :].rearrange("p (k n) -> p k n", n=P)).then_inc(ht_ready, 1)
                copy_x(0, 0, True)
                tiles(act, S, step)

            @block.vector
            def _(dve):
                def middle(t, uses, slot, first, last):
                    if gated:
                        dve.wait_ge(act_ready, t + 1)
                        if not first:
                            dve.wait_ge(h_flipped, t - 1)
                        dve.tensor_tensor(HH[:, slot, :], PRE[:, 0, :], bank[3 + 2 * slot][:, :], ALU.mult).then_inc(h_ready, 1)
                    else:
                        e = dve.value_load(r["expert"][0:1, bass.ds(t, 1)], min_val=0, max_val=E - 1)
                        dve.wait_ge(first_done, t + 1)
                        if not first:
                            dve.wait_ge(act_ready, t - 1)
                        for b in range(2):
                            ins = dve.tensor_tensor(PRE[:, slot, b * CH:(b + 1) * CH], bank[2 + 2 * slot + b][:, :],
                                                    BI[:, bass.ds(e * H + b * CH, CH)], ALU.add)
                        ins.then_inc(pre_ready, 1)

                def result(t, uses, slot, first, last):
                    if not gated:
                        e = dve.value_load(r["expert"][0:1, bass.ds(t, 1)], min_val=0, max_val=E - 1)
                    dve.wait_ge(second_done, t + 1)
                    if not first:
                        dve.wait_ge(scattered[slot], uses * 16)
                    if gated:
                        dve.tensor_copy(YS[:, slot, :], bank[7][:, 0:D]).then_inc(y_ready, 1)
                    else:
                        dve.tensor_tensor(YS[:, slot, :], bank[7][:, 0:D], BO[:, bass.ds(e * D, D)], ALU.add).then_inc(y_ready, 1)

                def step(t, uses, slot, first, last):
                    if not last:
                        middle(t + 1, uses + slot, 1 - slot, first and slot == 0, False)
                    result(t, uses, slot, first, last)
                if not gated:
                    dve.wait_ge(b_loaded, 32)
                middle(0, 0, 0, True, False)
                tiles(dve, S, step)


def neighbours(nc, a, bank, XH):
    GS = [(g, min(8, T - g)) for g in range(0, T, 8)]
    G = len(GS)
    assert G % 2 == 0
    with ExitStack() as ctx:
        s = Stage(nc, ctx, "nbr")
        NEG = s.sb("mask", [P, 2, NP], BF16)
        ID, IDF = s.sb("identity", [P, P], BF16), s.sb("identity_f32", [P, P])
        AT = s.sb("adj_t", [P, 2, 8 * P], F16)
        WT = s.sb("w_t", [P, KD, D])
        BB = s.sb("bias", [P, D])
        XB, XO = s.sb("x", [P, 2, D]), s.sb("x_out", [P, 2, D])
        AGH, AG = s.sb("sum_hi", [P, 2, D]), s.sb("sum", [P, 2, D])
        AGT = s.sb("sum_t", [P, 2, KD, P])
        PRE = s.sb("before_relu", [P, 2, D])
        consts, w_loaded = s.sem("identity_ready"), s.sem("w_loaded")
        mask_in = [s.sem(f"mask_loaded{i}") for i in range(2)]
        x_loaded = [s.sem(f"x_loaded{i}") for i in range(2)]
        x_stored = [s.sem(f"x_stored{i}") for i in range(2)]
        flipped, at_ready, used = s.sem("mask_transposed"), s.sem("adj_t_ready"), s.sem("group_multiplied")
        at_odd = s.sem("adj_t_odd_ready")
        hi_ready, ag_ready, ag_flipped, agt_ready = s.sem("sum_hi_ready"), s.sem("sum_ready"), s.sem("sum_transposed"), s.sem("sum_t_ready")
        out_done, pre_ready, x_ready = s.sem("product_ready"), s.sem("pre_ready"), s.sem("x_ready")
        bf = [bank[i][:, :].bitcast(BF16) for i in range(2)]
        with nc.Block() as block:
            @block.sync
            def _(sp):
                sp.dma_start(WT[:], a["w_t"]).then_inc(w_loaded, 16)
                sp.dma_start(BB[:], a["b"].partition_broadcast(P)).then_inc(w_loaded, 16)

                def store(t, slot):
                    sp.wait_ge(x_ready, t + 1)
                    sp.dma_start(a["x3"][bass.ds(t * P, P), :], XO[:, slot, :]).then_inc(x_stored[slot], 16)

                def step(t, uses, slot, first, last):
                    if not first:
                        sp.wait_ge(flipped, (t - 1) * G)
                    sp.dma_start(NEG[:, slot, :], a["mask"][t, :, :]).then_inc(mask_in[slot], 16)
                    if not first:
                        store(t - 2, slot)
                    sp.dma_start(XB[:, slot, :], a["x2"][bass.ds(t * P, P), :]).then_inc(x_loaded[slot], 16)
                tiles(sp, T, step)
                store(T - 2, 0)
                store(T - 1, 1)
                for slot in range(2):
                    sp.wait_ge(x_stored[slot], T // 2 * 16)

            @block.gpsimd
            def _(pool):
                for n, i in enumerate((ID, IDF)):
                    pool.memset(i[:], 0.0).then_inc(consts, 1)
                    pool.wait_ge(consts, 2 * n + 1)
                    pool.affine_select(out=i[:], in_=i[:], compare_op=ALU.not_equal, fill=1.0, base=0,
                                       pattern=[[-1, P]], channel_multiplier=1).then_inc(consts, 1)

            @block.tensor
            def _(pe):
                def flip(t, uses, slot, g, first):
                    g0, gn = GS[g]
                    if g == 0:
                        pe.wait_ge(mask_in[slot], (uses + 1) * 16)
                    if not (first and slot == 0 and g < 2):
                        pe.wait_ge(at_ready if g % 2 == 0 else at_odd, t * (G // 2) + g // 2)
                    for j in range(gn):
                        ins = pe.transpose(bf[g % 2][:, j * P:(j + 1) * P], NEG[:, slot, (g0 + j) * P:(g0 + j + 1) * P], ID[:])
                    ins.then_inc(flipped, 1)

                def multiply(t, slot, g):
                    g0, gn = GS[g]
                    pe.wait_ge(at_ready if g % 2 == 0 else at_odd, t * (G // 2) + g // 2 + 1)
                    for j in range(gn):
                        ins = pe.matmul(bank[2 + slot][:, :], AT[:, g % 2, j * P:(j + 1) * P],
                                        XH[:, g0 + j, :, :].rearrange("p a d -> p (a d)"), start=g0 + j == 0, stop=g0 + j == T - 1)
                    ins.then_inc(used, 1)

                def finish(t, slot, first):
                    pe.wait_ge(ag_ready, t + 1)
                    if not first:
                        pe.wait_ge(x_ready, t - 1)
                    for k in range(KD):
                        ins = pe.transpose(bank[4 + slot][:, k * P:(k + 1) * P], AG[:, slot, k * P:(k + 1) * P], IDF[:])
                    ins.then_inc(ag_flipped, 1)

                def project_out(t, slot):
                    pe.wait_ge(agt_ready, t + 1)
                    for k in range(KD):
                        ins = pe.matmul(bank[6 + slot][:, 0:D], AGT[:, slot, k, :], WT[:, k, :], start=k == 0, stop=k == KD - 1)
                    ins.then_inc(out_done, 1)

                def step(t, uses, slot, first, last):
                    very_first = first and slot == 0
                    if not first:
                        pe.wait_ge(ag_ready, t - 1)
                    for g in range(G):
                        if g + 1 < G:
                            flip(t, uses, slot, g + 1, first)
                        elif not last:
                            flip(t + 1, uses + slot, 1 - slot, 0, first and slot == 0)
                        multiply(t, slot, g)
                        if g == 1 and not very_first:
                            finish(t - 1, 1 - slot, first)
                        if g == 2 and not very_first:
                            project_out(t - 1, 1 - slot)
                    if last:
                        finish(t, slot, False)
                        project_out(t, slot)
                pe.wait_ge(consts, 4)
                pe.wait_ge(w_loaded, 32)
                flip(0, 0, 0, 0, True)
                tiles(pe, T, step)

            @block.scalar
            def _(act):
                def even(t, slot, g, first):
                    act.wait_ge(flipped, t * G + g + 1)
                    if not (first and slot == 0 and g < 2):
                        act.wait_ge(used, t * G + g - 1)
                    w = GS[g][1] * P
                    act.activation(AT[:, 0, 0:w], bf[0][:, 0:w], ACT.Copy, bias=1.0, scale=1.0 / BIG).then_inc(at_ready, 1)

                def tail(t, slot, first):
                    act.wait_ge(used, (t + 1) * G)
                    if not first:
                        act.wait_ge(ag_ready, t - 1)
                    act.copy(AGH[:, slot, :], bank[2 + slot][:, 0:D]).then_inc(hi_ready, 1)

                def flip_out(t, slot, first):
                    act.wait_ge(ag_flipped, t + 1)
                    if not first:
                        act.wait_ge(out_done, t - 1)
                    act.copy(AGT[:, slot, :, :], bank[4 + slot][:, 0:D].rearrange("p (k n) -> p k n", k=KD)).then_inc(agt_ready, 1)

                def step(t, uses, slot, first, last):
                    for g in range(0, G, 2):
                        even(t, slot, g, first)
                        if g == 0 and not (first and slot == 0):
                            tail(t - 1, 1 - slot, first)
                    if not (first and slot == 0):
                        flip_out(t - 1, 1 - slot, first)
                    if last:
                        tail(t, slot, False)
                        flip_out(t, slot, False)
                tiles(act, T, step)

            @block.vector
            def _(dve):
                def odd(t, slot, g, first):
                    if not (first and slot == 0 and g < 2):
                        dve.wait_ge(used, t * G + g - 1)
                    dve.wait_ge(flipped, t * G + g + 1)
                    w = GS[g][1] * P
                    dve.tensor_scalar(AT[:, 1, 0:w], bf[1][:, 0:w], 1.0 / BIG, 1.0, ALU.mult, ALU.add).then_inc(at_odd, 1)

                def add(t, slot, first):
                    dve.wait_ge(hi_ready, t + 1)
                    if not first:
                        dve.wait_ge(ag_flipped, t - 1)
                    dve.tensor_tensor(AG[:, slot, :], bank[2 + slot][:, D:2 * D], AGH[:, slot, :], ALU.add).then_inc(ag_ready, 1)

                def finish(t, uses, slot, first):
                    dve.wait_ge(out_done, t + 1)
                    dve.tensor_tensor(PRE[:, slot, :], bank[6 + slot][:, 0:D], BB[:], ALU.add).then_inc(pre_ready, 1)
                    dve.wait_ge(x_loaded[slot], (uses + 1) * 16)
                    if not first:
                        dve.wait_ge(x_stored[slot], uses * 16)
                    dve.wait_ge(pre_ready, t + 1)
                    dve.scalar_tensor_tensor(XO[:, slot, :], PRE[:, slot, :], 0.0, XB[:, slot, :], ALU.max, ALU.add).then_inc(x_ready, 1)

                def step(t, uses, slot, first, last):
                    very_first = first and slot == 0
                    if not very_first:
                        add(t - 1, 1 - slot, first)
                    odd(t, slot, 1, first)
                    odd(t, slot, 3, first)
                    if not very_first:
                        finish(t - 1, uses - (1 - slot), 1 - slot, first)
                    if last:
                        add(t, slot, False)
                        finish(t, uses, slot, False)
                tiles(dve, T, step)


def build(nc, x, adj, weight, bias, node_w, edge_w, wg, bg, w13, w2, w_t, b, gate_t, w1_t, b1, w2_t, b2, out, stop=99):
    with ExitStack() as ctx:
        bank = [ctx.enter_context(nc.psum_tensor(f"bank{i}", [P, CH], F32)) for i in range(8)]

        def dram(name, shape, dt=F32):
            return nc.dram_tensor(name, shape, dt, kind="Internal").ap()

        def routing(name, keep):
            t = lambda what, shape, dt: keep.enter_context(nc.sbuf_tensor(f"{name}_{what}", shape, dt))
            return dict(gates=t("gates", [P, 2, T], F32), tok=t("tok", [P, S], I32), dst=t("dst", [P, S], I32),
                        expert=t("expert", [P, S], I32))

        a = dict(x=x, adj=adj, weight=weight, bias=bias, node_w=node_w, edge_w=edge_w, w_t=w_t, b=b)
        a["mask"] = dram("mask", [T, P, NP], BF16)
        for name in ("x1", "x2", "x3", "xn"):
            a[name] = dram(name, [NP, D])
        a["y"] = dram("y", [PAIR_ROWS + S * P, D])
        with ExitStack() as keep:
            a["HT"] = keep.enter_context(nc.sbuf_tensor("h_t", [P, 2, KD, NP], F32R))
            a["SUP"] = keep.enter_context(nc.sbuf_tensor("support", [P, T, 2, D], F32R))
            a["NATT"] = keep.enter_context(nc.sbuf_tensor("node_attention", [P, T], F32))
            project(nc, a, bank)
            attend(nc, a, bank)
        with ExitStack() as keep:
            if stop >= 2:
                r = routing("route0", keep)
                route(nc, a, bank, "gate0", a["x1"], wg, bg, r)
                experts(nc, a, bank, "ffn0", w13, None, w2, None, H0, r)
            if stop >= 3:
                XH = keep.enter_context(nc.sbuf_tensor("normed_parts", [P, T, 2, D], F16))
                combine(nc, a, bank, a["x1"], r["gates"], a["x2"], XH)
            if stop >= 4:
                neighbours(nc, a, bank, XH)
        with ExitStack() as keep:
            if stop >= 5:
                r = routing("route1", keep)
                route(nc, a, bank, "gate1", a["x3"], gate_t, None, r)
                experts(nc, a, bank, "ffn1", w1_t, b1, w2_t, b2, H1, r)
                combine(nc, a, bank, a["x3"], r["gates"], out, None)


def layout(i):
    import numpy as np

    def blocks(w):
        e, n, m = w.shape
        return np.ascontiguousarray(w.reshape(e, n // P, P, m).transpose(2, 1, 0, 3).reshape(P, n // P, e * m))

    w13 = np.concatenate([i["L0_ffn_W1"], i["L0_ffn_W3"]], axis=2)
    return dict(
        x=i["x"], adj=i["adj"], weight=i["L0_gnn_weight"], bias=i["L0_gnn_bias"], node_w=i["L0_gnn_node_w"],
        edge_w=i["L0_gnn_edge_w"], wg=blocks(i["L0_ffn_Wg"][None]), bg=i["L0_ffn_bg"], w13=blocks(w13),
        w2=blocks(i["L0_ffn_W2"]), w_t=blocks(i["L1_gnn_W"].T[None]), b=i["L1_gnn_b"],
        gate_t=blocks(i["L1_ffn_gate_w"].T[None]), w1_t=blocks(i["L1_ffn_w1"].transpose(0, 2, 1)),
        b1=i["L1_ffn_b1"].reshape(-1), w2_t=blocks(i["L1_ffn_w2"].transpose(0, 2, 1)), b2=i["L1_ffn_b2"].reshape(-1))


def kernel(**inputs):
    import numpy as np
    import concourse.bacc as bacc
    from concourse.bass_utils import run_bass_kernel_spmd

    nc = bacc.Bacc("TRN2", target_bir_lowering=False, num_devices=1)
    arrays, args = {}, []
    for name, value in layout({k: np.asarray(v) for k, v in inputs.items()}).items():
        value = np.ascontiguousarray(value)
        arrays[f"in_{name}"] = value
        args.append(nc.dram_tensor(f"in_{name}", value.shape, mybir.dt.from_np(value.dtype), kind="ExternalInput").ap())
    out = nc.dram_tensor("out_0", (N, D), F32, kind="ExternalOutput").ap()
    build(nc, *args, out)
    r = run_bass_kernel_spmd(nc, [arrays], core_ids=[0])
    return r.results[0]["out_0"]
```

```python
import concourse.bass as bass
from concourse import mybir
from contextlib import ExitStack

F32 = mybir.dt.float32
F32R = mybir.dt.float32r
F16 = mybir.dt.float16
BF16 = mybir.dt.bfloat16
I32 = mybir.dt.int32
ALU = mybir.AluOpType
ACT = mybir.ActivationFunctionType
AX = mybir.AxisListType.X
RMAX = bass.bass_isa.ReduceOp.max
RADD = bass.bass_isa.ReduceOp.add

P = 128
N = 3327
T = (N + P - 1) // P
NP = T * P
TAIL = N - (T - 1) * P
TAIL_A = TAIL // 16 * 16
D = 256
KD = D // P
EPS = 1e-5
BIG = 2.0 ** 100
CH = 512
CHUNKS = [(c, min(CH, NP - c)) for c in range(0, NP, CH)]
NC = len(CHUNKS)
GROUPS = [(g, min(4, T - g)) for g in range(0, T, 4)]
NG = len(GROUPS)
E = 8
H0 = 512
H1 = 1024
PAIRS = 2 * N
S = (PAIRS - E) // P + E
PAIR_ROWS = 2 * NP


def tiles(eng, count, step):
    turns = (count - 2) // 2
    step(0, 0, 0, True, False)
    step(1, 0, 1, True, False)
    with eng.Fori(1, turns) as i:
        step(i * 2, i, 0, False, False)
        step(i * 2 + 1, i, 1, False, False)
    for t in range(2 * turns, count):
        step(t, t // 2, t % 2, False, t == count - 1)


def known(t):
    return isinstance(t, int)


class Chain:

    def __init__(self, eng, sem):
        self.eng, self.sem, self.n = eng, sem, 0

    def __call__(self, ins):
        ins.then_inc(self.sem, 1)
        self.n += 1
        self.eng.wait_ge(self.sem, self.n)


class Stage:

    def __init__(self, nc, ctx, name):
        self.nc, self.ctx, self.name, self.sems = nc, ctx, name, []
        ctx.callback(self.end)

    def sb(self, name, shape, dt=F32):
        return self.ctx.enter_context(self.nc.sbuf_tensor(f"{self.name}_{name}", shape, dt))

    def sem(self, name):
        self.sems.append(self.nc.alloc_semaphore(f"{self.name}_{name}"))
        return self.sems[-1]

    def end(self):
        self.nc.clear_and_free_semaphores(self.sems)
        self.nc.all_engine_barrier()


def load_nodes(sp, X, src, halves, tail):
    full = src[0:(T - 1) * P, :].rearrange("(t p) d -> p t d", p=P)
    mid = T // 2
    sp.dma_start(X[:, 0:mid, :], full[:, 0:mid, :]).then_inc(halves[0], 16)
    sp.dma_start(X[:, mid:T - 1, :], full[:, mid:T - 1, :]).then_inc(halves[1], 16)
    base = (T - 1) * P
    sp.dma_start(X[0:TAIL_A, T - 1, :], src[base:base + TAIL_A, :]).then_inc(tail, 16)
    sp.dma_start(X[TAIL_A:TAIL, T - 1, :], src[base + TAIL_A:N, :]).then_inc(tail, 16)


def row_statistics(dve, link, X, ST, MV, arrived, var_ready, std_ready):
    mid = T // 2
    start = link.n
    for lo, hi, (sem, n) in ((0, mid, arrived[0]), (mid, T - 1, arrived[1]), (T - 1, T, arrived[2])):
        dve.wait_ge(sem, n)
        if hi - lo > 1:
            with dve.Fori(lo, hi) as t:
                dve.bn_stats(ST[:, t, :], X[:, t, :]).then_inc(link.sem, 1)
        else:
            dve.bn_stats(ST[:, lo, :], X[:, lo, :]).then_inc(link.sem, 1)
    link.n = start + T
    dve.wait_ge(link.sem, link.n)
    me, qe, mo, qo = (ST[:, :, k] for k in (1, 2, 4, 5))
    mean, rstd, var, tmp = (MV[:, k, :] for k in range(4))
    link(dve.tensor_tensor(tmp, me, mo, ALU.subtract))
    link(dve.tensor_tensor(mean, me, mo, ALU.add))
    link(dve.tensor_tensor(tmp, tmp, tmp, ALU.mult))
    link(dve.tensor_scalar(mean, mean, 0.5, None, ALU.mult))
    link(dve.tensor_tensor(var, qe, qo, ALU.add))
    link(dve.scalar_tensor_tensor(tmp, tmp, D / 4.0, var, ALU.mult, ALU.add))
    dve.tensor_scalar(var, tmp, 1.0 / D, EPS, ALU.mult, ALU.add).then_inc(var_ready, 1)
    dve.wait_ge(std_ready, 1)
    link(dve.reciprocal(rstd, tmp))
    link(dve.tensor_tensor(tmp, rstd, rstd, ALU.mult))
    link(dve.tensor_tensor(tmp, tmp, var, ALU.mult))
    link(dve.tensor_scalar(tmp, tmp, -0.5, 1.5, ALU.mult, ALU.add))
    link(dve.tensor_tensor(rstd, rstd, tmp, ALU.mult))


def square_root(act, MV, var_ready, std_ready):
    act.wait_ge(var_ready, 1)
    act.activation(MV[:, 3, :], MV[:, 2, :], ACT.Sqrt).then_inc(std_ready, 1)


def project(nc, a, bank):
    with ExitStack() as ctx:
        s = Stage(nc, ctx, "proj")
        X = s.sb("x", [P, T, D])
        ST = s.sb("stats", [P, T, 6])
        MV = s.sb("mean_var", [P, 4, T])
        XS = s.sb("normed", [P, 2, D])
        XT = s.sb("normed_t", [P, 2, KD, P])
        EW = s.sb("edge_w", [P, KD, D])
        WN = s.sb("weight_node", [P, KD, D + 1])
        ID = s.sb("identity", [P, P])
        NL = s.sb("node_logits", [P, T])
        VAL = s.sb("valid", [P, T])
        SM = s.sb("small", [P, 4])
        HT, SUP, NATT = a["HT"], a["SUP"], a["NATT"]
        halves = [s.sem("x_first_half"), s.sem("x_second_half")]
        tail = s.sem("x_last_tile")
        edge_in, node_in = s.sem("edge_w_loaded"), s.sem("weight_loaded")
        chain = s.sem("dve_chain")
        padded = s.sem("pad_zeroed")
        consts = s.sem("constants_ready")
        var_ready, std_ready = s.sem("variance_ready"), s.sem("std_ready")
        normed, transposed, xt_ready = s.sem("normed"), s.sem("transposed"), s.sem("xt_ready")
        projected, hi_ready, lo_ready = s.sem("projected"), s.sem("hi_ready"), s.sem("lo_ready")
        mx_ready, mx_all = s.sem("logit_max_ready"), s.sem("logit_max_all")
        nmx_ready, e_ready, sum_all = s.sem("neg_max_ready"), s.sem("exp_ready"), s.sem("sum_all")
        with nc.Block() as block:
            @block.sync
            def _(sp):
                sp.wait_ge(padded, 1)
                load_nodes(sp, X, a["x"], halves, tail)
                sp.dma_start(EW[:], a["edge_w"].rearrange("(k p) f -> p k f", p=P)).then_inc(edge_in, 16)
                sp.dma_start(WN[:, :, 0:D], a["weight"].rearrange("(k p) f -> p k f", p=P)).then_inc(node_in, 16)
                sp.dma_start(WN[:, :, D:D + 1], a["node_w"].rearrange("(k p) f -> p k f", p=P), allow_slow_non_contiguous=True).then_inc(node_in, 16)

            @block.gpsimd
            def _(pool):
                pool.memset(ID[:], 0.0).then_inc(consts, 1)
                pool.wait_ge(consts, 1)
                pool.affine_select(out=ID[:], in_=ID[:], compare_op=ALU.not_equal, fill=1.0, base=0,
                                   pattern=[[-1, P]], channel_multiplier=1).then_inc(consts, 1)
                pool.memset(VAL[:], 1.0).then_inc(consts, 1)
                pool.wait_ge(consts, 3)
                pool.affine_select(out=VAL[:], in_=VAL[:], compare_op=ALU.is_gt, fill=0.0, base=N,
                                   pattern=[[-P, T]], channel_multiplier=-1).then_inc(consts, 1)
                pool.wait_ge(mx_ready, 1)
                pool.partition_all_reduce(SM[:, 1:2], SM[:, 0:1], P, RMAX).then_inc(mx_all, 1)
                pool.wait_ge(e_ready, 1)
                pool.partition_all_reduce(SM[:, 3:4], SM[:, 2:3], P, RADD).then_inc(sum_all, 1)

            @block.vector
            def _(dve):
                link = Chain(dve, chain)
                dve.memset(X[:, T - 1, :], 0.0).then_inc(padded, 1)
                row_statistics(dve, link, X, ST, MV, [(halves[0], 16), (halves[1], 16), (tail, 32)],
                               var_ready, std_ready)

                def norm(t, slot, first):
                    if not first:
                        dve.wait_ge(transposed, t - 1)
                    dve.tensor_scalar(XS[:, slot, :], X[:, t, :], MV[:, 0, bass.ds(t, 1)], MV[:, 1, bass.ds(t, 1)],
                                      ALU.subtract, ALU.mult).then_inc(normed, 1)

                def step(t, uses, slot, first, last):
                    if not known(t) or t + 2 < T:
                        norm(t + 2, slot, False)
                    dve.wait_ge(hi_ready, t + 1)
                    dve.tensor_tensor(SUP[:, t, 1, :], bank[2 + slot][:, 0:D], SUP[:, t, 0, :].bitcast(F32), ALU.subtract)
                    dve.tensor_tensor(HT[:, 1, :, bass.ds(t * P, P)],
                                      bank[4 + slot][:, 0:D].rearrange("p (k n) -> p k n", k=KD),
                                      HT[:, 0, :, bass.ds(t * P, P)].bitcast(F32), ALU.subtract).then_inc(lo_ready, 1)

                norm(0, 0, True)
                norm(1, 1, True)
                tiles(dve, T, step)
                dve.wait_ge(lo_ready, T)
                dve.wait_ge(consts, 4)
                link(dve.tensor_tensor(NL[:], NL[:], VAL[:], ALU.mult))
                link(dve.tensor_scalar(VAL[:], VAL[:], BIG, -BIG, ALU.mult, ALU.add))
                link(dve.tensor_tensor(NL[:], NL[:], VAL[:], ALU.add))
                dve.reduce_max(SM[:, 0:1], NL[:], AX).then_inc(mx_ready, 1)
                dve.wait_ge(mx_all, 1)
                dve.tensor_scalar(SM[:, 1:2], SM[:, 1:2], -1.0, None, ALU.mult).then_inc(nmx_ready, 1)
                dve.wait_ge(sum_all, 1)
                link(dve.reciprocal(SM[:, 3:4], SM[:, 3:4]))
                link(dve.tensor_scalar(NATT[:], NATT[:], SM[:, 3:4], None, ALU.mult))

            @block.scalar
            def _(act):
                square_root(act, MV, var_ready, std_ready)

                def copy_t(t, slot, first):
                    act.wait_ge(transposed, t + 1)
                    if not first:
                        act.wait_ge(projected, t - 1)
                    act.copy(XT[:, slot, :, :], bank[slot][:, 0:D].rearrange("p (k n) -> p k n", k=KD)).then_inc(xt_ready, 1)

                def step(t, uses, slot, first, last):
                    if not last:
                        copy_t(t + 1, 1 - slot, first and slot == 0)
                    act.wait_ge(projected, t + 1)
                    act.copy(SUP[:, t, 0, :], bank[2 + slot][:, 0:D])
                    act.copy(NL[:, bass.ds(t, 1)], bank[2 + slot][:, D:D + 1])
                    act.copy(HT[:, 0, :, bass.ds(t * P, P)],
                             bank[4 + slot][:, 0:D].rearrange("p (k n) -> p k n", k=KD)).then_inc(hi_ready, 1)

                copy_t(0, 0, True)
                tiles(act, T, step)
                act.wait_ge(nmx_ready, 1)
                act.activation(NATT[:], NL[:], ACT.Exp, bias=SM[:, 1:2], accum_out=SM[:, 2:3]).then_inc(e_ready, 1)

            @block.tensor
            def _(pe):
                def flip(t, slot, first):
                    pe.wait_ge(normed, t + 1)
                    if not first:
                        pe.wait_ge(xt_ready, t - 1)
                    for k in range(KD):
                        last = pe.transpose(bank[slot][:, k * P:(k + 1) * P], XS[:, slot, k * P:(k + 1) * P], ID[:])
                    last.then_inc(transposed, 1)

                def step(t, uses, slot, first, last):
                    if not last:
                        flip(t + 1, 1 - slot, first and slot == 0)
                    pe.wait_ge(xt_ready, t + 1)
                    if not first:
                        pe.wait_ge(lo_ready, t - 1)
                    for k in range(KD):
                        pe.matmul(bank[2 + slot][:, 0:D + 1], XT[:, slot, k, :], WN[:, k, :], start=k == 0, stop=k == KD - 1)
                    for f in range(KD):
                        for k in range(KD):
                            ins = pe.matmul(bank[4 + slot][:, f * P:(f + 1) * P], EW[:, k, f * P:(f + 1) * P],
                                            XT[:, slot, k, :], start=k == 0, stop=k == KD - 1)
                    ins.then_inc(projected, 1)

                pe.wait_ge(consts, 2)
                flip(0, 0, True)
                pe.wait_ge(edge_in, 16)
                pe.wait_ge(node_in, 32)
                tiles(pe, T, step)


def attend(nc, a, bank):
    HT, SUP, NATT = a["HT"], a["SUP"], a["NATT"]
    with ExitStack() as ctx:
        s = Stage(nc, ctx, "attn")
        ADJ = s.sb("adj", [P, 2, NP])
        NEG = s.sb("mask", [P, 2, NP], BF16)
        SC = s.sb("scores", [P, 2, NP])
        HS = s.sb("h_tile", [P, 2, 2, KD, P], F32R)
        PT = s.sb("probs_t", [P, 2, 2, CH], F32R)
        ID = s.sb("identity", [P, P])
        XB = s.sb("x", [P, 2, D])
        XO = s.sb("x_out", [P, 2, D])
        BB = s.sb("bias", [P, D])
        MX = s.sb("max", [P, 2, NC])
        TAKER = s.sb("wait_taker", [P, 2, NC])
        SM = s.sb("small", [P, 2, 6])
        consts = s.sem("constants_ready")
        bias_in = s.sem("bias_loaded")
        edge = s.sem("pad_column_zeroed")
        adj_in = [s.sem(f"adj_loaded{i}") for i in range(2)]
        x_in = [s.sem(f"x_loaded{i}") for i in range(2)]
        mask_ready = s.sem("mask_ready")
        mask_out = [s.sem(f"mask_stored{i}") for i in range(2)]
        h_ready, qk_done, masked = s.sem("h_ready"), s.sem("scores_ready"), s.sem("scores_masked")
        neg_max, exp_done = s.sem("neg_max_ready"), s.sem("probs_ready")
        max_ready, out_part, out_ready = s.sem("max_ready"), s.sem("out_part"), s.sem("out_ready")
        flipped, hi_ready, lo_ready = s.sem("probs_transposed"), s.sem("probs_hi"), s.sem("probs_lo")
        pv_group = s.sem("group_multiplied")
        factor, x_ready = s.sem("factor_ready"), s.sem("x_out_ready")
        x_out = [s.sem(f"x_stored{i}") for i in range(2)]

        def rows(dram, t):
            return dram[bass.ds(t * P, P), :]

        def half(slot, g):
            return (slot + g) % 2

        with nc.Block() as block:
            @block.sync
            def _(sp):
                sp.wait_ge(edge, 1)
                sp.dma_start(BB[:], a["bias"].partition_broadcast(P)).then_inc(bias_in, 16)

                def store(t, slot):
                    sp.wait_ge(out_ready, t + 1)
                    sp.dma_start(rows(a["x1"], t), XO[:, slot, :]).then_inc(x_out[slot], 16)

                def step(t, uses, slot, first, last):
                    if not first:
                        sp.wait_ge(mask_ready, t - 1)
                    base = (T - 1) * P
                    tail = ((0, TAIL_A), (TAIL_A, TAIL))
                    if last:
                        for lo, hi in tail:
                            sp.dma_start(ADJ[lo:hi, slot, 0:N], a["adj"][base + lo:base + hi, :]).then_inc(adj_in[slot], 16)
                    else:
                        sp.dma_start(ADJ[:, slot, 0:N], rows(a["adj"], t)).then_inc(adj_in[slot], 16)
                    if not first:
                        store(t - 2, slot)
                    if last:
                        for lo, hi in tail:
                            sp.dma_start(XB[lo:hi, slot, :], a["x"][base + lo:base + hi, :]).then_inc(x_in[slot], 16)
                    else:
                        sp.dma_start(XB[:, slot, :], rows(a["x"], t)).then_inc(x_in[slot], 16)
                tiles(sp, T, step)
                store(T - 2, T % 2)
                store(T - 1, (T - 1) % 2)
                for slot in range(2):
                    sp.wait_ge(x_out[slot], T // 2 * 16)

            @block.gpsimd
            def _(pool):
                pool.memset(ID[:], 0.0).then_inc(consts, 1)
                pool.wait_ge(consts, 1)
                pool.affine_select(out=ID[:], in_=ID[:], compare_op=ALU.not_equal, fill=1.0, base=0,
                                   pattern=[[-1, P]], channel_multiplier=1).then_inc(consts, 1)
                pool.memset(ADJ[:, :, N:NP], 0.0).then_inc(edge, 1)

                def step(t, uses, slot, first, last):
                    pool.wait_ge(adj_in[slot], (uses + 1) * 16 + (16 if last else 0))
                    if not first:
                        pool.wait_ge(masked, (t - 1) * NC)
                        pool.wait_ge(mask_out[slot], uses * 16)
                    pool.tensor_copy(HS[:, slot, :, :, :].rearrange("p a k n -> p (a k) n"),
                                     HT[:, :, :, bass.ds(t * P, P)].rearrange("p a k n -> p (a k) n").bitcast(F32)).then_inc(h_ready, 1)
                    pool.tensor_scalar(NEG[:, slot, :], ADJ[:, slot, :], BIG, -BIG, ALU.mult, ALU.add).then_inc(mask_ready, 1)
                pool.wait_ge(edge, 1)
                tiles(pool, T, step)

            @block.scalar
            def _(act):
                def step(t, uses, slot, first, last):
                    act.wait_ge(mask_ready, t + 1)
                    act.dma_start(a["mask"][t, :, :], NEG[:, slot, :]).then_inc(mask_out[slot], 16)
                    act.wait_ge(neg_max, t + 1)
                    act.activation(SC[:, slot, :], SC[:, slot, :], ACT.Exp, bias=SM[:, slot, 0:1],
                                   accum_out=SM[:, slot, 1:2]).then_inc(exp_done, 1)
                    for g, (g0, gn) in enumerate(GROUPS):
                        act.wait_ge(flipped, t * NG + g + 1)
                        if not (first and slot == 0 and g < 2):
                            act.wait_ge(pv_group, t * NG + (g - 1))
                        act.copy(PT[:, half(slot, g), 0, 0:gn * P], bank[4 + half(slot, g)][:, 0:gn * P]).then_inc(hi_ready, 1)
                tiles(act, T, step)
                for slot in range(2):
                    act.wait_ge(mask_out[slot], T // 2 * 16)

            @block.vector
            def _(dve):
                def score(t, slot, first):
                    dve.wait_ge(mask_ready, t + 1)
                    if not first:
                        dve.wait_ge(flipped, (t - 1) * NG)
                    for c, (c0, cn) in enumerate(CHUNKS):
                        dve.wait_ge(qk_done, t * NC + c + 1)
                        dve.memset(TAKER[:, slot, c:c + 1], 0.0)
                        dve.tensor_tensor_reduce(out=SC[:, slot, c0:c0 + cn], in0=bank[c % 4][:, 0:cn],
                                                 in1=NEG[:, slot, c0:c0 + cn], scale=1.0, scalar=-3.0e38,
                                                 op0=ALU.add, op1=ALU.max,
                                                 accum_out=MX[:, slot, c:c + 1]).then_inc(masked, 1)
                    dve.wait_ge(masked, t * NC + NC)
                    dve.reduce_max(SM[:, slot, 2:3], MX[:, slot, :], AX).then_inc(max_ready, 1)
                    dve.wait_ge(max_ready, t + 1)
                    dve.tensor_scalar(SM[:, slot, 3:4], SM[:, slot, 2:3], -BIG / 2, None, ALU.is_gt)
                    dve.tensor_scalar(SM[:, slot, 0:1], SM[:, slot, 2:3], -1.0, None, ALU.mult).then_inc(neg_max, 1)

                def step(t, uses, slot, first, last):
                    if not last:
                        score(t + 1, 1 - slot, first and slot == 0)
                    for g, (g0, gn) in enumerate(GROUPS):
                        dve.wait_ge(hi_ready, t * NG + g + 1)
                        dve.tensor_tensor(PT[:, half(slot, g), 1, 0:gn * P], bank[4 + half(slot, g)][:, 0:gn * P],
                                          PT[:, half(slot, g), 0, 0:gn * P].bitcast(F32), ALU.subtract).then_inc(lo_ready, 1)
                    dve.wait_ge(exp_done, t + 1)
                    dve.reciprocal(SM[:, slot, 4:5], SM[:, slot, 1:2]).then_inc(factor, 1)
                    dve.wait_ge(factor, t * 2 + 1)
                    dve.scalar_tensor_tensor(SM[:, slot, 5:6], SM[:, slot, 4:5], SM[:, slot, 3:4],
                                             NATT[:, bass.ds(t, 1)], ALU.mult, ALU.mult).then_inc(factor, 1)
                    dve.wait_ge(x_in[slot], (uses + 1) * 16 + (16 if last else 0))
                    if not first:
                        dve.wait_ge(x_out[slot], uses * 16)
                    dve.tensor_tensor(XO[:, slot, :], XB[:, slot, :], BB[:], ALU.add).then_inc(x_ready, 1)
                    dve.wait_ge(factor, t * 2 + 2)
                    dve.wait_ge(pv_group, (t + 1) * NG)
                    dve.wait_ge(x_ready, t + 1)
                    dve.scalar_tensor_tensor(XO[:, slot, :], bank[6 + slot][:, D:2 * D], SM[:, slot, 5:6],
                                             XO[:, slot, :], ALU.mult, ALU.add).then_inc(out_part, 1)
                    dve.wait_ge(out_part, t + 1)
                    dve.scalar_tensor_tensor(XO[:, slot, :], bank[6 + slot][:, 0:D], SM[:, slot, 5:6],
                                             XO[:, slot, :], ALU.mult, ALU.add).then_inc(out_ready, 1)

                dve.wait_ge(bias_in, 16)
                score(0, 0, True)
                tiles(dve, T, step)

            @block.tensor
            def _(pe):
                def scores(t, slot, first):
                    pe.wait_ge(h_ready, t + 1)
                    for c, (c0, cn) in enumerate(CHUNKS):
                        if c >= 4:
                            pe.wait_ge(masked, t * NC + c - 3)
                        elif not first or slot:
                            pe.wait_ge(masked, t * NC - NC + 1 + max(x for x in range(NC) if x % 4 == c))
                        parts = [(0, 0), (0, 1), (1, 0)]
                        for n, (hs, hm) in enumerate(parts):
                            for k in range(KD):
                                ins = pe.matmul(bank[c % 4][:, 0:cn], HS[:, slot, hs, k, :], HT[:, hm, k, c0:c0 + cn],
                                                start=n == 0 and k == 0, stop=n == 2 and k == KD - 1)
                        ins.then_inc(qk_done, 1)

                def flip(t, slot, g, first):
                    g0, gn = GROUPS[g]
                    if not (first and slot == 0 and g < 2):
                        pe.wait_ge(lo_ready, t * NG + g - 1)
                    for j in range(gn):
                        ins = pe.transpose(bank[4 + half(slot, g)][:, j * P:(j + 1) * P],
                                           SC[:, slot, (g0 + j) * P:(g0 + j + 1) * P], ID[:])
                    ins.then_inc(flipped, 1)

                def step(t, uses, slot, first, last):
                    if not last:
                        scores(t + 1, 1 - slot, first and slot == 0)
                    pe.wait_ge(exp_done, t + 1)
                    flip(t, slot, 0, first)
                    if not first:
                        pe.wait_ge(out_ready, t - 1)
                    for g, (g0, gn) in enumerate(GROUPS):
                        if g + 1 < NG:
                            flip(t, slot, g + 1, first)
                        pe.wait_ge(lo_ready, t * NG + g + 1)
                        for j in range(gn):
                            jt = g0 + j
                            part = PT[:, half(slot, g), :, j * P:(j + 1) * P]
                            if jt < T - 1:
                                pe.matmul(bank[6 + slot][:, :], part[:, 0, :], SUP[:, jt, :, :].rearrange("p a d -> p (a d)"),
                                          start=jt == 0, stop=False)
                            ins = pe.matmul(bank[6 + slot][:, 0:D], part[:, 1, :], SUP[:, jt, 0, :],
                                            start=False, stop=False)
                            if jt == T - 1:
                                ins = pe.matmul(bank[6 + slot][:, :], part[:, 0, :], SUP[:, jt, :, :].rearrange("p a d -> p (a d)"),
                                                start=False, stop=True)
                        ins.then_inc(pv_group, 1)
                pe.wait_ge(consts, 2)
                scores(0, 0, True)
                tiles(pe, T, step)


def combine(nc, a, bank, X, gates, x_out, parts):
    with ExitStack() as ctx:
        s = Stage(nc, ctx, "comb1" if parts is not None else "comb2")
        Y = s.sb("y", [P, 2, T, D])
        mid = T // 2
        spans = [(0, mid // 2), (mid // 2, mid), (mid, T)]
        y_loaded = [[s.sem(f"y{k}_loaded{i}") for i in range(len(spans))] for k in range(2)]
        first_added, added = s.sem("first_added"), s.sem("added")
        x_stored = s.sem("x_stored")
        chain = s.sem("dve_chain")
        var_ready, std_ready = s.sem("variance_ready"), s.sem("std_ready")
        normed, hi_ready = s.sem("normed"), s.sem("hi_ready")
        if parts is not None:
            ST = s.sb("stats", [P, T, 6])
            MV = s.sb("mean_var", [P, 4, T])

        def by_tile(dram):
            return dram.rearrange("(t p) d -> p t d", p=P)

        with nc.Block() as block:
            @block.sync
            def _(sp):
                for n, (lo, hi) in enumerate(spans):
                    for k in range(2):
                        sp.dma_start(Y[:, k, lo:hi, :], by_tile(a["y"][k * NP:(k + 1) * NP, :])[:, lo:hi, :]).then_inc(y_loaded[k][n], 16)
                if parts is not None:
                    for n, (lo, hi) in enumerate(spans):
                        sp.wait_ge(added, hi)
                        sp.dma_start(by_tile(x_out)[:, lo:hi, :], X[:, lo:hi, :]).then_inc(x_stored, 16)
                    sp.wait_ge(x_stored, len(spans) * 16)
                else:
                    base = (T - 1) * P
                    for lo, hi in ((0, mid), (mid, T - 1)):
                        sp.wait_ge(added, hi)
                        sp.dma_start(x_out[lo * P:hi * P, :].rearrange("(t p) d -> p t d", p=P), X[:, lo:hi, :]).then_inc(x_stored, 16)
                    sp.wait_ge(added, T)
                    sp.dma_start(x_out[base:base + TAIL_A, :], X[0:TAIL_A, T - 1, :]).then_inc(x_stored, 16)
                    sp.dma_start(x_out[base + TAIL_A:N, :], X[TAIL_A:TAIL, T - 1, :]).then_inc(x_stored, 16)
                    sp.wait_ge(x_stored, 64)

            @block.vector
            def _(dve):
                for n, (lo, hi) in enumerate(spans):
                    for k, sem in enumerate((first_added, added)):
                        dve.wait_ge(y_loaded[k][n], 16)
                        if k == 1:
                            dve.wait_ge(first_added, hi)
                        with dve.Fori(lo, hi) as t:
                            dve.scalar_tensor_tensor(X[:, t, :], Y[:, k, t, :], gates[:, k, bass.ds(t, 1)], X[:, t, :],
                                                     ALU.mult, ALU.add).then_inc(sem, 1)
                if parts is None:
                    return
                link = Chain(dve, chain)
                row_statistics(dve, link, X, ST, MV, [(added, mid), (added, T), (added, T)], var_ready, std_ready)
                with dve.Fori(0, T) as t:
                    dve.tensor_scalar(Y[:, 0, t, :], X[:, t, :], MV[:, 0, bass.ds(t, 1)], MV[:, 1, bass.ds(t, 1)],
                                      ALU.subtract, ALU.mult).then_inc(normed, 1)
                with dve.Fori(0, T) as t:
                    dve.wait_ge(hi_ready, t + 1)
                    dve.tensor_tensor(parts[:, t, 1, :], Y[:, 0, t, :], parts[:, t, 0, :], ALU.subtract)

            @block.scalar
            def _(act):
                if parts is None:
                    return
                square_root(act, MV, var_ready, std_ready)
                with act.Fori(0, T) as t:
                    act.wait_ge(normed, t + 1)
                    act.copy(parts[:, t, 0, :], Y[:, 0, t, :]).then_inc(hi_ready, 1)


def route(nc, a, bank, name, x_in, gate_w, gate_b, r, w, X):
    with ExitStack() as ctx:
        s = Stage(nc, ctx, name)
        ST = s.sb("stats", [P, T, 6])
        MV = s.sb("mean_var", [P, 4, T])
        XS = s.sb("normed", [P, 2, D])
        XT = s.sb("normed_t", [P, 2, KD, P])
        GW = s.sb("gate_w", [P, KD, E])
        GB = s.sb("gate_b", [P, E])
        ID = s.sb("identity", [P, P])
        ONES = s.sb("ones", [P, P])
        BEFORE = s.sb("before", [P, P])
        VAL = s.sb("valid", [P, T])
        IE, IK, IQ = s.sb("iota_expert", [P, E]), s.sb("iota_tile", [P, T]), s.sb("iota_place", [P, P])
        IS, ROW = s.sb("iota_slot_tile", [P, S]), s.sb("empty_row", [P, S])
        PAIR = s.sb("pair", [P, 2, T])
        LG = s.sb("logits", [P, T, E])
        W3D = [s.sb(f"work{i}", [P, T, E]) for i in range(3)]
        OH = [s.sb(f"one_hot{i}", [P, T, E]) for i in range(2)]
        TOP = s.sb("top", [P, 4, T])
        SCAN = [s.sb(f"scan{i}", [P, E, T]) for i in range(3)]
        EX = [s.sb(f"per_expert{i}", [P, E]) for i in range(4)]
        SL, SI, QI = s.sb("slot", [P, 2, T]), s.sb("slot_int", [P, 2, T], I32), s.sb("place_int", [P, 2, T], I32)
        SF, QF = s.sb("slot_tile", [P, 2, T]), s.sb("slot_place", [P, 2, T])
        OQ, OS = s.sb("hot_place", [P, 2, 2, P]), s.sb("hot_tile", [P, 2, 2, S])
        EC = s.sb("expert_cmp", [P, S, E])
        V = [s.sb(f"value{i}", [P, S]) for i in range(3)]
        halves = [s.sem("x_first_half"), s.sem("x_second_half")]
        gate_in = s.sem("gate_loaded")
        consts, c0 = s.sem("constants_ready"), s.sem("constants_begun")
        chain = s.sem("dve_chain")
        var_ready, std_ready = s.sem("variance_ready"), s.sem("std_ready")
        normed, transposed, xt_ready = s.sem("normed"), s.sem("transposed"), s.sem("xt_ready")
        gated, logit_ready = s.sem("gated"), s.sem("logit_ready")
        kept, xn_stored = s.sem("normed_kept"), s.sem("normed_stored")
        diff_ready, exp_ready = s.sem("difference_ready"), s.sem("gate_exp_ready")
        used_ready, counted = s.sem("pairs_ready"), s.sem("pairs_counted")
        hot_ready, hot_used = s.sem("one_hots_ready"), s.sem("one_hots_used")
        mid = T // 2
        NCONST = 10
        with nc.Block() as block:
            @block.sync
            def _(sp):
                view = x_in.rearrange("(t p) d -> p t d", p=P)
                sp.dma_start(X[:, 0:mid, :], view[:, 0:mid, :]).then_inc(halves[0], 16)
                sp.dma_start(X[:, mid:T, :], view[:, mid:T, :]).then_inc(halves[1], 16)
                sp.dma_start(GW[:], gate_w).then_inc(gate_in, 16)
                if gate_b is not None:
                    sp.dma_start(GB[:], gate_b.partition_broadcast(P)).then_inc(gate_in, 16)
                w.load(sp)
                out = a["xn"].rearrange("(t p) d -> p t d", p=P)
                for lo, hi in ((0, mid), (mid, T)):
                    sp.wait_ge(kept, hi)
                    sp.dma_start(out[:, lo:hi, :], X[:, lo:hi, :]).then_inc(xn_stored, 16)
                sp.wait_ge(xn_stored, 32)

            @block.gpsimd
            def _(pool):
                pool.memset(ID[:], 0.0).then_inc(c0, 1)
                pool.memset(BEFORE[:], 1.0).then_inc(c0, 1)
                pool.memset(VAL[:], 1.0).then_inc(c0, 1)
                if gate_b is None:
                    pool.memset(GB[:], 0.0).then_inc(consts, 1)
                else:
                    pool.memset(ST[:, 0, :], 0.0).then_inc(consts, 1)
                pool.wait_ge(c0, 3)
                pool.affine_select(out=ID[:], in_=ID[:], compare_op=ALU.not_equal, fill=1.0, base=0,
                                   pattern=[[-1, P]], channel_multiplier=1).then_inc(consts, 1)
                pool.affine_select(out=BEFORE[:], in_=BEFORE[:], compare_op=ALU.is_gt, fill=0.0, base=0,
                                   pattern=[[1, P]], channel_multiplier=-1).then_inc(consts, 1)
                pool.affine_select(out=VAL[:], in_=VAL[:], compare_op=ALU.is_gt, fill=0.0, base=N,
                                   pattern=[[-P, T]], channel_multiplier=-1).then_inc(consts, 1)
                small = dict(allow_small_or_imprecise_dtypes=True)
                pool.iota(IE[:], [[1, E]], base=0, channel_multiplier=0, **small).then_inc(consts, 1)
                pool.iota(IK[:], [[P, T]], base=0, channel_multiplier=0, **small).then_inc(consts, 1)
                pool.iota(IQ[:], [[1, P]], base=0, channel_multiplier=0, **small).then_inc(consts, 1)
                pool.iota(IS[:], [[1, S]], base=0, channel_multiplier=0, **small).then_inc(consts, 1)
                pool.iota(ROW[:], [[P, S]], base=PAIR_ROWS + 1, channel_multiplier=1, **small).then_inc(consts, 1)
                pool.iota(PAIR[:], [[NP, 2], [P, T]], base=1, channel_multiplier=1, **small).then_inc(consts, 1)

                def keep(t, uses, slot, first, last):
                    pool.wait_ge(normed, t + 1)
                    pool.tensor_copy(X[:, t, :], XS[:, slot, :]).then_inc(kept, 1)
                tiles(pool, T, keep)

            @block.tensor
            def _(pe):
                def flip(t, slot, first):
                    pe.wait_ge(normed, t + 1)
                    if not first:
                        pe.wait_ge(xt_ready, t - 1)
                    for k in range(KD):
                        last = pe.transpose(bank[slot][:, k * P:(k + 1) * P], XS[:, slot, k * P:(k + 1) * P], ID[:])
                    last.then_inc(transposed, 1)

                def step(t, uses, slot, first, last):
                    if not last:
                        flip(t + 1, 1 - slot, first and slot == 0)
                    pe.wait_ge(xt_ready, t + 1)
                    if not first:
                        pe.wait_ge(logit_ready, t - 1)
                    for k in range(KD):
                        ins = pe.matmul(bank[2 + slot][:, 0:E], XT[:, slot, k, :], GW[:, k, :], start=k == 0, stop=k == KD - 1)
                    ins.then_inc(gated, 1)

                pe.wait_ge(consts, NCONST)
                flip(0, 0, True)
                pe.wait_ge(gate_in, 16 if gate_b is None else 32)
                tiles(pe, T, step)
                pe.wait_ge(used_ready, 1)
                used = W3D[0][:].rearrange("p t e -> p (t e)")
                pe.matmul(bank[6][:, 0:T * E], BEFORE[:], used, start=True, stop=True)
                pe.matmul(bank[7][:, 0:T * E], ONES[:], used, start=True, stop=True).then_inc(counted, 1)

                def invert(t, uses, slot, first, last):
                    pe.wait_ge(hot_ready, t + 1)
                    for k in range(2):
                        ins = pe.matmul(bank[0][:, 0:S], OQ[:, slot, k, :], OS[:, slot, k, :],
                                        start=first and slot == 0 and k == 0, stop=last and k == 1)
                    ins.then_inc(hot_used, 1)
                tiles(pe, T, invert)

            @block.scalar
            def _(act):
                square_root(act, MV, var_ready, std_ready)

                def copy_t(t, uses, slot, first, last):
                    act.wait_ge(transposed, t + 1)
                    if not first:
                        act.wait_ge(gated, t - 1)
                    act.copy(XT[:, slot, :, :], bank[slot][:, 0:D].rearrange("p (k n) -> p k n", k=KD)).then_inc(xt_ready, 1)
                tiles(act, T, copy_t)
                act.wait_ge(diff_ready, 1)
                act.activation(TOP[:, 3, :], TOP[:, 2, :], ACT.Exp).then_inc(exp_ready, 1)

            @block.vector
            def _(dve):
                link = Chain(dve, chain)
                link(dve.memset(ONES[:], 1.0))
                dve.wait_ge(consts, NCONST)
                row_statistics(dve, link, X, ST, MV, [(halves[0], 16), (halves[1], 16), (halves[1], 16)],
                               var_ready, std_ready)
                dve.wait_ge(gate_in, 16 if gate_b is None else 32)

                def norm(t, slot, first):
                    if not first:
                        dve.wait_ge(transposed, t - 1)
                        dve.wait_ge(kept, t - 1)
                    dve.tensor_scalar(XS[:, slot, :], X[:, t, :], MV[:, 0, bass.ds(t, 1)], MV[:, 1, bass.ds(t, 1)],
                                      ALU.subtract, ALU.mult).then_inc(normed, 1)

                def step(t, uses, slot, first, last):
                    if not known(t) or t + 2 < T:
                        norm(t + 2, slot, False)
                    dve.wait_ge(gated, t + 1)
                    dve.tensor_tensor(LG[:, t, :], bank[2 + slot][:, 0:E], GB[:], ALU.add).then_inc(logit_ready, 1)
                norm(0, 0, True)
                norm(1, 1, True)
                tiles(dve, T, step)
                dve.wait_ge(logit_ready, T)

                def per_tile(v):
                    return v.unsqueeze(2).to_broadcast([P, T, E])

                def per_expert(v):
                    return v.unsqueeze(1).to_broadcast([P, T, E])

                A, B, C = (w[:] for w in W3D)
                m = [TOP[:, 0, :], TOP[:, 1, :]]
                rest = LG[:]
                for k in range(2):
                    link(dve.reduce_max(m[k], rest, AX))
                    link(dve.tensor_tensor(A, rest, per_tile(m[k]), ALU.is_equal))
                    link(dve.scalar_tensor_tensor(B, A, -float(E), per_expert(IE[:]), ALU.mult, ALU.add))
                    link(dve.tensor_reduce(out=TOP[:, 2, :], in_=B, axis=AX, op=ALU.min))
                    link(dve.tensor_tensor(OH[k][:], B, per_tile(TOP[:, 2, :]), ALU.is_equal))
                    if k == 0:
                        link(dve.scalar_tensor_tensor(C, OH[0][:], -3.0e38, rest, ALU.mult, ALU.add))
                        rest = C
                dve.tensor_tensor(TOP[:, 2, :], m[1], m[0], ALU.subtract).then_inc(diff_ready, 1)
                link(dve.tensor_tensor(B, OH[0][:], OH[1][:], ALU.add))
                dve.tensor_tensor(A, B, per_tile(VAL[:]), ALU.mult).then_inc(used_ready, 1)
                dve.wait_ge(exp_ready, 1)
                link(dve.tensor_scalar(TOP[:, 2, :], TOP[:, 3, :], 1.0, None, ALU.add))
                link(dve.reciprocal(r["gates"][:, 0, :], TOP[:, 2, :]))
                link(dve.tensor_tensor(r["gates"][:, 1, :], r["gates"][:, 0, :], TOP[:, 3, :], ALU.mult))
                dve.wait_ge(counted, 1)
                tot, ping, pong = (v[:] for v in SCAN)
                link(dve.tensor_copy(tot, bank[7][:, 0:T * E].rearrange("p (t e) -> p e t", e=E)))
                src, dst, other = tot, ping, pong
                shift = 1
                while shift < T:
                    dve.tensor_copy(dst[:, :, 0:shift], src[:, :, 0:shift]).then_inc(chain, 1)
                    link.n += 1
                    link(dve.tensor_tensor(dst[:, :, shift:T], src[:, :, shift:T], src[:, :, 0:T - shift], ALU.add))
                    src, dst, other = dst, other, dst
                    shift *= 2
                count, held, ends, more = (v[:] for v in EX)
                link(dve.tensor_copy(count.unsqueeze(2), src[:, :, T - 1:T]))
                link(dve.tensor_tensor(dst, count.unsqueeze(2).to_broadcast([P, E, T]),
                                       IK[:].unsqueeze(1).to_broadcast([P, E, T]), ALU.is_gt))
                link(dve.reduce_sum(held, dst, AX))
                e_src, e_dst, e_other = held, ends, more
                shift = 1
                while shift < E:
                    dve.tensor_copy(e_dst[:, 0:shift], e_src[:, 0:shift]).then_inc(chain, 1)
                    link.n += 1
                    link(dve.tensor_tensor(e_dst[:, shift:E], e_src[:, shift:E], e_src[:, 0:E - shift], ALU.add))
                    e_src, e_dst, e_other = e_dst, e_other, e_dst
                    shift *= 2
                ends = e_src
                link(dve.tensor_tensor(EC[:], ends.unsqueeze(1).to_broadcast([P, S, E]),
                                       IS[:].unsqueeze(2).to_broadcast([P, S, E]), ALU.is_le))
                link(dve.reduce_sum(V[0][:], EC[:], AX))
                link(dve.tensor_scalar(V[1][:], V[0][:], E - 1.0, None, ALU.min))
                link(dve.tensor_copy(r["expert"][:], V[1][:]))
                link(dve.tensor_tensor(count, ends, held, ALU.subtract))
                link(dve.tensor_scalar(count, count, float(P), None, ALU.mult))
                link(dve.tensor_tensor(A, src.rearrange("p e t -> p t e"), tot.rearrange("p e t -> p t e"), ALU.subtract))
                link(dve.tensor_tensor(B, A, bank[6][:, 0:T * E].rearrange("p (t e) -> p t e", e=E), ALU.add))
                link(dve.tensor_tensor(A, B, per_expert(count), ALU.add))
                link(dve.tensor_scalar(TOP[:, 0, :], VAL[:], -float(S * P), float(S * P), ALU.mult, ALU.add))
                for k in range(2):
                    link(dve.tensor_tensor(B, A, OH[k][:], ALU.mult))
                    link(dve.reduce_sum(TOP[:, 1, :], B, AX))
                    link(dve.tensor_tensor(TOP[:, 2, :], TOP[:, 1, :], VAL[:], ALU.mult))
                    link(dve.tensor_tensor(SL[:, k, :], TOP[:, 2, :], TOP[:, 0, :], ALU.add))
                link(dve.tensor_copy(SI[:], SL[:]))
                link(dve.tensor_scalar(QI[:], SI[:], P - 1, None, ALU.bitwise_and))
                link(dve.tensor_copy(QF[:], QI[:]))
                link(dve.tensor_scalar(QI[:], SI[:], P.bit_length() - 1, None, ALU.arith_shift_right))
                link(dve.tensor_copy(SF[:], QI[:]))

                def hot(t, uses, slot, first, last):
                    if not first:
                        dve.wait_ge(hot_used, t - 1)
                    for k in range(2):
                        dve.tensor_scalar(OQ[:, slot, k, :], IQ[:], QF[:, k, bass.ds(t, 1)], None, ALU.is_equal)
                        ins = dve.tensor_scalar(OS[:, slot, k, :], IS[:], SF[:, k, bass.ds(t, 1)], PAIR[:, k, bass.ds(t, 1)],
                                                ALU.is_equal, ALU.mult)
                    ins.then_inc(hot_ready, 1)
                tiles(dve, T, hot)
                dve.wait_ge(hot_used, T)
                v0, v1, v2 = (v[:] for v in V)
                link(dve.tensor_copy(v0, bank[0][:, 0:S]))
                link(dve.tensor_scalar(v1, v0, 0.0, None, ALU.is_equal))
                link(dve.tensor_tensor(v2, v1, ROW[:], ALU.mult))
                link(dve.scalar_tensor_tensor(v1, v0, -1.0, v2, ALU.add, ALU.add))
                link(dve.tensor_copy(r["dst"][:], v1))
                link(dve.tensor_scalar(v1, v0, NP + 0.5, -float(NP), ALU.is_gt, ALU.mult))
                link(dve.scalar_tensor_tensor(v2, v0, -1.0, v1, ALU.add, ALU.add))
                link(dve.tensor_scalar(v1, v2, 0.0, None, ALU.max))
                link(dve.tensor_copy(r["tok"][:], v1))


class Weights:

    def __init__(self, nc, keep, name, w_in, w_out, b_in=None, b_out=None):
        s = Stage(nc, keep, name)
        self.w_in, self.w_out, self.b_in, self.b_out = w_in, w_out, b_in, b_out
        self.WI, self.WO = s.sb("w_in", [P, KD, w_in.shape[2]]), s.sb("w_out", list(w_out.shape))
        self.in_loaded, self.out_loaded = s.sem("w_in_loaded"), s.sem("w_out_loaded")
        if b_in is not None:
            self.BI, self.BO = s.sb("b_in", list(b_in.shape)), s.sb("b_out", [P, E * D])
            self.b_loaded = s.sem("b_loaded")

    def load(self, sp):
        for k in range(KD):
            sp.dma_start(self.WI[:, k, :], self.w_in[:, k, :]).then_inc(self.in_loaded, 16)
        sp.dma_start(self.WO[:], self.w_out).then_inc(self.out_loaded, 16)
        if self.b_in is not None:
            sp.dma_start(self.BI[:], self.b_in).then_inc(self.b_loaded, 16)
            sp.dma_start(self.BO[:], self.b_out.partition_broadcast(P)).then_inc(self.b_loaded, 16)


def experts(nc, a, bank, name, w, H, r, x_in, XR):
    gated = w.b_in is None
    KH = H // P
    HB = H // CH
    WIN = 2 * H if gated else H
    assert WIN == 2 * CH
    WI, WO = w.WI, w.WO
    with ExitStack() as ctx:
        s = Stage(nc, ctx, name)
        ID = s.sb("identity", [P, P])
        XG = s.sb("x_gathered", [P, 2, D])
        TAKER = s.sb("wait_taker", [P, 2, 2])
        ZERO = s.sb("zero", [NP - N, D])
        XT = s.sb("x_t", [P, 2, KD, P])
        GATE = s.sb("silu", [P, CH])
        HH = s.sb("hidden", [P, 2, H])
        HTT = s.sb("hidden_t", [P, 2, KH, P])
        YS = s.sb("y", [P, 2, D])
        TOKS, DSTS = s.sb("tok", [P, 2], I32), s.sb("dst", [P, 2], I32)
        zeroed, pad_stored = s.sem("zeroed"), s.sem("pad_stored")
        consts, x_back = s.sem("identity_ready"), s.sem("x_back")
        tok_ready, dst_ready = s.sem("tok_ready"), s.sem("dst_ready")
        gathered = [s.sem(f"gathered{i}") for i in range(2)]
        scattered = [s.sem(f"scattered{i}") for i in range(2)]
        x_flipped, xt_ready = s.sem("x_transposed"), s.sem("xt_ready")
        first_done, silu_ready, h_ready = s.sem("first_product"), s.sem("silu_ready"), s.sem("hidden_ready")
        h_flipped, ht_ready = s.sem("hidden_transposed"), s.sem("hidden_t_ready")
        second_done, y_ready = s.sem("second_product"), s.sem("y_ready")
        h_bank = [bank[1], bank[6]]

        def ahead(t, uses, slot, n):
            if known(t) and not 0 <= t + n < S:
                return None
            return t + n, uses + (slot + n) // 2, (slot + n) % 2

        def reused(t):
            return not known(t) or t >= 2

        def expert_of(eng, t):
            return eng.value_load(r["expert"][0:1, bass.ds(t, 1)], min_val=0, max_val=E - 1)

        with nc.Block() as block:
            @block.sync
            def _(sp):
                sp.wait_ge(zeroed, 1)
                for k in range(2):
                    sp.dma_start(a["y"][k * NP + N:k * NP + NP, :], ZERO[:]).then_inc(pad_stored, 16)
                sp.dma_start(XR[:], x_in.rearrange("(t p) d -> p t d", p=P)).then_inc(x_back, 16)
                sp.wait_ge(pad_stored, 32)
                sp.wait_ge(x_back, 16)

            @block.gpsimd
            def _(pool):
                pool.memset(ZERO[:], 0.0).then_inc(zeroed, 1)
                pool.memset(ID[:], 0.0).then_inc(consts, 1)
                pool.wait_ge(consts, 1)
                pool.affine_select(out=ID[:], in_=ID[:], compare_op=ALU.not_equal, fill=1.0, base=0,
                                   pattern=[[-1, P]], channel_multiplier=1).then_inc(consts, 1)

                def gather(t, uses, slot):
                    if reused(t):
                        pool.wait_ge(x_flipped, t - 1)
                    pool.tensor_copy(TOKS[:, slot:slot + 1], r["tok"][:, bass.ds(t, 1)]).then_inc(tok_ready, 1)
                    pool.wait_ge(tok_ready, t + 1)
                    pool.tensor_tensor(TAKER[:, 0, slot:slot + 1], ID[:, 0:1], ID[:, 0:1], ALU.add)
                    pool.indirect_dma_start(out=XG[:, slot, :], out_offset=None, in_=a["xn"],
                                            in_offset=bass.IndirectOffsetOnAxis(ap=TOKS[:, slot:slot + 1], axis=0)
                                            ).then_inc(gathered[slot], 16)

                def scatter(t, uses, slot):
                    if reused(t):
                        pool.wait_ge(scattered[slot], uses * 16)
                    pool.tensor_copy(DSTS[:, slot:slot + 1], r["dst"][:, bass.ds(t, 1)]).then_inc(dst_ready, 1)
                    pool.wait_ge(dst_ready, t + 1)
                    pool.wait_ge(y_ready, t + 1)
                    pool.tensor_tensor(TAKER[:, 1, slot:slot + 1], ID[:, 0:1], ID[:, 0:1], ALU.add)
                    pool.indirect_dma_start(out=a["y"], out_offset=bass.IndirectOffsetOnAxis(ap=DSTS[:, slot:slot + 1], axis=0),
                                            in_=YS[:, slot, :], in_offset=None).then_inc(scattered[slot], 16)

                def step(t, uses, slot, first, last):
                    if nxt := ahead(t, uses, slot, 2):
                        gather(*nxt)
                    if before := ahead(t, uses, slot, -1):
                        scatter(*before)
                    if last:
                        scatter(t, uses, slot)
                pool.wait_ge(consts, 2)
                gather(0, 0, 0)
                gather(1, 0, 1)
                tiles(pool, S, step)
                pool.wait_ge(scattered[0], (S + 1) // 2 * 16)
                pool.wait_ge(scattered[1], S // 2 * 16)

            @block.tensor
            def _(pe):
                def flip_x(t, uses, slot):
                    pe.wait_ge(gathered[slot], (uses + 1) * 16)
                    if not known(t) or t >= 1:
                        pe.wait_ge(xt_ready, t)
                    for k in range(KD):
                        ins = pe.transpose(bank[0][:, k * P:(k + 1) * P], XG[:, slot, k * P:(k + 1) * P], ID[:])
                    ins.then_inc(x_flipped, 1)

                def first_layer(t, uses, slot):
                    e = expert_of(pe, t)
                    pe.wait_ge(xt_ready, t + 1)
                    if reused(t):
                        pe.wait_ge(h_ready, t - 1)
                    for b in range(2):
                        for k in range(KD):
                            ins = pe.matmul(bank[2 + 2 * slot + b][:, :], XT[:, slot, k, :],
                                            WI[:, k, bass.ds(e * WIN + b * CH, CH)], start=k == 0, stop=k == KD - 1)
                    ins.then_inc(first_done, 1)

                def flip_hidden(t, uses, slot):
                    pe.wait_ge(h_ready, t + 1)
                    for j in range(HB):
                        if not known(t) or t * HB + j >= 2:
                            pe.wait_ge(ht_ready, t * HB + j - 1)
                        for k in range(4):
                            ins = pe.transpose(h_bank[slot if HB == 1 else j][:, k * P:(k + 1) * P],
                                               HH[:, slot, (4 * j + k) * P:(4 * j + k + 1) * P], ID[:])
                        ins.then_inc(h_flipped, 1)

                def second_layer(t, uses, slot):
                    e = expert_of(pe, t)
                    pe.wait_ge(ht_ready, (t + 1) * HB)
                    if not known(t) or t >= 1:
                        pe.wait_ge(y_ready, t)
                    for k in range(KH):
                        ins = pe.matmul(bank[7][:, 0:D], HTT[:, slot, k, :], WO[:, k, bass.ds(e * D, D)],
                                        start=k == 0, stop=k == KH - 1)
                    ins.then_inc(second_done, 1)

                def step(t, uses, slot, first, last):
                    flip_hidden(t, uses, slot)
                    if nxt := ahead(t, uses, slot, 1):
                        first_layer(*nxt)
                    if nxt := ahead(t, uses, slot, 2):
                        flip_x(*nxt)
                    second_layer(t, uses, slot)

                pe.wait_ge(consts, 2)
                flip_x(0, 0, 0)
                flip_x(1, 0, 1)
                pe.wait_ge(w.in_loaded, KD * 16)
                first_layer(0, 0, 0)
                pe.wait_ge(w.out_loaded, 16)
                tiles(pe, S, step)

            @block.scalar
            def _(act):
                def copy_x(t, uses, slot):
                    act.wait_ge(x_flipped, t + 1)
                    if reused(t):
                        act.wait_ge(first_done, t - 1)
                    act.copy(XT[:, slot, :, :], bank[0][:, 0:D].rearrange("p (k n) -> p k n", k=KD)).then_inc(xt_ready, 1)

                def silu(t, uses, slot):
                    act.wait_ge(first_done, t + 1)
                    if not known(t) or t >= 1:
                        act.wait_ge(h_ready, t)
                    act.activation(GATE[:], bank[2 + 2 * slot][:, :], ACT.Silu).then_inc(silu_ready, 1)

                def hidden_out(t, uses, slot):
                    e = None if gated else expert_of(act, t)
                    for j in range(HB):
                        src = h_bank[slot if HB == 1 else j]
                        act.wait_ge(h_flipped, t * HB + j + 1)
                        if reused(t):
                            act.wait_ge(second_done, t - 1)
                        if gated:
                            ins = act.copy(HTT[:, slot, 4 * j:4 * j + 4, :], src[:, :].rearrange("p (k n) -> p k n", n=P))
                        else:
                            for k in range(4):
                                ins = act.activation(HTT[:, slot, 4 * j + k, :], src[:, k * P:(k + 1) * P], ACT.Gelu,
                                                     bias=w.BI[:, bass.ds(e * KH + (4 * j + k), 1)])
                        ins.then_inc(ht_ready, 1)

                def step(t, uses, slot, first, last):
                    hidden_out(t, uses, slot)
                    nxt = ahead(t, uses, slot, 1)
                    if gated and nxt:
                        silu(*nxt)
                    if nxt := ahead(t, uses, slot, 2):
                        copy_x(*nxt)
                copy_x(0, 0, 0)
                copy_x(1, 0, 1)
                if gated:
                    silu(0, 0, 0)
                else:
                    act.wait_ge(w.b_loaded, 32)
                tiles(act, S, step)

            @block.vector
            def _(dve):
                def hidden(t, uses, slot):
                    dve.wait_ge(silu_ready if gated else first_done, t + 1)
                    if reused(t):
                        dve.wait_ge(h_flipped, (t - 1) * HB)
                    if gated:
                        ins = dve.tensor_tensor(HH[:, slot, :], GATE[:], bank[3 + 2 * slot][:, :], ALU.mult)
                    else:
                        for b in range(2):
                            ins = dve.tensor_copy(HH[:, slot, b * CH:(b + 1) * CH], bank[2 + 2 * slot + b][:, :])
                    ins.then_inc(h_ready, 1)

                def result(t, uses, slot):
                    e = None if gated else expert_of(dve, t)
                    dve.wait_ge(second_done, t + 1)
                    if reused(t):
                        dve.wait_ge(scattered[slot], uses * 16)
                    if gated:
                        dve.tensor_copy(YS[:, slot, :], bank[7][:, 0:D]).then_inc(y_ready, 1)
                    else:
                        dve.tensor_tensor(YS[:, slot, :], bank[7][:, 0:D], w.BO[:, bass.ds(e * D, D)], ALU.add).then_inc(y_ready, 1)

                def step(t, uses, slot, first, last):
                    if nxt := ahead(t, uses, slot, 1):
                        hidden(*nxt)
                    result(t, uses, slot)
                if not gated:
                    dve.wait_ge(w.b_loaded, 32)
                hidden(0, 0, 0)
                tiles(dve, S, step)


def neighbours(nc, a, bank, XH):
    GS = [(g, min(8, T - g)) for g in range(0, T, 8)]
    G = len(GS)
    assert G % 2 == 0
    with ExitStack() as ctx:
        s = Stage(nc, ctx, "nbr")
        NEG = s.sb("mask", [P, 2, NP], BF16)
        ID, IDF = s.sb("identity", [P, P], BF16), s.sb("identity_f32", [P, P])
        AT = s.sb("adj_t", [P, 2, 8 * P], F16)
        WT = s.sb("w_t", [P, KD, D])
        BB = s.sb("bias", [P, D])
        XB, XO = s.sb("x", [P, 2, D]), s.sb("x_out", [P, 2, D])
        AGH, AG = s.sb("sum_hi", [P, 2, D]), s.sb("sum", [P, 2, D])
        AGT = s.sb("sum_t", [P, 2, KD, P])
        PRE = s.sb("before_relu", [P, 2, D])
        consts, w_loaded = s.sem("identity_ready"), s.sem("w_loaded")
        mask_in = [s.sem(f"mask_loaded{i}") for i in range(2)]
        x_loaded = [s.sem(f"x_loaded{i}") for i in range(2)]
        x_stored = [s.sem(f"x_stored{i}") for i in range(2)]
        flipped, at_ready, used = s.sem("mask_transposed"), s.sem("adj_t_ready"), s.sem("group_multiplied")
        at_odd = s.sem("adj_t_odd_ready")
        hi_ready, ag_ready, ag_flipped, agt_ready = s.sem("sum_hi_ready"), s.sem("sum_ready"), s.sem("sum_transposed"), s.sem("sum_t_ready")
        out_done, pre_ready, x_ready = s.sem("product_ready"), s.sem("pre_ready"), s.sem("x_ready")
        bf = [bank[i][:, :].bitcast(BF16) for i in range(2)]
        with nc.Block() as block:
            @block.sync
            def _(sp):
                sp.dma_start(WT[:], a["w_t"]).then_inc(w_loaded, 16)
                sp.dma_start(BB[:], a["b"].partition_broadcast(P)).then_inc(w_loaded, 16)

                def store(t, slot):
                    sp.wait_ge(x_ready, t + 1)
                    sp.dma_start(a["x3"][bass.ds(t * P, P), :], XO[:, slot, :]).then_inc(x_stored[slot], 16)

                def step(t, uses, slot, first, last):
                    if not first:
                        sp.wait_ge(flipped, (t - 1) * G)
                    sp.dma_start(NEG[:, slot, :], a["mask"][t, :, :]).then_inc(mask_in[slot], 16)
                    if not first:
                        store(t - 2, slot)
                    sp.dma_start(XB[:, slot, :], a["x2"][bass.ds(t * P, P), :]).then_inc(x_loaded[slot], 16)
                tiles(sp, T, step)
                store(T - 2, 0)
                store(T - 1, 1)
                for slot in range(2):
                    sp.wait_ge(x_stored[slot], T // 2 * 16)

            @block.gpsimd
            def _(pool):
                for n, i in enumerate((ID, IDF)):
                    pool.memset(i[:], 0.0).then_inc(consts, 1)
                    pool.wait_ge(consts, 2 * n + 1)
                    pool.affine_select(out=i[:], in_=i[:], compare_op=ALU.not_equal, fill=1.0, base=0,
                                       pattern=[[-1, P]], channel_multiplier=1).then_inc(consts, 1)

            @block.tensor
            def _(pe):
                def flip(t, uses, slot, g, first):
                    g0, gn = GS[g]
                    if g == 0:
                        pe.wait_ge(mask_in[slot], (uses + 1) * 16)
                    if not (first and slot == 0 and g < 2):
                        pe.wait_ge(at_ready if g % 2 == 0 else at_odd, t * (G // 2) + g // 2)
                    for j in range(gn):
                        ins = pe.transpose(bf[g % 2][:, j * P:(j + 1) * P], NEG[:, slot, (g0 + j) * P:(g0 + j + 1) * P], ID[:])
                    ins.then_inc(flipped, 1)

                def multiply(t, slot, g):
                    g0, gn = GS[g]
                    pe.wait_ge(at_ready if g % 2 == 0 else at_odd, t * (G // 2) + g // 2 + 1)
                    for j in range(gn):
                        ins = pe.matmul(bank[2 + slot][:, :], AT[:, g % 2, j * P:(j + 1) * P],
                                        XH[:, g0 + j, :, :].rearrange("p a d -> p (a d)"), start=g0 + j == 0, stop=g0 + j == T - 1)
                    ins.then_inc(used, 1)

                def finish(t, slot, first):
                    pe.wait_ge(ag_ready, t + 1)
                    if not first:
                        pe.wait_ge(x_ready, t - 1)
                    for k in range(KD):
                        ins = pe.transpose(bank[4 + slot][:, k * P:(k + 1) * P], AG[:, slot, k * P:(k + 1) * P], IDF[:])
                    ins.then_inc(ag_flipped, 1)

                def project_out(t, slot):
                    pe.wait_ge(agt_ready, t + 1)
                    for k in range(KD):
                        ins = pe.matmul(bank[6 + slot][:, 0:D], AGT[:, slot, k, :], WT[:, k, :], start=k == 0, stop=k == KD - 1)
                    ins.then_inc(out_done, 1)

                def step(t, uses, slot, first, last):
                    very_first = first and slot == 0
                    if not first:
                        pe.wait_ge(ag_ready, t - 1)
                    for g in range(G):
                        if g + 1 < G:
                            flip(t, uses, slot, g + 1, first)
                        elif not last:
                            flip(t + 1, uses + slot, 1 - slot, 0, first and slot == 0)
                        multiply(t, slot, g)
                        if g == 1 and not very_first:
                            finish(t - 1, 1 - slot, first)
                        if g == 2 and not very_first:
                            project_out(t - 1, 1 - slot)
                    if last:
                        finish(t, slot, False)
                        project_out(t, slot)
                pe.wait_ge(consts, 4)
                pe.wait_ge(w_loaded, 32)
                flip(0, 0, 0, 0, True)
                tiles(pe, T, step)

            @block.scalar
            def _(act):
                def even(t, slot, g, first):
                    act.wait_ge(flipped, t * G + g + 1)
                    if not (first and slot == 0 and g < 2):
                        act.wait_ge(used, t * G + g - 1)
                    w = GS[g][1] * P
                    act.activation(AT[:, 0, 0:w], bf[0][:, 0:w], ACT.Copy, bias=1.0, scale=1.0 / BIG).then_inc(at_ready, 1)

                def tail(t, slot, first):
                    act.wait_ge(used, (t + 1) * G)
                    if not first:
                        act.wait_ge(ag_ready, t - 1)
                    act.copy(AGH[:, slot, :], bank[2 + slot][:, 0:D]).then_inc(hi_ready, 1)

                def flip_out(t, slot, first):
                    act.wait_ge(ag_flipped, t + 1)
                    if not first:
                        act.wait_ge(out_done, t - 1)
                    act.copy(AGT[:, slot, :, :], bank[4 + slot][:, 0:D].rearrange("p (k n) -> p k n", k=KD)).then_inc(agt_ready, 1)

                def step(t, uses, slot, first, last):
                    for g in range(0, G, 2):
                        even(t, slot, g, first)
                        if g == 0 and not (first and slot == 0):
                            tail(t - 1, 1 - slot, first)
                    if not (first and slot == 0):
                        flip_out(t - 1, 1 - slot, first)
                    if last:
                        tail(t, slot, False)
                        flip_out(t, slot, False)
                tiles(act, T, step)

            @block.vector
            def _(dve):
                def odd(t, slot, g, first):
                    if not (first and slot == 0 and g < 2):
                        dve.wait_ge(used, t * G + g - 1)
                    dve.wait_ge(flipped, t * G + g + 1)
                    w = GS[g][1] * P
                    dve.tensor_scalar(AT[:, 1, 0:w], bf[1][:, 0:w], 1.0 / BIG, 1.0, ALU.mult, ALU.add).then_inc(at_odd, 1)

                def add(t, slot, first):
                    dve.wait_ge(hi_ready, t + 1)
                    if not first:
                        dve.wait_ge(ag_flipped, t - 1)
                    dve.tensor_tensor(AG[:, slot, :], bank[2 + slot][:, D:2 * D], AGH[:, slot, :], ALU.add).then_inc(ag_ready, 1)

                def finish(t, uses, slot, first):
                    dve.wait_ge(out_done, t + 1)
                    dve.tensor_tensor(PRE[:, slot, :], bank[6 + slot][:, 0:D], BB[:], ALU.add).then_inc(pre_ready, 1)
                    dve.wait_ge(x_loaded[slot], (uses + 1) * 16)
                    if not first:
                        dve.wait_ge(x_stored[slot], uses * 16)
                    dve.wait_ge(pre_ready, t + 1)
                    dve.scalar_tensor_tensor(XO[:, slot, :], PRE[:, slot, :], 0.0, XB[:, slot, :], ALU.max, ALU.add).then_inc(x_ready, 1)

                def step(t, uses, slot, first, last):
                    very_first = first and slot == 0
                    if not very_first:
                        add(t - 1, 1 - slot, first)
                    odd(t, slot, 1, first)
                    odd(t, slot, 3, first)
                    if not very_first:
                        finish(t - 1, uses - (1 - slot), 1 - slot, first)
                    if last:
                        add(t, slot, False)
                        finish(t, uses, slot, False)
                tiles(dve, T, step)


def build(nc, x, adj, weight, bias, node_w, edge_w, wg, bg, w13, w2, w_t, b, gate_t, w1_t, b1, w2_t, b2, out, stop=99):
    with ExitStack() as ctx:
        bank = [ctx.enter_context(nc.psum_tensor(f"bank{i}", [P, CH], F32)) for i in range(8)]

        def dram(name, shape, dt=F32):
            return nc.dram_tensor(name, shape, dt, kind="Internal").ap()

        def routing(name, keep):
            t = lambda what, shape, dt: keep.enter_context(nc.sbuf_tensor(f"{name}_{what}", shape, dt))
            return dict(gates=t("gates", [P, 2, T], F32), tok=t("tok", [P, S], I32), dst=t("dst", [P, S], I32),
                        expert=t("expert", [P, S], I32))

        a = dict(x=x, adj=adj, weight=weight, bias=bias, node_w=node_w, edge_w=edge_w, w_t=w_t, b=b)
        a["mask"] = dram("mask", [T, P, NP], BF16)
        for name in ("x1", "x2", "x3", "xn"):
            a[name] = dram(name, [NP, D])
        a["y"] = dram("y", [PAIR_ROWS + S * P, D])
        with ExitStack() as keep:
            a["HT"] = keep.enter_context(nc.sbuf_tensor("h_t", [P, 2, KD, NP], F32R))
            a["SUP"] = keep.enter_context(nc.sbuf_tensor("support", [P, T, 2, D], F32R))
            a["NATT"] = keep.enter_context(nc.sbuf_tensor("node_attention", [P, T], F32))
            project(nc, a, bank)
            attend(nc, a, bank)
        for layer, (x_in, gate, gate_b, weights, H) in enumerate((
                (a["x1"], wg, bg, (w13, w2), H0), (a["x3"], gate_t, None, (w1_t, w2_t, b1, b2), H1))):
            with ExitStack() as keep:
                r = routing(f"route{layer}", keep)
                X = keep.enter_context(nc.sbuf_tensor(f"x_kept{layer}", [P, T, D], F32))
                with ExitStack() as while_used:
                    w = Weights(nc, while_used, f"w{layer}", *weights)
                    route(nc, a, bank, f"gate{layer}", x_in, gate, gate_b, r, w, X)
                    experts(nc, a, bank, f"ffn{layer}", w, H, r, x_in, X)
                if layer == 0:
                    XH = keep.enter_context(nc.sbuf_tensor("normed_parts", [P, T, 2, D], F16))
                    combine(nc, a, bank, X, r["gates"], a["x2"], XH)
                    neighbours(nc, a, bank, XH)
                else:
                    combine(nc, a, bank, X, r["gates"], out, None)


def layout(i):
    import numpy as np

    def blocks(w):
        e, n, m = w.shape
        return np.ascontiguousarray(w.reshape(e, n // P, P, m).transpose(2, 1, 0, 3).reshape(P, n // P, e * m))

    w13 = np.concatenate([i["L0_ffn_W1"], i["L0_ffn_W3"]], axis=2)
    return dict(
        x=i["x"], adj=i["adj"], weight=i["L0_gnn_weight"], bias=i["L0_gnn_bias"], node_w=i["L0_gnn_node_w"],
        edge_w=i["L0_gnn_edge_w"], wg=blocks(i["L0_ffn_Wg"][None]), bg=i["L0_ffn_bg"], w13=blocks(w13),
        w2=blocks(i["L0_ffn_W2"]), w_t=blocks(i["L1_gnn_W"].T[None]), b=i["L1_gnn_b"],
        gate_t=blocks(i["L1_ffn_gate_w"].T[None]), w1_t=blocks(i["L1_ffn_w1"].transpose(0, 2, 1)),
        b1=i["L1_ffn_b1"].reshape(E * H1 // P, P).T, w2_t=blocks(i["L1_ffn_w2"].transpose(0, 2, 1)), b2=i["L1_ffn_b2"].reshape(-1))


def kernel(**inputs):
    import numpy as np
    import concourse.bacc as bacc
    from concourse.bass_utils import run_bass_kernel_spmd

    nc = bacc.Bacc("TRN2", target_bir_lowering=False, num_devices=1)
    arrays, args = {}, []
    for name, value in layout({k: np.asarray(v) for k, v in inputs.items()}).items():
        value = np.ascontiguousarray(value)
        arrays[f"in_{name}"] = value
        args.append(nc.dram_tensor(f"in_{name}", value.shape, mybir.dt.from_np(value.dtype), kind="ExternalInput").ap())
    out = nc.dram_tensor("out_0", (N, D), F32, kind="ExternalOutput").ap()
    build(nc, *args, out)
    r = run_bass_kernel_spmd(nc, [arrays], core_ids=[0])
    return r.results[0]["out_0"]
```

```python
import concourse.bass as bass
from concourse import mybir
from contextlib import ExitStack

F32 = mybir.dt.float32
F32R = mybir.dt.float32r
F16 = mybir.dt.float16
BF16 = mybir.dt.bfloat16
I32 = mybir.dt.int32
ALU = mybir.AluOpType
ACT = mybir.ActivationFunctionType
AX = mybir.AxisListType.X
RMAX = bass.bass_isa.ReduceOp.max
RADD = bass.bass_isa.ReduceOp.add

P = 128
N = 3327
T = (N + P - 1) // P
NP = T * P
TAIL = N - (T - 1) * P
TAIL_A = TAIL // 16 * 16
D = 256
KD = D // P
EPS = 1e-5
BIG = 2.0 ** 100
CH = 512
CHUNKS = [(c, min(CH, NP - c)) for c in range(0, NP, CH)]
NC = len(CHUNKS)
GROUPS = [(g, min(4, T - g)) for g in range(0, T, 4)]
NG = len(GROUPS)
GROUP = 2
NT = T // GROUP
assert NT * GROUP == T and GROUP * D == CH
E = 8
H0 = 512
H1 = 1024
PAIRS = 2 * N
S = (PAIRS - E) // P + E
PAIR_ROWS = 2 * NP


def tiles(eng, count, step):
    turns = (count - 2) // 2
    step(0, 0, 0, True, False)
    step(1, 0, 1, True, False)
    with eng.Fori(1, turns) as i:
        step(i * 2, i, 0, False, False)
        step(i * 2 + 1, i, 1, False, False)
    for t in range(2 * turns, count):
        step(t, t // 2, t % 2, False, t == count - 1)


def each(eng, lo, hi, step):
    turns = (hi - lo) // 3
    if turns > 1:
        with eng.Fori(0, turns) as i:
            for j in range(3):
                step(i * 3 + (lo + j))
    else:
        turns = 0
    for t in range(lo + 3 * turns, hi):
        step(t)


def known(t):
    return isinstance(t, int)


class Chain:

    def __init__(self, eng, sem):
        self.eng, self.sem, self.n = eng, sem, 0

    def __call__(self, ins):
        ins.then_inc(self.sem, 1)
        self.n += 1
        self.eng.wait_ge(self.sem, self.n)


class Stage:

    def __init__(self, nc, ctx, name):
        self.nc, self.ctx, self.name, self.sems = nc, ctx, name, []
        ctx.callback(self.end)

    def sb(self, name, shape, dt=F32):
        return self.ctx.enter_context(self.nc.sbuf_tensor(f"{self.name}_{name}", shape, dt))

    def sem(self, name):
        self.sems.append(self.nc.alloc_semaphore(f"{self.name}_{name}"))
        return self.sems[-1]

    def end(self):
        self.nc.clear_and_free_semaphores(self.sems)
        self.nc.all_engine_barrier()


def load_nodes(sp, X, src, halves, tail):
    full = src[0:(T - 1) * P, :].rearrange("(t p) d -> p t d", p=P)
    mid = T // 2
    sp.dma_start(X[:, 0:mid, :], full[:, 0:mid, :]).then_inc(halves[0], 16)
    sp.dma_start(X[:, mid:T - 1, :], full[:, mid:T - 1, :]).then_inc(halves[1], 16)
    base = (T - 1) * P
    sp.dma_start(X[0:TAIL_A, T - 1, :], src[base:base + TAIL_A, :]).then_inc(tail, 16)
    sp.dma_start(X[TAIL_A:TAIL, T - 1, :], src[base + TAIL_A:N, :]).then_inc(tail, 16)


def row_sums(dve, link, X, ST, arrived):
    mid = T // 2
    start = link.n
    for lo, hi, (sem, n) in ((0, mid, arrived[0]), (mid, T - 1, arrived[1]), (T - 1, T, arrived[2])):
        dve.wait_ge(sem, n)
        each(dve, lo, hi, lambda t: dve.bn_stats(ST[:, t, :], X[:, t, :]).then_inc(link.sem, 1))
    link.n = start + T
    dve.wait_ge(link.sem, link.n)


def row_statistics(dve, link, ST, MV, var_ready, std_ready):
    me, qe, mo, qo = (ST[:, :, k] for k in (1, 2, 4, 5))
    mean, rstd, var, tmp = (MV[:, k, :] for k in range(4))
    link(dve.tensor_tensor(tmp, me, mo, ALU.subtract))
    link(dve.tensor_tensor(mean, me, mo, ALU.add))
    link(dve.tensor_tensor(tmp, tmp, tmp, ALU.mult))
    link(dve.tensor_scalar(mean, mean, 0.5, None, ALU.mult))
    link(dve.tensor_tensor(var, qe, qo, ALU.add))
    link(dve.scalar_tensor_tensor(tmp, tmp, D / 4.0, var, ALU.mult, ALU.add))
    dve.tensor_scalar(var, tmp, 1.0 / D, EPS, ALU.mult, ALU.add).then_inc(var_ready, 1)
    dve.wait_ge(std_ready, 1)
    link(dve.reciprocal(rstd, tmp))
    link(dve.tensor_tensor(tmp, rstd, rstd, ALU.mult))
    link(dve.tensor_tensor(tmp, tmp, var, ALU.mult))
    link(dve.tensor_scalar(tmp, tmp, -0.5, 1.5, ALU.mult, ALU.add))
    link(dve.tensor_tensor(rstd, rstd, tmp, ALU.mult))


def square_root(act, MV, var_ready, std_ready):
    act.wait_ge(var_ready, 1)
    act.activation(MV[:, 3, :], MV[:, 2, :], ACT.Sqrt).then_inc(std_ready, 1)


def project(nc, a, bank):
    with ExitStack() as ctx:
        s = Stage(nc, ctx, "proj")
        X = s.sb("x", [P, T, D])
        MV = s.sb("mean_var", [P, 4, T])
        XS = s.sb("normed", [P, 2, D])
        XT = s.sb("normed_t", [P, 2, KD, P])
        EW = s.sb("edge_w", [P, KD, D])
        WN = s.sb("weight_node", [P, KD, D + 1])
        ID = s.sb("identity", [P, P])
        NL = s.sb("node_logits", [P, T])
        VAL = s.sb("valid", [P, T])
        SM = s.sb("small", [P, 4])
        HT, SUP, NATT = a["HT"], a["SUP"], a["NATT"]
        halves = [s.sem("x_first_half"), s.sem("x_second_half")]
        tail = s.sem("x_last_tile")
        edge_in, node_in = s.sem("edge_w_loaded"), s.sem("weight_loaded")
        adj_in = s.sem("adj_loaded")
        chain = s.sem("dve_chain")
        padded = s.sem("pad_zeroed")
        consts = s.sem("constants_ready")
        var_ready, std_ready = s.sem("variance_ready"), s.sem("std_ready")
        normed, transposed, xt_ready = s.sem("normed"), s.sem("transposed"), s.sem("xt_ready")
        projected, hi_ready, lo_ready = s.sem("projected"), s.sem("hi_ready"), s.sem("lo_ready")
        mx_ready, mx_all = s.sem("logit_max_ready"), s.sem("logit_max_all")
        nmx_ready, e_ready, sum_all = s.sem("neg_max_ready"), s.sem("exp_ready"), s.sem("sum_all")
        with nc.Block() as block:
            @block.sync
            def _(sp):
                sp.wait_ge(padded, 1)
                load_nodes(sp, X, a["x"], halves, tail)
                sp.wait_ge(halves[1], 16)
                for t in range(2):
                    sp.dma_start(a["ADJ"][:, t, 0:N], a["adj"][t * P:(t + 1) * P, :]).then_inc(adj_in, 16)
                sp.wait_ge(adj_in, 32)

            @block.gpsimd
            def _(pool):
                pool.memset(ID[:], 0.0).then_inc(consts, 1)
                pool.wait_ge(consts, 1)
                pool.affine_select(out=ID[:], in_=ID[:], compare_op=ALU.not_equal, fill=1.0, base=0,
                                   pattern=[[-1, P]], channel_multiplier=1).then_inc(consts, 1)
                pool.memset(VAL[:], 1.0).then_inc(consts, 1)
                pool.wait_ge(consts, 3)
                pool.affine_select(out=VAL[:], in_=VAL[:], compare_op=ALU.is_gt, fill=0.0, base=N,
                                   pattern=[[-P, T]], channel_multiplier=-1).then_inc(consts, 1)
                pool.wait_ge(mx_ready, 1)
                pool.partition_all_reduce(SM[:, 1:2], SM[:, 0:1], P, RMAX).then_inc(mx_all, 1)
                pool.wait_ge(e_ready, 1)
                pool.partition_all_reduce(SM[:, 3:4], SM[:, 2:3], P, RADD).then_inc(sum_all, 1)

            @block.vector
            def _(dve):
                link = Chain(dve, chain)
                dve.memset(X[:, T - 1, :], 0.0).then_inc(padded, 1)
                row_sums(dve, link, X, a["ST"], [(halves[0], 16), (halves[1], 16), (tail, 32)])
                row_statistics(dve, link, a["ST"], MV, var_ready, std_ready)

                def norm(t, slot, first):
                    if not first:
                        dve.wait_ge(transposed, t - 1)
                    dve.tensor_scalar(XS[:, slot, :], X[:, t, :], MV[:, 0, bass.ds(t, 1)], MV[:, 1, bass.ds(t, 1)],
                                      ALU.subtract, ALU.mult).then_inc(normed, 1)

                def step(t, uses, slot, first, last):
                    if not known(t) or t + 2 < T:
                        norm(t + 2, slot, False)
                    dve.wait_ge(hi_ready, t * 2 + 1)
                    dve.tensor_copy(NL[:, bass.ds(t, 1)], bank[2 + slot][:, D:D + 1])
                    dve.tensor_tensor(SUP[:, t, 1, :], bank[2 + slot][:, 0:D], SUP[:, t, 0, :].bitcast(F32), ALU.subtract).then_inc(lo_ready, 1)
                    dve.wait_ge(hi_ready, t * 2 + 2)
                    dve.tensor_tensor(HT[:, 1, :, bass.ds(t * P, P)],
                                      bank[4 + slot][:, 0:D].rearrange("p (k n) -> p k n", k=KD),
                                      HT[:, 0, :, bass.ds(t * P, P)].bitcast(F32), ALU.subtract).then_inc(lo_ready, 1)

                norm(0, 0, True)
                norm(1, 1, True)
                tiles(dve, T, step)
                dve.wait_ge(lo_ready, T * 2)
                dve.wait_ge(consts, 4)
                link(dve.tensor_tensor(NL[:], NL[:], VAL[:], ALU.mult))
                link(dve.tensor_scalar(VAL[:], VAL[:], BIG, -BIG, ALU.mult, ALU.add))
                link(dve.tensor_tensor(NL[:], NL[:], VAL[:], ALU.add))
                dve.reduce_max(SM[:, 0:1], NL[:], AX).then_inc(mx_ready, 1)
                dve.wait_ge(mx_all, 1)
                dve.tensor_scalar(SM[:, 1:2], SM[:, 1:2], -1.0, None, ALU.mult).then_inc(nmx_ready, 1)
                dve.wait_ge(sum_all, 1)
                link(dve.reciprocal(SM[:, 3:4], SM[:, 3:4]))
                link(dve.tensor_scalar(NATT[:], NATT[:], SM[:, 3:4], None, ALU.mult))

            @block.scalar
            def _(act):
                act.dma_start(EW[:], a["edge_w"].rearrange("(k p) f -> p k f", p=P)).then_inc(edge_in, 16)
                act.dma_start(WN[:, :, 0:D], a["weight"].rearrange("(k p) f -> p k f", p=P)).then_inc(node_in, 16)
                act.dma_start(WN[:, :, D:D + 1], a["node_w"].rearrange("(k p) f -> p k f", p=P), allow_slow_non_contiguous=True).then_inc(node_in, 16)
                square_root(act, MV, var_ready, std_ready)

                def copy_t(t, slot, first):
                    act.wait_ge(transposed, t + 1)
                    if not first:
                        act.wait_ge(projected, t - 1)
                    act.copy(XT[:, slot, :, :], bank[slot][:, 0:D].rearrange("p (k n) -> p k n", k=KD)).then_inc(xt_ready, 1)

                def step(t, uses, slot, first, last):
                    if not last:
                        copy_t(t + 1, 1 - slot, first and slot == 0)
                    act.wait_ge(projected, t + 1)
                    act.copy(SUP[:, t, 0, :], bank[2 + slot][:, 0:D]).then_inc(hi_ready, 1)
                    act.copy(HT[:, 0, :, bass.ds(t * P, P)],
                             bank[4 + slot][:, 0:D].rearrange("p (k n) -> p k n", k=KD)).then_inc(hi_ready, 1)

                copy_t(0, 0, True)
                tiles(act, T, step)
                act.wait_ge(nmx_ready, 1)
                act.activation(NATT[:], NL[:], ACT.Exp, bias=SM[:, 1:2], accum_out=SM[:, 2:3]).then_inc(e_ready, 1)

            @block.tensor
            def _(pe):
                def flip(t, slot, first):
                    pe.wait_ge(normed, t + 1)
                    if not first:
                        pe.wait_ge(xt_ready, t - 1)
                    for k in range(KD):
                        last = pe.transpose(bank[slot][:, k * P:(k + 1) * P], XS[:, slot, k * P:(k + 1) * P], ID[:])
                    last.then_inc(transposed, 1)

                def step(t, uses, slot, first, last):
                    if not last:
                        flip(t + 1, 1 - slot, first and slot == 0)
                    pe.wait_ge(xt_ready, t + 1)
                    if not first:
                        pe.wait_ge(lo_ready, (t - 1) * 2 - 1)
                    for k in range(KD):
                        pe.matmul(bank[2 + slot][:, 0:D + 1], XT[:, slot, k, :], WN[:, k, :], start=k == 0, stop=k == KD - 1)
                    if not first:
                        pe.wait_ge(lo_ready, (t - 1) * 2)
                    for f in range(KD):
                        for k in range(KD):
                            ins = pe.matmul(bank[4 + slot][:, f * P:(f + 1) * P], EW[:, k, f * P:(f + 1) * P],
                                            XT[:, slot, k, :], start=k == 0, stop=k == KD - 1)
                    ins.then_inc(projected, 1)

                pe.wait_ge(consts, 2)
                flip(0, 0, True)
                pe.wait_ge(edge_in, 16)
                pe.wait_ge(node_in, 32)
                tiles(pe, T, step)


def attend(nc, a, bank):
    HT, SUP, NATT = a["HT"], a["SUP"], a["NATT"]
    with ExitStack() as ctx:
        s = Stage(nc, ctx, "attn")
        ADJ = a["ADJ"]
        NEG = s.sb("mask", [P, 2, NP], BF16)
        SC = s.sb("scores", [P, 2, NP])
        HS = s.sb("h_tile", [P, 2, 2, KD, P], F32R)
        PT = s.sb("probs_t", [P, 2, 2, CH], F32R)
        ID = s.sb("identity", [P, P])
        XB = s.sb("x", [P, 2, D])
        XO = s.sb("x_out", [P, 2, D])
        BB = s.sb("bias", [P, D])
        MX = s.sb("max", [P, 2, NC])
        TAKER = s.sb("wait_taker", [P, 2, NC])
        SM = s.sb("small", [P, 2, 6])
        consts = s.sem("constants_ready")
        bias_in = s.sem("bias_loaded")
        edge = s.sem("pad_column_zeroed")
        adj_in = [s.sem(f"adj_loaded{i}") for i in range(2)]
        x_in = [s.sem(f"x_loaded{i}") for i in range(2)]
        mask_ready = s.sem("mask_ready")
        mask_out = [s.sem(f"mask_stored{i}") for i in range(2)]
        h_ready, qk_done, masked = s.sem("h_ready"), s.sem("scores_ready"), s.sem("scores_masked")
        neg_max, exp_done = s.sem("neg_max_ready"), s.sem("probs_ready")
        max_ready, out_part, out_ready = s.sem("max_ready"), s.sem("out_part"), s.sem("out_ready")
        flipped, hi_ready, lo_ready = s.sem("probs_transposed"), s.sem("probs_hi"), s.sem("probs_lo")
        pv_group = s.sem("group_multiplied")
        factor, x_ready = s.sem("factor_ready"), s.sem("x_out_ready")
        x_out = [s.sem(f"x_stored{i}") for i in range(2)]
        sums_ready = s.sem("sums_ready")

        def rows(dram, t):
            return dram[bass.ds(t * P, P), :]

        EARLY = 2

        def half(slot, g):
            return (slot + g) % 2

        with nc.Block() as block:
            @block.sync
            def _(sp):
                sp.wait_ge(edge, 1)
                sp.dma_start(BB[:], a["bias"].partition_broadcast(P)).then_inc(bias_in, 16)

                def store(t, slot):
                    sp.wait_ge(out_ready, t + 1)
                    sp.dma_start(rows(a["x1"], t), XO[:, slot, :]).then_inc(x_out[slot], 16)

                def step(t, uses, slot, first, last):
                    if not first:
                        sp.wait_ge(mask_ready, t - 1)
                    base = (T - 1) * P
                    tail = ((0, TAIL_A), (TAIL_A, TAIL))
                    if last:
                        for lo, hi in tail:
                            sp.dma_start(ADJ[lo:hi, slot, 0:N], a["adj"][base + lo:base + hi, :]).then_inc(adj_in[slot], 16)
                    elif not first:
                        sp.dma_start(ADJ[:, slot, 0:N], rows(a["adj"], t)).then_inc(adj_in[slot], 16)
                    if not first:
                        store(t - 2, slot)
                    if last:
                        for lo, hi in tail:
                            sp.dma_start(XB[lo:hi, slot, :], a["x"][base + lo:base + hi, :]).then_inc(x_in[slot], 16)
                    else:
                        sp.dma_start(XB[:, slot, :], rows(a["x"], t)).then_inc(x_in[slot], 16)
                tiles(sp, T, step)
                store(T - 2, T % 2)
                store(T - 1, (T - 1) % 2)
                for slot in range(2):
                    sp.wait_ge(x_out[slot], T // 2 * 16)

            @block.gpsimd
            def _(pool):
                pool.memset(ID[:], 0.0).then_inc(consts, 1)
                pool.wait_ge(consts, 1)
                pool.affine_select(out=ID[:], in_=ID[:], compare_op=ALU.not_equal, fill=1.0, base=0,
                                   pattern=[[-1, P]], channel_multiplier=1).then_inc(consts, 1)
                pool.memset(ADJ[:, :, N:NP], 0.0).then_inc(edge, 1)

                def step(t, uses, slot, first, last):
                    if not first:
                        pool.wait_ge(adj_in[slot], uses * 16 + (16 if last else 0))
                        pool.wait_ge(masked, (t - 1) * NC)
                        pool.wait_ge(mask_out[slot], uses * 16)
                    pool.tensor_copy(HS[:, slot, :, :, :].rearrange("p a k n -> p (a k) n"),
                                     HT[:, :, :, bass.ds(t * P, P)].rearrange("p a k n -> p (a k) n").bitcast(F32)).then_inc(h_ready, 1)
                    pool.tensor_scalar(NEG[:, slot, :], ADJ[:, slot, :], BIG, -BIG, ALU.mult, ALU.add).then_inc(mask_ready, 1)
                pool.wait_ge(edge, 1)
                tiles(pool, T, step)

            @block.scalar
            def _(act):
                def step(t, uses, slot, first, last):
                    act.wait_ge(mask_ready, t + 1)
                    act.dma_start(a["mask"][t, :, :], NEG[:, slot, :]).then_inc(mask_out[slot], 16)
                    act.wait_ge(neg_max, t + 1)
                    act.activation(SC[:, slot, :], SC[:, slot, :], ACT.Exp, bias=SM[:, slot, 0:1],
                                   accum_out=SM[:, slot, 1:2]).then_inc(exp_done, 1)
                    for g, (g0, gn) in enumerate(GROUPS):
                        act.wait_ge(flipped, t * NG + g + 1)
                        if not (first and slot == 0 and g < 2):
                            act.wait_ge(pv_group, t * NG + (g - 1))
                        act.copy(PT[:, half(slot, g), 0, 0:gn * P], bank[4 + half(slot, g)][:, 0:gn * P]).then_inc(hi_ready, 1)
                tiles(act, T, step)
                for slot in range(2):
                    act.wait_ge(mask_out[slot], T // 2 * 16)

            @block.vector
            def _(dve):
                def rest(t, slot, groups):
                    for g in groups:
                        g0, gn = GROUPS[g]
                        dve.wait_ge(hi_ready, t * NG + g + 1)
                        dve.tensor_tensor(PT[:, half(slot, g), 1, 0:gn * P], bank[4 + half(slot, g)][:, 0:gn * P],
                                          PT[:, half(slot, g), 0, 0:gn * P].bitcast(F32), ALU.subtract).then_inc(lo_ready, 1)

                def score(t, slot, first, midway=None):
                    dve.wait_ge(mask_ready, t + 1)
                    if not first:
                        dve.wait_ge(flipped, (t - 1) * NG)
                    for c, (c0, cn) in enumerate(CHUNKS):
                        if c == NC - 2 and midway:
                            midway()
                        dve.wait_ge(qk_done, t * NC + c + 1)
                        dve.memset(TAKER[:, slot, c:c + 1], 0.0)
                        dve.tensor_tensor_reduce(out=SC[:, slot, c0:c0 + cn], in0=bank[c % 4][:, 0:cn],
                                                 in1=NEG[:, slot, c0:c0 + cn], scale=1.0, scalar=-3.0e38,
                                                 op0=ALU.add, op1=ALU.max,
                                                 accum_out=MX[:, slot, c:c + 1]).then_inc(masked, 1)
                    dve.wait_ge(masked, t * NC + NC)
                    dve.reduce_max(SM[:, slot, 2:3], MX[:, slot, :], AX).then_inc(max_ready, 1)
                    dve.wait_ge(max_ready, t + 1)
                    dve.tensor_scalar(SM[:, slot, 3:4], SM[:, slot, 2:3], -BIG / 2, None, ALU.is_gt)
                    dve.tensor_scalar(SM[:, slot, 0:1], SM[:, slot, 2:3], -1.0, None, ALU.mult).then_inc(neg_max, 1)

                def step(t, uses, slot, first, last):
                    if last:
                        rest(t, slot, range(EARLY))
                    else:
                        score(t + 1, 1 - slot, first and slot == 0, lambda: rest(t, slot, range(EARLY)))
                    rest(t, slot, range(EARLY, NG))
                    dve.wait_ge(exp_done, t + 1)
                    dve.reciprocal(SM[:, slot, 4:5], SM[:, slot, 1:2]).then_inc(factor, 1)
                    dve.wait_ge(factor, t * 2 + 1)
                    dve.scalar_tensor_tensor(SM[:, slot, 5:6], SM[:, slot, 4:5], SM[:, slot, 3:4],
                                             NATT[:, bass.ds(t, 1)], ALU.mult, ALU.mult).then_inc(factor, 1)
                    dve.wait_ge(x_in[slot], (uses + 1) * 16 + (16 if last else 0))
                    if not first:
                        dve.wait_ge(x_out[slot], uses * 16)
                        dve.wait_ge(sums_ready, t - 1)
                    dve.tensor_tensor(XO[:, slot, :], XB[:, slot, :], BB[:], ALU.add).then_inc(x_ready, 1)
                    dve.wait_ge(factor, t * 2 + 2)
                    dve.wait_ge(pv_group, (t + 1) * NG)
                    dve.wait_ge(x_ready, t + 1)
                    dve.scalar_tensor_tensor(XO[:, slot, :], bank[6 + slot][:, D:2 * D], SM[:, slot, 5:6],
                                             XO[:, slot, :], ALU.mult, ALU.add).then_inc(out_part, 1)
                    dve.wait_ge(out_part, t + 1)
                    dve.scalar_tensor_tensor(XO[:, slot, :], bank[6 + slot][:, 0:D], SM[:, slot, 5:6],
                                             XO[:, slot, :], ALU.mult, ALU.add).then_inc(out_ready, 1)
                    dve.wait_ge(out_ready, t + 1)
                    dve.bn_stats(a["ST"][:, t, :], XO[:, slot, :]).then_inc(sums_ready, 1)

                dve.wait_ge(bias_in, 16)
                score(0, 0, True)
                tiles(dve, T, step)

            @block.tensor
            def _(pe):
                def scores(t, slot, first, midway=None):
                    pe.wait_ge(h_ready, t + 1)
                    for c, (c0, cn) in enumerate(CHUNKS):
                        if c == NC - 2 and midway:
                            midway()
                        if c >= 4:
                            pe.wait_ge(masked, t * NC + c - 3)
                        elif not first or slot:
                            pe.wait_ge(masked, t * NC - NC + 1 + max(x for x in range(NC) if x % 4 == c))
                        parts = [(0, 0), (0, 1), (1, 0)]
                        for n, (hs, hm) in enumerate(parts):
                            for k in range(KD):
                                ins = pe.matmul(bank[c % 4][:, 0:cn], HS[:, slot, hs, k, :], HT[:, hm, k, c0:c0 + cn],
                                                start=n == 0 and k == 0, stop=n == 2 and k == KD - 1)
                        ins.then_inc(qk_done, 1)

                def flip(t, slot, g, first):
                    g0, gn = GROUPS[g]
                    if not (first and slot == 0 and g < 2):
                        pe.wait_ge(lo_ready, t * NG + g - 1)
                    for j in range(gn):
                        ins = pe.transpose(bank[4 + half(slot, g)][:, j * P:(j + 1) * P],
                                           SC[:, slot, (g0 + j) * P:(g0 + j + 1) * P], ID[:])
                    ins.then_inc(flipped, 1)

                def early(t, slot, first):
                    pe.wait_ge(exp_done, t + 1)
                    for g in range(EARLY):
                        flip(t, slot, g, first)

                def step(t, uses, slot, first, last):
                    if last:
                        early(t, slot, first)
                    else:
                        scores(t + 1, 1 - slot, first and slot == 0, lambda: early(t, slot, first))
                    if not first:
                        pe.wait_ge(out_ready, t - 1)
                    for g, (g0, gn) in enumerate(GROUPS):
                        if EARLY <= g + 1 < NG:
                            flip(t, slot, g + 1, first)
                        pe.wait_ge(lo_ready, t * NG + g + 1)
                        for j in range(gn):
                            jt = g0 + j
                            part = PT[:, half(slot, g), :, j * P:(j + 1) * P]
                            if jt < T - 1:
                                pe.matmul(bank[6 + slot][:, :], part[:, 0, :], SUP[:, jt, :, :].rearrange("p a d -> p (a d)"),
                                          start=jt == 0, stop=False)
                            ins = pe.matmul(bank[6 + slot][:, 0:D], part[:, 1, :], SUP[:, jt, 0, :],
                                            start=False, stop=False)
                            if jt == T - 1:
                                ins = pe.matmul(bank[6 + slot][:, :], part[:, 0, :], SUP[:, jt, :, :].rearrange("p a d -> p (a d)"),
                                                start=False, stop=True)
                        ins.then_inc(pv_group, 1)
                pe.wait_ge(consts, 2)
                scores(0, 0, True)
                tiles(pe, T, step)


def combine(nc, a, bank, x_in, gates, x_out, parts):
    with ExitStack() as ctx:
        s = Stage(nc, ctx, "comb1" if parts is not None else "comb2")
        X = s.sb("x", [P, T, D])
        Y = s.sb("y", [P, 2, T, D])
        edges = [0, 3, 9, 15, 21, 24, T]
        spans = list(zip(edges[:-1], edges[1:]))
        y_loaded = [[s.sem(f"y{k}_loaded{i}") for i in range(len(spans))] for k in range(2)]
        x_loaded = [s.sem(f"x_loaded{i}") for i in range(len(spans))]
        gated = [s.sem(f"y{k}_gated") for k in range(2)]
        first_added, added = s.sem("first_added"), s.sem("added")
        x_stored = s.sem("x_stored")
        chain = s.sem("dve_chain")
        var_ready, std_ready = s.sem("variance_ready"), s.sem("std_ready")
        normed, hi_ready = s.sem("normed"), s.sem("hi_ready")
        if parts is not None:
            MV = s.sb("mean_var", [P, 4, T])

        def by_tile(dram):
            return dram.rearrange("(t p) d -> p t d", p=P)

        with nc.Block() as block:
            @block.sync
            def _(sp):
                for n, (lo, hi) in enumerate(spans):
                    sp.dma_start(X[:, lo:hi, :], by_tile(x_in)[:, lo:hi, :]).then_inc(x_loaded[n], 16)
                    for k in range(2):
                        sp.dma_start(Y[:, k, lo:hi, :], by_tile(a["y"][k * NP:(k + 1) * NP, :])[:, lo:hi, :]).then_inc(y_loaded[k][n], 16)
                for n, (lo, hi) in enumerate(spans):
                    sp.wait_ge(added, n + 1)
                    if parts is not None:
                        sp.dma_start(by_tile(x_out)[:, lo:hi, :], X[:, lo:hi, :]).then_inc(x_stored, 16)
                        continue
                    hi = min(hi, T - 1)
                    sp.dma_start(by_tile(x_out[lo * P:hi * P, :]), X[:, lo:hi, :]).then_inc(x_stored, 16)
                if parts is None:
                    base = (T - 1) * P
                    sp.dma_start(x_out[base:base + TAIL_A, :], X[0:TAIL_A, T - 1, :]).then_inc(x_stored, 16)
                    sp.dma_start(x_out[base + TAIL_A:N, :], X[TAIL_A:TAIL, T - 1, :]).then_inc(x_stored, 16)
                sp.wait_ge(x_stored, (len(spans) + (2 if parts is None else 0)) * 16)

            @block.vector
            def _(dve):
                link = Chain(dve, chain)
                for n, (lo, hi) in enumerate(spans):
                    dve.wait_ge(x_loaded[n], 16)
                    for k in range(2):
                        dve.wait_ge(gated[k], hi)
                        if k == 1:
                            dve.wait_ge(first_added, n + 1)
                        dve.tensor_tensor(X[:, lo:hi, :], X[:, lo:hi, :], Y[:, k, lo:hi, :],
                                          ALU.add).then_inc(added if k else first_added, 1)
                    if parts is not None:
                        dve.wait_ge(added, n + 1)
                        each(dve, lo, hi, lambda t: dve.bn_stats(a["ST"][:, t, :], X[:, t, :]).then_inc(chain, 1))
                if parts is None:
                    return
                link.n = T
                dve.wait_ge(chain, T)
                row_statistics(dve, link, a["ST"], MV, var_ready, std_ready)

                def rest(n):
                    lo, hi = spans[n]
                    dve.wait_ge(hi_ready, n + 1)
                    dve.tensor_tensor(parts[:, lo:hi, 1, :], Y[:, 0, lo:hi, :], parts[:, lo:hi, 0, :], ALU.subtract)
                for n, (lo, hi) in enumerate(spans):
                    each(dve, lo, hi, lambda t: dve.tensor_scalar(
                        Y[:, 0, t, :], X[:, t, :], MV[:, 0, bass.ds(t, 1)], MV[:, 1, bass.ds(t, 1)],
                        ALU.subtract, ALU.mult).then_inc(normed, 1))
                    if n:
                        rest(n - 1)
                rest(len(spans) - 1)

            @block.scalar
            def _(act):
                for n, (lo, hi) in enumerate(spans):
                    for k in range(2):
                        act.wait_ge(y_loaded[k][n], 16)
                        each(act, lo, hi, lambda t: act.mul(Y[:, k, t, :], Y[:, k, t, :], gates[:, k, bass.ds(t, 1)]).then_inc(gated[k], 1))
                if parts is None:
                    return
                square_root(act, MV, var_ready, std_ready)
                for lo, hi in spans:
                    act.wait_ge(normed, hi)
                    act.copy(parts[:, lo:hi, 0, :], Y[:, 0, lo:hi, :]).then_inc(hi_ready, 1)


def route(nc, a, bank, name, x_in, gate_w, gate_b, r, w, X):
    with ExitStack() as ctx:
        s = Stage(nc, ctx, name)
        MV = s.sb("mean_var", [P, 4, T])
        XT = s.sb("normed_t", [P, 2, GROUP, KD, P])
        GW = s.sb("gate_w", [P, KD, E])
        GB = s.sb("gate_b", [P, E])
        ID = s.sb("identity", [P, P])
        ONES = s.sb("ones", [P, P], BF16)
        BEFORE, USED = s.sb("before", [P, P], BF16), s.sb("pair_count", [P, T, E], BF16)
        VAL = s.sb("valid", [P, T])
        IE, IK, IQ = s.sb("iota_expert", [P, E]), s.sb("iota_tile", [P, T]), s.sb("iota_place", [P, P], BF16)
        IS, ROW = s.sb("iota_slot_tile", [P, S], BF16), s.sb("empty_row", [P, S])
        TILE, LOW = s.sb("pair_tile", [P, 2, T], BF16), s.sb("pair_low", [P, 1])
        LG = s.sb("logits", [P, T, E])
        W3D = [s.sb(f"work{i}", [P, T, E]) for i in range(3)]
        OH = [s.sb(f"one_hot{i}", [P, T, E]) for i in range(2)]
        TOP = s.sb("top", [P, 4, T])
        SCAN = [s.sb(f"scan{i}", [P, E, T]) for i in range(3)]
        EX = [s.sb(f"per_expert{i}", [P, E]) for i in range(4)]
        SL, SI, QI = s.sb("slot", [P, 2, T]), s.sb("slot_int", [P, 2, T], I32), s.sb("place_int", [P, 2, T], I32)
        SF, QF = s.sb("slot_tile", [P, 2, T], BF16), s.sb("slot_place", [P, 2, T], BF16)
        OQ, OS = s.sb("hot_place", [P, 2, 2, GROUP, P], BF16), s.sb("hot_tile", [P, 2, 2, GROUP, S], BF16)
        OV = s.sb("hot_value", [P, 2, 2, GROUP, 2, S], BF16)
        EC = s.sb("expert_cmp", [P, S, E])
        V = [s.sb(f"value{i}", [P, S]) for i in range(3)]
        edges = [0, 6, 12, 18, T]
        spans = list(zip(edges[:-1], edges[1:]))
        x_loaded = [s.sem(f"x_loaded{i}") for i in range(len(spans))]
        gate_in = s.sem("gate_loaded")
        consts, c0 = s.sem("constants_ready"), s.sem("constants_begun")
        chain = s.sem("dve_chain")
        var_ready, std_ready = s.sem("variance_ready"), s.sem("std_ready")
        normed, transposed, xt_ready = s.sem("normed"), s.sem("transposed"), s.sem("xt_ready")
        gated, logit_ready = s.sem("gated"), s.sem("logit_ready")
        xn_stored = s.sem("normed_stored")
        diff_ready, exp_ready = s.sem("difference_ready"), s.sem("gate_exp_ready")
        used_ready, counted = s.sem("pairs_ready"), s.sem("pairs_counted")
        tile_hot, hot_ready, hot_used = s.sem("tile_one_hot"), s.sem("one_hots_ready"), s.sem("one_hots_used")
        BLOCKS = [(j, k) for j in range(GROUP) for k in range(KD)]
        NCONST = 12 if gate_b is None else 11
        with nc.Block() as block:
            @block.sync
            def _(sp):
                view = x_in.rearrange("(t p) d -> p t d", p=P)
                for sem, (lo, hi) in zip(x_loaded, spans):
                    sp.dma_start(X[:, lo:hi, :], view[:, lo:hi, :]).then_inc(sem, 16)
                sp.wait_ge(x_loaded[-1], 16)
                w.load(sp)
                out = a["xn"].rearrange("(t p) d -> p t d", p=P)
                for lo, hi in spans:
                    sp.wait_ge(normed, hi)
                    sp.dma_start(out[:, lo:hi, :], X[:, lo:hi, :]).then_inc(xn_stored, 16)
                sp.wait_ge(xn_stored, len(spans) * 16)

            @block.gpsimd
            def _(pool):
                pool.memset(ID[:], 0.0).then_inc(c0, 1)
                pool.memset(BEFORE[:], 1.0).then_inc(c0, 1)
                pool.memset(VAL[:], 1.0).then_inc(c0, 1)
                if gate_b is None:
                    pool.memset(GB[:], 0.0).then_inc(consts, 1)
                pool.memset(ONES[:], 1.0).then_inc(consts, 1)
                pool.wait_ge(c0, 3)
                pool.affine_select(out=ID[:], in_=ID[:], compare_op=ALU.not_equal, fill=1.0, base=0,
                                   pattern=[[-1, P]], channel_multiplier=1).then_inc(consts, 1)
                pool.affine_select(out=BEFORE[:], in_=BEFORE[:], compare_op=ALU.is_gt, fill=0.0, base=0,
                                   pattern=[[1, P]], channel_multiplier=-1).then_inc(consts, 1)
                pool.affine_select(out=VAL[:], in_=VAL[:], compare_op=ALU.is_gt, fill=0.0, base=N,
                                   pattern=[[-P, T]], channel_multiplier=-1).then_inc(consts, 1)
                small = dict(allow_small_or_imprecise_dtypes=True)
                pool.iota(IE[:], [[1, E]], base=0, channel_multiplier=0, **small).then_inc(consts, 1)
                pool.iota(IK[:], [[P, T]], base=0, channel_multiplier=0, **small).then_inc(consts, 1)
                pool.iota(IQ[:], [[1, P]], base=0, channel_multiplier=0, **small).then_inc(consts, 1)
                pool.iota(IS[:], [[1, S]], base=0, channel_multiplier=0, **small).then_inc(consts, 1)
                pool.iota(ROW[:], [[P, S]], base=PAIR_ROWS + 1, channel_multiplier=1, **small).then_inc(consts, 1)
                pool.iota(TILE[:], [[T, 2], [1, T]], base=0, channel_multiplier=0, **small).then_inc(consts, 1)
                pool.iota(LOW[:], [[0, 1]], base=1, channel_multiplier=1, **small).then_inc(consts, 1)

            @block.tensor
            def _(pe):
                def flip(g):
                    pe.wait_ge(normed, (g + 1) * GROUP)
                    if g >= 2:
                        pe.wait_ge(xt_ready, g - 1)
                    for n, (j, k) in enumerate(BLOCKS):
                        last = pe.transpose(bank[g % 2][:, n * P:(n + 1) * P],
                                            X[:, g * GROUP + j, k * P:(k + 1) * P], ID[:])
                    last.then_inc(transposed, 1)

                pe.wait_ge(consts, NCONST)
                flip(0)
                pe.wait_ge(gate_in, 16 if gate_b is None else 32)
                for g in range(NT):
                    if g + 1 < NT:
                        flip(g + 1)
                    pe.wait_ge(xt_ready, g + 1)
                    for n, (j, k) in enumerate(BLOCKS):
                        tile = g * GROUP + j
                        ins = pe.matmul(bank[2][:, tile * E:(tile + 1) * E], XT[:, g % 2, j, k, :], GW[:, k, :],
                                        start=k == 0, stop=k == KD - 1)
                    ins.then_inc(gated, 1)
                pe.wait_ge(used_ready, 1)
                used = USED[:].rearrange("p t e -> p (t e)")
                pe.matmul(bank[6][:, 0:T * E], BEFORE[:], used, start=True, stop=True)
                pe.matmul(bank[7][:, 0:T * E], ONES[:], used, start=True, stop=True).then_inc(counted, 1)

                def invert(t, uses, slot, first, last):
                    pe.wait_ge(hot_ready, t + 1)
                    for n in range(2 * GROUP):
                        k, j = divmod(n, GROUP)
                        ins = pe.matmul(bank[0][:, 0:2 * S], OQ[:, slot, k, j, :], OV[:, slot, k, j, :, :].rearrange("p v s -> p (v s)"),
                                        start=first and slot == 0 and n == 0, stop=last and n == 2 * GROUP - 1)
                    ins.then_inc(hot_used, 1)
                tiles(pe, NT, invert)

            @block.scalar
            def _(act):
                act.dma_start(GW[:], gate_w).then_inc(gate_in, 16)
                if gate_b is not None:
                    act.dma_start(GB[:], gate_b.partition_broadcast(P)).then_inc(gate_in, 16)
                square_root(act, MV, var_ready, std_ready)

                def copy_t(t, uses, slot, first, last):
                    act.wait_ge(transposed, t + 1)
                    if not first:
                        act.wait_ge(gated, t - 1)
                    act.copy(XT[:, slot, :, :, :].rearrange("p j k n -> p (j k n)"), bank[slot][:, :]).then_inc(xt_ready, 1)
                tiles(act, NT, copy_t)
                act.wait_ge(diff_ready, 1)
                act.activation(TOP[:, 3, :], TOP[:, 2, :], ACT.Exp).then_inc(exp_ready, 1)

            @block.vector
            def _(dve):
                link = Chain(dve, chain)
                row_statistics(dve, link, a["ST"], MV, var_ready, std_ready)
                dve.wait_ge(consts, NCONST)
                dve.wait_ge(gate_in, 16 if gate_b is None else 32)

                def norm(t):
                    dve.tensor_scalar(X[:, t, :], X[:, t, :], MV[:, 0, bass.ds(t, 1)], MV[:, 1, bass.ds(t, 1)],
                                      ALU.subtract, ALU.mult).then_inc(normed, 1)

                for sem, (lo, hi) in zip(x_loaded, spans):
                    dve.wait_ge(sem, 16)
                    each(dve, lo, hi, norm)
                dve.wait_ge(gated, NT)
                dve.tensor_tensor(LG[:], bank[2][:, 0:T * E].rearrange("p (t e) -> p t e", e=E),
                                  GB[:].unsqueeze(1).to_broadcast([P, T, E]), ALU.add).then_inc(logit_ready, 1)
                dve.wait_ge(logit_ready, 1)

                def per_tile(v):
                    return v.unsqueeze(2).to_broadcast([P, T, E])

                def per_expert(v):
                    return v.unsqueeze(1).to_broadcast([P, T, E])

                A, B, C = (w[:] for w in W3D)
                m = [TOP[:, 0, :], TOP[:, 1, :]]
                rest = LG[:]
                for k in range(2):
                    link(dve.reduce_max(m[k], rest, AX))
                    link(dve.tensor_tensor(A, rest, per_tile(m[k]), ALU.is_equal))
                    link(dve.scalar_tensor_tensor(B, A, -float(E), per_expert(IE[:]), ALU.mult, ALU.add))
                    link(dve.tensor_reduce(out=TOP[:, 2, :], in_=B, axis=AX, op=ALU.min))
                    link(dve.tensor_tensor(OH[k][:], B, per_tile(TOP[:, 2, :]), ALU.is_equal))
                    if k == 0:
                        link(dve.scalar_tensor_tensor(C, OH[0][:], -3.0e38, rest, ALU.mult, ALU.add))
                        rest = C
                dve.tensor_tensor(TOP[:, 2, :], m[1], m[0], ALU.subtract).then_inc(diff_ready, 1)
                link(dve.tensor_tensor(B, OH[0][:], OH[1][:], ALU.add))
                dve.tensor_tensor(USED[:], B, per_tile(VAL[:]), ALU.mult).then_inc(used_ready, 1)
                dve.wait_ge(exp_ready, 1)
                link(dve.tensor_scalar(TOP[:, 2, :], TOP[:, 3, :], 1.0, None, ALU.add))
                link(dve.reciprocal(r["gates"][:, 0, :], TOP[:, 2, :]))
                link(dve.tensor_tensor(r["gates"][:, 1, :], r["gates"][:, 0, :], TOP[:, 3, :], ALU.mult))
                dve.wait_ge(counted, 1)
                tot, ping, pong = (v[:] for v in SCAN)
                link(dve.tensor_copy(tot, bank[7][:, 0:T * E].rearrange("p (t e) -> p e t", e=E)))
                src, dst, other = tot, ping, pong
                shift = 1
                while shift < T:
                    dve.tensor_copy(dst[:, :, 0:shift], src[:, :, 0:shift]).then_inc(chain, 1)
                    link.n += 1
                    link(dve.tensor_tensor(dst[:, :, shift:T], src[:, :, shift:T], src[:, :, 0:T - shift], ALU.add))
                    src, dst, other = dst, other, dst
                    shift *= 2
                count, held, ends, more = (v[:] for v in EX)
                link(dve.tensor_copy(count.unsqueeze(2), src[:, :, T - 1:T]))
                link(dve.tensor_tensor(dst, count.unsqueeze(2).to_broadcast([P, E, T]),
                                       IK[:].unsqueeze(1).to_broadcast([P, E, T]), ALU.is_gt))
                link(dve.reduce_sum(held, dst, AX))
                e_src, e_dst, e_other = held, ends, more
                shift = 1
                while shift < E:
                    dve.tensor_copy(e_dst[:, 0:shift], e_src[:, 0:shift]).then_inc(chain, 1)
                    link.n += 1
                    link(dve.tensor_tensor(e_dst[:, shift:E], e_src[:, shift:E], e_src[:, 0:E - shift], ALU.add))
                    e_src, e_dst, e_other = e_dst, e_other, e_dst
                    shift *= 2
                ends = e_src
                link(dve.tensor_tensor(EC[:], ends.unsqueeze(1).to_broadcast([P, S, E]),
                                       IS[:].unsqueeze(2).to_broadcast([P, S, E]), ALU.is_le))
                link(dve.reduce_sum(V[0][:], EC[:], AX))
                link(dve.tensor_scalar(V[1][:], V[0][:], E - 1.0, None, ALU.min))
                link(dve.tensor_copy(r["expert"][:], V[1][:]))
                link(dve.tensor_tensor(count, ends, held, ALU.subtract))
                link(dve.tensor_scalar(count, count, float(P), None, ALU.mult))
                link(dve.tensor_tensor(A, src.rearrange("p e t -> p t e"), tot.rearrange("p e t -> p t e"), ALU.subtract))
                link(dve.tensor_tensor(B, A, bank[6][:, 0:T * E].rearrange("p (t e) -> p t e", e=E), ALU.add))
                link(dve.tensor_tensor(A, B, per_expert(count), ALU.add))
                link(dve.tensor_scalar(TOP[:, 0, :], VAL[:], -float(S * P), float(S * P), ALU.mult, ALU.add))
                for k in range(2):
                    link(dve.tensor_tensor(B, A, OH[k][:], ALU.mult))
                    link(dve.reduce_sum(TOP[:, 1, :], B, AX))
                    link(dve.tensor_tensor(TOP[:, 2, :], TOP[:, 1, :], VAL[:], ALU.mult))
                    link(dve.tensor_tensor(SL[:, k, :], TOP[:, 2, :], TOP[:, 0, :], ALU.add))
                link(dve.tensor_copy(SI[:], SL[:]))
                link(dve.tensor_scalar(QI[:], SI[:], P - 1, None, ALU.bitwise_and))
                link(dve.tensor_copy(QF[:], QI[:]))
                link(dve.tensor_scalar(QI[:], SI[:], P.bit_length() - 1, None, ALU.arith_shift_right))
                link(dve.tensor_copy(SF[:], QI[:]))

                def hot(t, uses, slot, first, last):
                    if not first:
                        dve.wait_ge(hot_used, t - 1)

                    def of(v):
                        return lambda n: v[:, :, bass.ds(t * GROUP, GROUP)].unsqueeze(3).to_broadcast([P, 2, GROUP, n])

                    def row(v, n):
                        return v[:].unsqueeze(1).unsqueeze(1).to_broadcast([P, 2, GROUP, n])
                    dve.tensor_tensor(OS[:, slot], row(IS, S), of(SF)(S), ALU.is_equal).then_inc(tile_hot, 1)
                    dve.tensor_tensor(OQ[:, slot], row(IQ, P), of(QF)(P), ALU.is_equal)
                    dve.wait_ge(tile_hot, t + 1)
                    dve.tensor_tensor(OV[:, slot, :, :, 0, :], OS[:, slot], of(TILE)(S), ALU.mult)
                    dve.tensor_scalar(OV[:, slot, :, :, 1, :], OS[:, slot], LOW[:], None, ALU.mult).then_inc(hot_ready, 1)
                tiles(dve, NT, hot)
                dve.wait_ge(hot_used, NT)
                v0, v1, v2 = (v[:] for v in V)
                link(dve.tensor_scalar(v1, bank[0][:, 0:S], float(P), None, ALU.mult))
                link(dve.tensor_tensor(v0, v1, bank[0][:, S:2 * S], ALU.add))
                link(dve.tensor_scalar(v1, v0, 0.0, None, ALU.is_equal))
                link(dve.tensor_tensor(v2, v1, ROW[:], ALU.mult))
                link(dve.scalar_tensor_tensor(v1, v0, -1.0, v2, ALU.add, ALU.add))
                link(dve.tensor_copy(r["dst"][:], v1))
                link(dve.tensor_scalar(v1, v0, NP + 0.5, -float(NP), ALU.is_gt, ALU.mult))
                link(dve.scalar_tensor_tensor(v2, v0, -1.0, v1, ALU.add, ALU.add))
                link(dve.tensor_scalar(v1, v2, 0.0, None, ALU.max))
                link(dve.tensor_copy(r["tok"][:], v1))


class Weights:

    def __init__(self, nc, keep, name, w_in, w_out, b_in=None, b_out=None):
        s = Stage(nc, keep, name)
        self.w_in, self.w_out, self.b_in, self.b_out = w_in, w_out, b_in, b_out
        self.WI, self.WO = s.sb("w_in", [P, KD, w_in.shape[2]]), s.sb("w_out", list(w_out.shape))
        self.in_loaded, self.out_loaded = s.sem("w_in_loaded"), s.sem("w_out_loaded")
        if b_in is not None:
            self.BI, self.BO = s.sb("b_in", list(b_in.shape)), s.sb("b_out", [P, E * D])
            self.b_loaded = s.sem("b_loaded")

    def load(self, sp):
        for k in range(KD):
            sp.dma_start(self.WI[:, k, :], self.w_in[:, k, :]).then_inc(self.in_loaded, 16)
        sp.dma_start(self.WO[:], self.w_out).then_inc(self.out_loaded, 16)
        if self.b_in is not None:
            sp.dma_start(self.BI[:], self.b_in).then_inc(self.b_loaded, 16)
            sp.dma_start(self.BO[:], self.b_out.partition_broadcast(P)).then_inc(self.b_loaded, 16)


def experts(nc, a, bank, name, w, H, r):
    gated = w.b_in is None
    KH = H // P
    HB = H // CH
    WIN = 2 * H if gated else H
    assert WIN == 2 * CH
    WI, WO = w.WI, w.WO
    with ExitStack() as ctx:
        s = Stage(nc, ctx, name)
        ID = s.sb("identity", [P, P])
        XG = s.sb("x_gathered", [P, 2, D])
        TAKER = s.sb("wait_taker", [P, 2, 2])
        ZERO = s.sb("zero", [NP - N, D])
        XT = s.sb("x_t", [P, 2, 2, KD, P], F32R)
        GATE = s.sb("silu_or_gelu", [P, HB, CH])
        HH = s.sb("hidden", [P, H])
        HTT = s.sb("hidden_t", [P, 2, KH, P], F32R)
        WIP, WOP = s.sb("w_in_parts", [P, 2, KD, WIN], F32R), s.sb("w_out_parts", [P, 2, KH, D], F32R)
        DVE_TAKER = s.sb("dve_wait_taker", [P, 1])
        YS = s.sb("y", [P, 2, D])
        TOKS, DSTS = s.sb("tok", [P, 2], I32), s.sb("dst", [P, 2], I32)
        zeroed, pad_stored = s.sem("zeroed"), s.sem("pad_stored")
        consts = s.sem("identity_ready")
        tok_ready, dst_ready = s.sem("tok_ready"), s.sem("dst_ready")
        gathered = [s.sem(f"gathered{i}") for i in range(2)]
        scattered = [s.sem(f"scattered{i}") for i in range(2)]
        x_flipped, xt_hi, xt_ready = s.sem("x_transposed"), s.sem("xt_hi"), s.sem("xt_ready")
        w_in_hi, w_in_ready = s.sem("w_in_hi"), s.sem("w_in_ready")
        w_out_hi, w_out_ready = s.sem("w_out_hi"), s.sem("w_out_ready")
        gelu_ready, ht_hi = s.sem("gelu_ready"), s.sem("hidden_t_hi")
        first_done, silu_ready, h_ready = s.sem("first_product"), s.sem("silu_ready"), s.sem("hidden_ready")
        h_flipped, ht_ready = s.sem("hidden_transposed"), s.sem("hidden_t_ready")
        second_done, y_ready = s.sem("second_product"), s.sem("y_ready")
        h_bank = [bank[1], bank[6]]

        def ahead(t, uses, slot, n):
            if known(t) and not 0 <= t + n < S:
                return None
            return t + n, uses + (slot + n) // 2, (slot + n) % 2

        def reused(t):
            return not known(t) or t >= 2

        def expert_of(eng, t):
            return eng.value_load(r["expert"][0:1, bass.ds(t, 1)], min_val=0, max_val=E - 1)

        with nc.Block() as block:
            @block.sync
            def _(sp):
                sp.wait_ge(zeroed, 1)
                for k in range(2):
                    sp.dma_start(a["y"][k * NP + N:k * NP + NP, :], ZERO[:]).then_inc(pad_stored, 16)
                sp.wait_ge(pad_stored, 32)

            @block.gpsimd
            def _(pool):
                pool.memset(ZERO[:], 0.0).then_inc(zeroed, 1)
                pool.memset(ID[:], 0.0).then_inc(consts, 1)
                pool.wait_ge(consts, 1)
                pool.affine_select(out=ID[:], in_=ID[:], compare_op=ALU.not_equal, fill=1.0, base=0,
                                   pattern=[[-1, P]], channel_multiplier=1).then_inc(consts, 1)

                def gather(t, uses, slot):
                    if reused(t):
                        pool.wait_ge(x_flipped, t - 1)
                    pool.tensor_copy(TOKS[:, slot:slot + 1], r["tok"][:, bass.ds(t, 1)]).then_inc(tok_ready, 1)
                    pool.wait_ge(tok_ready, t + 1)
                    pool.tensor_tensor(TAKER[:, 0, slot:slot + 1], ID[:, 0:1], ID[:, 0:1], ALU.add)
                    pool.indirect_dma_start(out=XG[:, slot, :], out_offset=None, in_=a["xn"],
                                            in_offset=bass.IndirectOffsetOnAxis(ap=TOKS[:, slot:slot + 1], axis=0)
                                            ).then_inc(gathered[slot], 16)

                def scatter(t, uses, slot):
                    if reused(t):
                        pool.wait_ge(scattered[slot], uses * 16)
                    pool.tensor_copy(DSTS[:, slot:slot + 1], r["dst"][:, bass.ds(t, 1)]).then_inc(dst_ready, 1)
                    pool.wait_ge(dst_ready, t + 1)
                    pool.wait_ge(y_ready, t + 1)
                    pool.tensor_tensor(TAKER[:, 1, slot:slot + 1], ID[:, 0:1], ID[:, 0:1], ALU.add)
                    pool.indirect_dma_start(out=a["y"], out_offset=bass.IndirectOffsetOnAxis(ap=DSTS[:, slot:slot + 1], axis=0),
                                            in_=YS[:, slot, :], in_offset=None).then_inc(scattered[slot], 16)

                def step(t, uses, slot, first, last):
                    if nxt := ahead(t, uses, slot, 2):
                        gather(*nxt)
                    if before := ahead(t, uses, slot, -1):
                        scatter(*before)
                    if last:
                        scatter(t, uses, slot)
                pool.wait_ge(consts, 2)
                gather(0, 0, 0)
                gather(1, 0, 1)
                tiles(pool, S, step)
                pool.wait_ge(scattered[0], (S + 1) // 2 * 16)
                pool.wait_ge(scattered[1], S // 2 * 16)

            @block.tensor
            def _(pe):
                PARTS = ((0, 0), (0, 1), (1, 0))

                def flip_x(t, uses, slot):
                    pe.wait_ge(gathered[slot], (uses + 1) * 16)
                    if not known(t) or t >= 1:
                        pe.wait_ge(xt_ready, t)
                    for k in range(KD):
                        ins = pe.transpose(bank[0][:, k * P:(k + 1) * P], XG[:, slot, k * P:(k + 1) * P], ID[:])
                    ins.then_inc(x_flipped, 1)

                def first_layer(t, uses, slot):
                    pe.wait_ge(xt_ready, t + 1)
                    if reused(t):
                        pe.wait_ge(h_ready, t - 1)
                    for b in range(2):
                        pe.wait_ge(w_in_ready, t * 2 + b + 1)
                        for n, (xp, wp) in enumerate(PARTS):
                            for k in range(KD):
                                ins = pe.matmul(bank[2 + 2 * slot + b][:, :], XT[:, slot, xp, k, :],
                                                WIP[:, wp, k, b * CH:(b + 1) * CH],
                                                start=n == 0 and k == 0, stop=n == 2 and k == KD - 1)
                        ins.then_inc(first_done, 1)

                def flip_hidden(t, uses, slot):
                    pe.wait_ge(h_ready, t + 1)
                    for j in range(HB):
                        if not known(t) or t * HB + j >= 2:
                            pe.wait_ge(ht_ready, t * HB + j - 1)
                        for k in range(4):
                            ins = pe.transpose(h_bank[slot if HB == 1 else j][:, k * P:(k + 1) * P],
                                               HH[:, (4 * j + k) * P:(4 * j + k + 1) * P], ID[:])
                        ins.then_inc(h_flipped, 1)

                def second_layer(t, uses, slot):
                    if not known(t) or t >= 1:
                        pe.wait_ge(y_ready, t)
                    for c in range(2):
                        pe.wait_ge(w_out_ready, t * 2 + c + 1)
                        if c < HB:
                            pe.wait_ge(ht_ready, t * HB + c + 1)
                        for n, (hp, wp) in enumerate(PARTS):
                            for k in range(c * KH // 2, (c + 1) * KH // 2):
                                ins = pe.matmul(bank[7][:, 0:D], HTT[:, hp, k, :], WOP[:, wp, k, :],
                                                start=n == 0 and k == 0, stop=n == 2 and k == KH - 1)
                    ins.then_inc(second_done, 1)

                def step(t, uses, slot, first, last):
                    flip_hidden(t, uses, slot)
                    if nxt := ahead(t, uses, slot, 1):
                        first_layer(*nxt)
                    if nxt := ahead(t, uses, slot, 2):
                        flip_x(*nxt)
                    second_layer(t, uses, slot)

                pe.wait_ge(consts, 2)
                flip_x(0, 0, 0)
                flip_x(1, 0, 1)
                first_layer(0, 0, 0)
                tiles(pe, S, step)

            @block.scalar
            def _(act):
                def copy_x(t, uses, slot):
                    act.wait_ge(x_flipped, t + 1)
                    if reused(t):
                        act.wait_ge(first_done, (t - 1) * 2)
                    act.copy(XT[:, slot, 0, :, :], bank[0][:, 0:D].rearrange("p (k n) -> p k n", k=KD)).then_inc(xt_hi, 1)

                def silu(t, uses, slot):
                    act.wait_ge(first_done, t * 2 + 1)
                    if not known(t) or t >= 1:
                        act.wait_ge(h_ready, t)
                    act.activation(GATE[:, 0, :], bank[2 + 2 * slot][:, :], ACT.Silu).then_inc(silu_ready, 1)

                def hidden_out(t, uses, slot):
                    e = None if gated else expert_of(act, t)
                    for j in range(HB):
                        src = h_bank[slot if HB == 1 else j]
                        act.wait_ge(h_flipped, t * HB + j + 1)
                        if not gated:
                            if not known(t) or t >= 1:
                                act.wait_ge(ht_ready, (t - 1) * HB + j + 1)
                            for k in range(4):
                                ins = act.activation(GATE[:, j, k * P:(k + 1) * P], src[:, k * P:(k + 1) * P], ACT.Gelu,
                                                     bias=w.BI[:, bass.ds(e * KH + (4 * j + k), 1)])
                            ins.then_inc(gelu_ready, 1)
                            act.wait_ge(gelu_ready, t * HB + j + 1)
                        if not known(t) or t >= 1:
                            act.wait_ge(second_done, t)
                        act.copy(HTT[:, 0, 4 * j:4 * j + 4, :],
                                 (src[:, :] if gated else GATE[:, j, :]).rearrange("p (k n) -> p k n", n=P)).then_inc(ht_hi, 1)

                def step(t, uses, slot, first, last):
                    hidden_out(t, uses, slot)
                    nxt = ahead(t, uses, slot, 1)
                    if gated and nxt:
                        silu(*nxt)
                    if nxt := ahead(t, uses, slot, 2):
                        copy_x(*nxt)
                copy_x(0, 0, 0)
                copy_x(1, 0, 1)
                if gated:
                    silu(0, 0, 0)
                else:
                    act.wait_ge(w.b_loaded, 32)
                tiles(act, S, step)

            @block.vector
            def _(dve):
                def hidden(t, uses, slot):
                    if gated:
                        dve.wait_ge(silu_ready, t + 1)
                        dve.wait_ge(first_done, t * 2 + 2)
                    if not known(t) or t >= 1:
                        dve.wait_ge(h_flipped, t * HB)
                    if gated:
                        ins = dve.tensor_tensor(HH[:], GATE[:, 0, :], bank[3 + 2 * slot][:, :], ALU.mult)
                    else:
                        for b in range(2):
                            dve.wait_ge(first_done, t * 2 + b + 1)
                            ins = dve.tensor_copy(HH[:, b * CH:(b + 1) * CH], bank[2 + 2 * slot + b][:, :])
                    ins.then_inc(h_ready, 1)

                def x_rest(t, uses, slot):
                    dve.wait_ge(xt_hi, t + 1)
                    dve.tensor_tensor(XT[:, slot, 1, :, :], bank[0][:, 0:D].rearrange("p (k n) -> p k n", k=KD),
                                      XT[:, slot, 0, :, :].bitcast(F32), ALU.subtract).then_inc(xt_ready, 1)

                def hidden_rest(t, uses, slot):
                    for j in range(HB):
                        src = h_bank[slot][:, :] if gated else GATE[:, j, :]
                        dve.wait_ge(ht_hi, t * HB + j + 1)
                        dve.tensor_tensor(HTT[:, 1, 4 * j:4 * j + 4, :], src.rearrange("p (k n) -> p k n", n=P),
                                          HTT[:, 0, 4 * j:4 * j + 4, :].bitcast(F32), ALU.subtract).then_inc(ht_ready, 1)

                def split(halves, hi, ready, t, reusable=None):
                    for c, (parts, weights) in enumerate(halves):
                        if reusable:
                            dve.wait_ge(*reusable(c))
                            dve.memset(DVE_TAKER[:], 0.0)
                        dve.tensor_copy(parts[:, 0, :, :], weights).then_inc(hi, 1)
                        dve.wait_ge(hi, t * 2 + c + 1)
                        dve.tensor_tensor(parts[:, 1, :, :], weights, parts[:, 0, :, :].bitcast(F32), ALU.subtract).then_inc(ready, 1)

                experts_of = [dve.alloc_register(f"{name}_expert_of_tile_{n}_on") for n in range(3)]

                def split_if_new(halves_of, hi, ready, reusable, t, n):
                    with dve.If_ne(experts_of[n], experts_of[n - 1]):
                        split(halves_of(expert_of(dve, t)), hi, ready, t, reusable)
                    with dve.Else():
                        dve.sem_inc(hi, 2)
                        dve.sem_inc(ready, 2)

                def w_in_of(e):
                    return [(WIP[:, :, :, b * CH:(b + 1) * CH], WI[:, :, bass.ds(e * WIN + b * CH, CH)]) for b in range(2)]

                def w_out_of(e):
                    return [(WOP[:, :, c * KH // 2:(c + 1) * KH // 2, :], WO[:, c * KH // 2:(c + 1) * KH // 2, bass.ds(e * D, D)])
                            for c in range(2)]

                def split_w_in(t, n):
                    split_if_new(w_in_of, w_in_hi, w_in_ready, lambda b: (first_done, t * 2 + (b - 1)), t, n)

                def split_w_out(t, n):
                    split_if_new(w_out_of, w_out_hi, w_out_ready, lambda c: (second_done, t), t, n)

                def result(t, uses, slot):
                    e = None if gated else expert_of(dve, t)
                    dve.wait_ge(second_done, t + 1)
                    if reused(t):
                        dve.wait_ge(scattered[slot], uses * 16)
                    if gated:
                        dve.tensor_copy(YS[:, slot, :], bank[7][:, 0:D]).then_inc(y_ready, 1)
                    else:
                        dve.tensor_tensor(YS[:, slot, :], bank[7][:, 0:D], w.BO[:, bass.ds(e * D, D)], ALU.add).then_inc(y_ready, 1)

                def load_expert(n, t):
                    dve.reg_load(experts_of[n], r["expert"][0:1, bass.ds(t, 1)])

                def step(t, uses, slot, first, last):
                    dve.reg_mov(experts_of[0], experts_of[1])
                    dve.reg_mov(experts_of[1], experts_of[2])
                    if nxt := ahead(t, uses, slot, 2):
                        load_expert(2, nxt[0])
                    hidden_rest(t, uses, slot)
                    if nxt := ahead(t, uses, slot, 1):
                        hidden(*nxt)
                    if nxt := ahead(t, uses, slot, 2):
                        x_rest(*nxt)
                        split_w_in(nxt[0], 2)
                    result(t, uses, slot)
                    if nxt := ahead(t, uses, slot, 1):
                        split_w_out(nxt[0], 1)
                e = expert_of(dve, 0)
                dve.wait_ge(w.in_loaded, KD * 16)
                split(w_in_of(e), w_in_hi, w_in_ready, 0)
                x_rest(0, 0, 0)
                x_rest(1, 0, 1)
                dve.wait_ge(w.out_loaded, 16)
                split(w_out_of(e), w_out_hi, w_out_ready, 0)
                if not gated:
                    dve.wait_ge(w.b_loaded, 32)
                hidden(0, 0, 0)
                load_expert(1, 0)
                load_expert(2, 1)
                split_w_in(1, 2)
                tiles(dve, S, step)


def neighbours(nc, a, bank, XH):
    GS = [(g, min(8, T - g)) for g in range(0, T, 8)]
    G = len(GS)
    assert G % 2 == 0
    with ExitStack() as ctx:
        s = Stage(nc, ctx, "nbr")
        NEG = s.sb("mask", [P, 2, NP], BF16)
        ID, IDF = s.sb("identity", [P, P], BF16), s.sb("identity_f32", [P, P])
        AT = s.sb("adj_t", [P, 2, 8 * P], F16)
        WT = s.sb("w_t", [P, KD, D])
        BB = s.sb("bias", [P, D])
        XB, XO = s.sb("x", [P, 2, D]), s.sb("x_out", [P, 2, D])
        AGH, AG = s.sb("sum_hi", [P, 2, D]), s.sb("sum", [P, 2, D])
        AGT = s.sb("sum_t", [P, 2, KD, P])
        PRE = s.sb("before_relu", [P, 2, D])
        consts, w_loaded = s.sem("identity_ready"), s.sem("w_loaded")
        mask_in = [s.sem(f"mask_loaded{i}") for i in range(2)]
        x_loaded = [s.sem(f"x_loaded{i}") for i in range(2)]
        x_stored = [s.sem(f"x_stored{i}") for i in range(2)]
        flipped, at_ready, used = s.sem("mask_transposed"), s.sem("adj_t_ready"), s.sem("group_multiplied")
        at_odd = s.sem("adj_t_odd_ready")
        hi_ready, ag_ready, ag_flipped, agt_ready = s.sem("sum_hi_ready"), s.sem("sum_ready"), s.sem("sum_transposed"), s.sem("sum_t_ready")
        out_done, pre_ready, x_ready = s.sem("product_ready"), s.sem("pre_ready"), s.sem("x_ready")
        sums_ready = s.sem("sums_ready")
        bf = [bank[i][:, :].bitcast(BF16) for i in range(2)]
        with nc.Block() as block:
            @block.sync
            def _(sp):
                def store(t, slot):
                    sp.wait_ge(x_ready, t + 1)
                    sp.dma_start(a["x3"][bass.ds(t * P, P), :], XO[:, slot, :]).then_inc(x_stored[slot], 16)

                def step(t, uses, slot, first, last):
                    if not first:
                        sp.wait_ge(flipped, (t - 1) * G)
                    sp.dma_start(NEG[:, slot, :], a["mask"][t, :, :]).then_inc(mask_in[slot], 16)
                    if not first:
                        store(t - 2, slot)
                    sp.dma_start(XB[:, slot, :], a["x2"][bass.ds(t * P, P), :]).then_inc(x_loaded[slot], 16)
                tiles(sp, T, step)
                store(T - 2, 0)
                store(T - 1, 1)
                for slot in range(2):
                    sp.wait_ge(x_stored[slot], T // 2 * 16)

            @block.gpsimd
            def _(pool):
                for n, i in enumerate((ID, IDF)):
                    pool.memset(i[:], 0.0).then_inc(consts, 1)
                    pool.wait_ge(consts, 2 * n + 1)
                    pool.affine_select(out=i[:], in_=i[:], compare_op=ALU.not_equal, fill=1.0, base=0,
                                       pattern=[[-1, P]], channel_multiplier=1).then_inc(consts, 1)

            @block.tensor
            def _(pe):
                def flip(t, uses, slot, g, first):
                    g0, gn = GS[g]
                    if g == 0:
                        pe.wait_ge(mask_in[slot], (uses + 1) * 16)
                    if not (first and slot == 0 and g < 2):
                        pe.wait_ge(at_ready if g % 2 == 0 else at_odd, t * (G // 2) + g // 2)
                    for j in range(gn):
                        ins = pe.transpose(bf[g % 2][:, j * P:(j + 1) * P], NEG[:, slot, (g0 + j) * P:(g0 + j + 1) * P], ID[:])
                    ins.then_inc(flipped, 1)

                def multiply(t, slot, g):
                    g0, gn = GS[g]
                    pe.wait_ge(at_ready if g % 2 == 0 else at_odd, t * (G // 2) + g // 2 + 1)
                    for j in range(gn):
                        ins = pe.matmul(bank[2 + slot][:, :], AT[:, g % 2, j * P:(j + 1) * P],
                                        XH[:, g0 + j, :, :].rearrange("p a d -> p (a d)"), start=g0 + j == 0, stop=g0 + j == T - 1)
                    ins.then_inc(used, 1)

                def finish(t, slot, first):
                    pe.wait_ge(ag_ready, t + 1)
                    if not first:
                        pe.wait_ge(x_ready, t - 1)
                    for k in range(KD):
                        ins = pe.transpose(bank[4 + slot][:, k * P:(k + 1) * P], AG[:, slot, k * P:(k + 1) * P], IDF[:])
                    ins.then_inc(ag_flipped, 1)

                def project_out(t, slot):
                    pe.wait_ge(agt_ready, t + 1)
                    for k in range(KD):
                        ins = pe.matmul(bank[6 + slot][:, 0:D], AGT[:, slot, k, :], WT[:, k, :], start=k == 0, stop=k == KD - 1)
                    ins.then_inc(out_done, 1)

                def step(t, uses, slot, first, last):
                    very_first = first and slot == 0
                    if not first:
                        pe.wait_ge(ag_ready, t - 1)
                    for g in range(G):
                        if g + 1 < G:
                            flip(t, uses, slot, g + 1, first)
                        elif not last:
                            flip(t + 1, uses + slot, 1 - slot, 0, first and slot == 0)
                        multiply(t, slot, g)
                        if g == 1 and not very_first:
                            finish(t - 1, 1 - slot, first)
                        if g == 2 and not very_first:
                            project_out(t - 1, 1 - slot)
                    if last:
                        finish(t, slot, False)
                        project_out(t, slot)
                pe.wait_ge(consts, 4)
                flip(0, 0, 0, 0, True)
                pe.wait_ge(w_loaded, 32)
                tiles(pe, T, step)

            @block.scalar
            def _(act):
                act.dma_start(WT[:], a["w_t"]).then_inc(w_loaded, 16)
                act.dma_start(BB[:], a["b"].partition_broadcast(P)).then_inc(w_loaded, 16)

                def even(t, slot, g, first):
                    act.wait_ge(flipped, t * G + g + 1)
                    if not (first and slot == 0 and g < 2):
                        act.wait_ge(used, t * G + g - 1)
                    w = GS[g][1] * P
                    act.activation(AT[:, 0, 0:w], bf[0][:, 0:w], ACT.Copy, bias=1.0, scale=1.0 / BIG).then_inc(at_ready, 1)

                def tail(t, slot, first):
                    act.wait_ge(used, (t + 1) * G)
                    if not first:
                        act.wait_ge(ag_ready, t - 1)
                    act.copy(AGH[:, slot, :], bank[2 + slot][:, 0:D]).then_inc(hi_ready, 1)

                def flip_out(t, slot, first):
                    act.wait_ge(ag_flipped, t + 1)
                    if not first:
                        act.wait_ge(out_done, t - 1)
                    act.copy(AGT[:, slot, :, :], bank[4 + slot][:, 0:D].rearrange("p (k n) -> p k n", k=KD)).then_inc(agt_ready, 1)

                def step(t, uses, slot, first, last):
                    for g in range(0, G, 2):
                        even(t, slot, g, first)
                        if g == 0 and not (first and slot == 0):
                            tail(t - 1, 1 - slot, first)
                    if not (first and slot == 0):
                        flip_out(t - 1, 1 - slot, first)
                    if last:
                        tail(t, slot, False)
                        flip_out(t, slot, False)
                tiles(act, T, step)

            @block.vector
            def _(dve):
                def odd(t, slot, g, first):
                    if not (first and slot == 0 and g < 2):
                        dve.wait_ge(used, t * G + g - 1)
                    dve.wait_ge(flipped, t * G + g + 1)
                    w = GS[g][1] * P
                    dve.tensor_scalar(AT[:, 1, 0:w], bf[1][:, 0:w], 1.0 / BIG, 1.0, ALU.mult, ALU.add).then_inc(at_odd, 1)

                def add(t, slot, first):
                    dve.wait_ge(hi_ready, t + 1)
                    if not first:
                        dve.wait_ge(ag_flipped, t - 1)
                    dve.tensor_tensor(AG[:, slot, :], bank[2 + slot][:, D:2 * D], AGH[:, slot, :], ALU.add).then_inc(ag_ready, 1)

                def finish(t, uses, slot, first):
                    dve.wait_ge(out_done, t + 1)
                    dve.tensor_tensor(PRE[:, slot, :], bank[6 + slot][:, 0:D], BB[:], ALU.add).then_inc(pre_ready, 1)
                    dve.wait_ge(x_loaded[slot], (uses + 1) * 16)
                    if not first:
                        dve.wait_ge(x_stored[slot], uses * 16)
                        dve.wait_ge(sums_ready, t - 1)
                    dve.wait_ge(pre_ready, t + 1)
                    dve.scalar_tensor_tensor(XO[:, slot, :], PRE[:, slot, :], 0.0, XB[:, slot, :], ALU.max, ALU.add).then_inc(x_ready, 1)
                    dve.wait_ge(x_ready, t + 1)
                    dve.bn_stats(a["ST"][:, t, :], XO[:, slot, :]).then_inc(sums_ready, 1)

                def step(t, uses, slot, first, last):
                    very_first = first and slot == 0
                    if not very_first:
                        add(t - 1, 1 - slot, first)
                    odd(t, slot, 1, first)
                    odd(t, slot, 3, first)
                    if not very_first:
                        finish(t - 1, uses - (1 - slot), 1 - slot, first)
                    if last:
                        add(t, slot, False)
                        finish(t, uses, slot, False)
                tiles(dve, T, step)


def build(nc, x, adj, weight, bias, node_w, edge_w, wg, bg, w13, w2, w_t, b, gate_t, w1_t, b1, w2_t, b2, out, stop=99):
    with ExitStack() as ctx:
        bank = [ctx.enter_context(nc.psum_tensor(f"bank{i}", [P, CH], F32)) for i in range(8)]

        def dram(name, shape, dt=F32):
            return nc.dram_tensor(name, shape, dt, kind="Internal").ap()

        def routing(name, keep):
            t = lambda what, shape, dt: keep.enter_context(nc.sbuf_tensor(f"{name}_{what}", shape, dt))
            return dict(gates=t("gates", [P, 2, T], F32), tok=t("tok", [P, S], I32), dst=t("dst", [P, S], I32),
                        expert=t("expert", [P, S], I32))

        a = dict(x=x, adj=adj, weight=weight, bias=bias, node_w=node_w, edge_w=edge_w, w_t=w_t, b=b)
        a["mask"] = dram("mask", [T, P, NP], BF16)
        for name in ("x1", "x2", "x3", "xn"):
            a[name] = dram(name, [NP, D])
        a["y"] = dram("y", [PAIR_ROWS + S * P, D])
        a["ST"] = ctx.enter_context(nc.sbuf_tensor("row_sums", [P, T, 6], F32))
        with ExitStack() as keep:
            a["ADJ"] = keep.enter_context(nc.sbuf_tensor("adj_tile", [P, 2, NP], F32))
            a["HT"] = keep.enter_context(nc.sbuf_tensor("h_t", [P, 2, KD, NP], F32R))
            a["SUP"] = keep.enter_context(nc.sbuf_tensor("support", [P, T, 2, D], F32R))
            a["NATT"] = keep.enter_context(nc.sbuf_tensor("node_attention", [P, T], F32))
            project(nc, a, bank)
            attend(nc, a, bank)
        for layer, (x_in, gate, gate_b, weights, H) in enumerate((
                (a["x1"], wg, bg, (w13, w2), H0), (a["x3"], gate_t, None, (w1_t, w2_t, b1, b2), H1))):
            with ExitStack() as keep:
                r = routing(f"route{layer}", keep)
                with ExitStack() as while_used:
                    w = Weights(nc, while_used, f"w{layer}", *weights)
                    with ExitStack() as normed:
                        X = normed.enter_context(nc.sbuf_tensor(f"x_normed{layer}", [P, T, D], F32))
                        route(nc, a, bank, f"gate{layer}", x_in, gate, gate_b, r, w, X)
                    experts(nc, a, bank, f"ffn{layer}", w, H, r)
                if layer == 0:
                    XH = keep.enter_context(nc.sbuf_tensor("normed_parts", [P, T, 2, D], F16))
                    combine(nc, a, bank, x_in, r["gates"], a["x2"], XH)
                    neighbours(nc, a, bank, XH)
                else:
                    combine(nc, a, bank, x_in, r["gates"], out, None)


def layout(i):
    import numpy as np

    def blocks(w):
        e, n, m = w.shape
        return np.ascontiguousarray(w.reshape(e, n // P, P, m).transpose(2, 1, 0, 3).reshape(P, n // P, e * m))

    w13 = np.concatenate([i["L0_ffn_W1"], i["L0_ffn_W3"]], axis=2)
    return dict(
        x=i["x"], adj=i["adj"], weight=i["L0_gnn_weight"], bias=i["L0_gnn_bias"], node_w=i["L0_gnn_node_w"],
        edge_w=i["L0_gnn_edge_w"], wg=blocks(i["L0_ffn_Wg"][None]), bg=i["L0_ffn_bg"], w13=blocks(w13),
        w2=blocks(i["L0_ffn_W2"]), w_t=blocks(i["L1_gnn_W"].T[None]), b=i["L1_gnn_b"],
        gate_t=blocks(i["L1_ffn_gate_w"].T[None]), w1_t=blocks(i["L1_ffn_w1"].transpose(0, 2, 1)),
        b1=i["L1_ffn_b1"].reshape(E * H1 // P, P).T, w2_t=blocks(i["L1_ffn_w2"].transpose(0, 2, 1)), b2=i["L1_ffn_b2"].reshape(-1))


def kernel(**inputs):
    import numpy as np
    import concourse.bacc as bacc
    from concourse.bass_utils import run_bass_kernel_spmd

    nc = bacc.Bacc("TRN2", target_bir_lowering=False, num_devices=1)
    arrays, args = {}, []
    for name, value in layout({k: np.asarray(v) for k, v in inputs.items()}).items():
        value = np.ascontiguousarray(value)
        arrays[f"in_{name}"] = value
        args.append(nc.dram_tensor(f"in_{name}", value.shape, mybir.dt.from_np(value.dtype), kind="ExternalInput").ap())
    out = nc.dram_tensor("out_0", (N, D), F32, kind="ExternalOutput").ap()
    build(nc, *args, out)
    r = run_bass_kernel_spmd(nc, [arrays], core_ids=[0])
    return r.results[0]["out_0"]
```
